# Optimizing a Trainium2 kernel written in Bass

```python
import numpy as np
import jax
import jax.numpy as jnp

def _softmax(x, axis=-1):
    return jax.nn.softmax(x, axis=axis)

def _gelu(x):
    return jax.nn.gelu(x, approximate=True)

def _silu(x):
    return jax.nn.silu(x)

def _sigmoid(x):
    return jax.nn.sigmoid(x)

def _layernorm(x, axis=-1, eps=1e-05):
    m = jnp.mean(x, axis=axis, keepdims=True)
    v = jnp.var(x, axis=axis, keepdims=True)
    return (x - m) / jnp.sqrt(v + eps)

def _scatter_add(tgt, idx, src, axis=0):
    return tgt.at[idx].add(src)

def _segment_sum(src, seg, n):
    return jax.ops.segment_sum(src, seg, n)
kernel_name = 'mk_recurrent_d2_jaxref_r4_040c70'

def setup_inputs(seed: int=0):
    np.random.seed(seed)
    _w = jnp.asarray

    def _L0_attn_setup():
        import jax, jax.numpy as jnp
        import numpy as np
        B, T, D = (4, 1024, 512)
        LAYER_ID, N_LAYERS = (0, 12)
        LN_EPS = 1e-05

        def _wkv(w, u, k, v):
            Bb, Tt, Dd = k.shape
            neg_ew = -jnp.exp(w)

            def step(carry, kv):
                aa, bb, pp = carry
                kt, vt = kv
                qt = jnp.maximum(pp, kt + u)
                e1 = jnp.exp(pp - qt)
                e2 = jnp.exp(kt + u - qt)
                out = (e1 * aa + e2 * vt) / (e1 * bb + e2)
                pp_new = jnp.maximum(pp + neg_ew, kt)
                f1 = jnp.exp(pp - pp_new)
                f2 = jnp.exp(kt - pp_new)
                return ((f1 * aa + f2 * vt, f1 * bb + f2, pp_new), out)
            init = (jnp.zeros((Bb, Dd), k.dtype), jnp.zeros((Bb, Dd), k.dtype), jnp.full((Bb, Dd), -1e+38, k.dtype))
            kT = jnp.swapaxes(k, 0, 1)
            vT = jnp.swapaxes(v, 0, 1)
            _, outT = jax.lax.scan(step, init, (kT, vT))
            return jnp.swapaxes(outT, 0, 1)
        key = jax.random.key(seed)
        ks = jax.random.split(key, 9)
        s = 0.02
        x = jax.random.normal(ks[0], (B, T, D), jnp.float32)
        Wk = jax.random.normal(ks[1], (D, D), jnp.float32) * s
        Wv = jax.random.normal(ks[2], (D, D), jnp.float32) * s
        Wr = jax.random.normal(ks[3], (D, D), jnp.float32) * s
        Wo = jax.random.normal(ks[4], (D, D), jnp.float32) * s
        tm_k = jax.random.uniform(ks[5], (1, 1, D), jnp.float32)
        tm_v = jax.random.uniform(ks[6], (1, 1, D), jnp.float32)
        tm_r = jax.random.uniform(ks[7], (1, 1, D), jnp.float32)
        ratio_0_to_1 = LAYER_ID / max(N_LAYERS - 1, 1)
        ratio_1_to_almost_0 = 1.0 - LAYER_ID / N_LAYERS
        i = jnp.arange(D, dtype=jnp.float32)
        time_decay = -5.0 + 8.0 * (i / (D - 1)) ** (0.7 + 1.3 * ratio_0_to_1)
        zigzag = (jnp.arange(D) % 3 - 1).astype(jnp.float32) * ratio_1_to_almost_0
        time_first = jnp.full((D,), jnp.log(jnp.float32(0.3))) + zigzag
        ln_g = jnp.ones((D,), jnp.float32)
        ln_b = jnp.zeros((D,), jnp.float32)
        return {'x': x, 'Wk': Wk, 'Wv': Wv, 'Wr': Wr, 'Wo': Wo, 'tm_k': tm_k, 'tm_v': tm_v, 'tm_r': tm_r, 'time_decay': time_decay, 'time_first': time_first, 'ln_g': ln_g, 'ln_b': ln_b}
    _L0_attn_in = _L0_attn_setup()

    def _L0_ffn_setup():
        import jax, jax.numpy as jnp
        import numpy as np
        B, S, D, FF, E = (4, 512, 512, 2048, 2)
        key = jax.random.key(seed)
        k0, k1, k2, k3, k4 = jax.random.split(key, 5)
        s = 0.02
        return {'hidden_states': jax.random.normal(k0, (B, S, D), jnp.float32), 'gate_w': jax.random.normal(k1, (E, D), jnp.float32) * s, 'w_gate': jax.random.normal(k2, (E, FF, D), jnp.float32) * s, 'w_up': jax.random.normal(k3, (E, FF, D), jnp.float32) * s, 'w_down': jax.random.normal(k4, (E, D, FF), jnp.float32) * s}
    _L0_ffn_in = _L0_ffn_setup()

    def _L1_attn_setup():
        import jax, jax.numpy as jnp
        import numpy as np
        D_MODEL = 512
        H = 16
        HKV = 4
        DS = 32
        DG = 32
        DV = 64
        B, T = (2, 1024)
        MB = 64
        LW = 256
        ROPE_BASE = 10000.0
        NEG_INF = -1000000000.0

        def _rope(x, pos, base):
            d = x.shape[-1]
            inv_freq = 1.0 / base ** (jnp.arange(0, d, 2, dtype=jnp.float32) / d)
            ang = pos.astype(jnp.float32)[:, None] * inv_freq
            cos, sin = (jnp.cos(ang), jnp.sin(ang))
            x1, x2 = jnp.split(x, 2, axis=-1)
            return jnp.concatenate([x1 * cos - x2 * sin, x2 * cos + x1 * sin], axis=-1)
        key = jax.random.key(seed)
        ks = jax.random.split(key, 8)
        w = lambda k, sh: jax.random.normal(k, sh, jnp.float32) * 0.02
        return {'x': jax.random.normal(ks[0], (B, T, D_MODEL), jnp.float32), 'Wq_sem': w(ks[1], (D_MODEL, H * DS)), 'Wk_sem': w(ks[2], (D_MODEL, HKV * DS)), 'Wq_geo': w(ks[3], (D_MODEL, H * DG)), 'Wk_geo': w(ks[4], (D_MODEL, HKV * DG)), 'Wv': w(ks[5], (D_MODEL, HKV * DV)), 'Wo': w(ks[6], (H * DV, D_MODEL)), 'logit_scale': jnp.zeros((H,), jnp.float32)}
    _L1_attn_in = _L1_attn_setup()

    def _L1_ffn_setup():
        import jax, jax.numpy as jnp
        import numpy as np
        D_MODEL, D_FF, NS, NR, KR = (512, 352, 2, 16, 4)
        B, S = (4, 512)

        def _moe_forward(u, shared_w1, shared_b1, shared_w2, shared_b2, routed_w1, routed_b1, routed_w2, routed_b2, centroids, bias):
            b, s, d = u.shape
            flat = u.reshape(-1, d)
            T = flat.shape[0]
            h = jax.nn.relu(jnp.einsum('td,ndf->ntf', flat, shared_w1) + shared_b1[:, None, :])
            shared_out = jnp.einsum('ntf,nfd->td', h, shared_w2) + shared_b2.sum(0)
            out = flat + shared_out
            scores = jax.nn.sigmoid(flat @ centroids.T) + bias
            vals, idx = jax.lax.top_k(scores, KR)
            gating = jnp.zeros_like(scores).at[jnp.arange(T)[:, None], idx].set(vals)
            gating = gating / jnp.clip(gating.sum(-1, keepdims=True), 1e-08)

            def step(acc, ew):
                w1, b1, w2, b2, g = ew
                hj = jax.nn.relu(flat @ w1 + b1)
                yj = hj @ w2 + b2
                return (acc + yj * g[:, None], None)
            rout0 = jnp.zeros_like(flat)
            rout, _ = jax.lax.scan(step, rout0, (routed_w1, routed_b1, routed_w2, routed_b2, gating.T))
            return (out + rout).reshape(b, s, d)
        key = jax.random.key(seed)
        ks = jax.random.split(key, 10)
        s1 = 1.0 / np.sqrt(D_MODEL)
        s2 = 1.0 / np.sqrt(D_FF)
        return {'u': jax.random.normal(ks[0], (B, S, D_MODEL), dtype=jnp.float32), 'shared_w1': jax.random.normal(ks[1], (NS, D_MODEL, D_FF), dtype=jnp.float32) * s1, 'shared_b1': jnp.zeros((NS, D_FF), dtype=jnp.float32), 'shared_w2': jax.random.normal(ks[2], (NS, D_FF, D_MODEL), dtype=jnp.float32) * s2, 'shared_b2': jnp.zeros((NS, D_MODEL), dtype=jnp.float32), 'routed_w1': jax.random.normal(ks[3], (NR, D_MODEL, D_FF), dtype=jnp.float32) * s1, 'routed_b1': jnp.zeros((NR, D_FF), dtype=jnp.float32), 'routed_w2': jax.random.normal(ks[4], (NR, D_FF, D_MODEL), dtype=jnp.float32) * s2, 'routed_b2': jnp.zeros((NR, D_MODEL), dtype=jnp.float32), 'centroids': jax.random.normal(ks[5], (NR, D_MODEL), dtype=jnp.float32) * s1, 'bias': jnp.zeros((NR,), dtype=jnp.float32)}
    _L1_ffn_in = _L1_ffn_setup()
    _d = {'L0_attn_x': _L0_attn_in['x'], 'L0_attn_Wk': _L0_attn_in['Wk'], 'L0_attn_Wv': _L0_attn_in['Wv'], 'L0_attn_Wr': _L0_attn_in['Wr'], 'L0_attn_Wo': _L0_attn_in['Wo'], 'L0_attn_tm_k': _L0_attn_in['tm_k'], 'L0_attn_tm_v': _L0_attn_in['tm_v'], 'L0_attn_tm_r': _L0_attn_in['tm_r'], 'L0_attn_time_decay': _L0_attn_in['time_decay'], 'L0_attn_time_first': _L0_attn_in['time_first'], 'L0_attn_ln_g': _L0_attn_in['ln_g'], 'L0_attn_ln_b': _L0_attn_in['ln_b'], 'L0_ffn_gate_w': _L0_ffn_in['gate_w'], 'L0_ffn_w_gate': _L0_ffn_in['w_gate'], 'L0_ffn_w_up': _L0_ffn_in['w_up'], 'L0_ffn_w_down': _L0_ffn_in['w_down'], 'L1_attn_Wq_sem': _L1_attn_in['Wq_sem'], 'L1_attn_Wk_sem': _L1_attn_in['Wk_sem'], 'L1_attn_Wq_geo': _L1_attn_in['Wq_geo'], 'L1_attn_Wk_geo': _L1_attn_in['Wk_geo'], 'L1_attn_Wv': _L1_attn_in['Wv'], 'L1_attn_Wo': _L1_attn_in['Wo'], 'L1_attn_logit_scale': _L1_attn_in['logit_scale'], 'L1_ffn_shared_w1': _L1_ffn_in['shared_w1'], 'L1_ffn_shared_b1': _L1_ffn_in['shared_b1'], 'L1_ffn_shared_w2': _L1_ffn_in['shared_w2'], 'L1_ffn_shared_b2': _L1_ffn_in['shared_b2'], 'L1_ffn_routed_w1': _L1_ffn_in['routed_w1'], 'L1_ffn_routed_b1': _L1_ffn_in['routed_b1'], 'L1_ffn_routed_w2': _L1_ffn_in['routed_w2'], 'L1_ffn_routed_b2': _L1_ffn_in['routed_b2'], 'L1_ffn_centroids': _L1_ffn_in['centroids'], 'L1_ffn_bias': _L1_ffn_in['bias']}
    _x0 = _d['L0_attn_x']
    _d['L0_attn_x'] = jax.random.normal(jax.random.fold_in(jax.random.key(seed), 1), (1, 2048, 512), dtype=_x0.dtype)
    del _x0
    return _d

def reference(L0_attn_x, L0_attn_Wk, L0_attn_Wv, L0_attn_Wr, L0_attn_Wo, L0_attn_tm_k, L0_attn_tm_v, L0_attn_tm_r, L0_attn_time_decay, L0_attn_time_first, L0_attn_ln_g, L0_attn_ln_b, L0_ffn_gate_w, L0_ffn_w_gate, L0_ffn_w_up, L0_ffn_w_down, L1_attn_Wq_sem, L1_attn_Wk_sem, L1_attn_Wq_geo, L1_attn_Wk_geo, L1_attn_Wv, L1_attn_Wo, L1_attn_logit_scale, L1_ffn_shared_w1, L1_ffn_shared_b1, L1_ffn_shared_w2, L1_ffn_shared_b2, L1_ffn_routed_w1, L1_ffn_routed_b1, L1_ffn_routed_w2, L1_ffn_routed_b2, L1_ffn_centroids, L1_ffn_bias):

    def _L0_attn_ref(x, Wk, Wv, Wr, Wo, tm_k, tm_v, tm_r, time_decay, time_first, ln_g, ln_b):
        import jax, jax.numpy as jnp
        import numpy as np
        B, T, D = (4, 1024, 512)
        LAYER_ID, N_LAYERS = (0, 12)
        LN_EPS = 1e-05

        def _wkv(w, u, k, v):
            Bb, Tt, Dd = k.shape
            neg_ew = -jnp.exp(w)

            def step(carry, kv):
                aa, bb, pp = carry
                kt, vt = kv
                qt = jnp.maximum(pp, kt + u)
                e1 = jnp.exp(pp - qt)
                e2 = jnp.exp(kt + u - qt)
                out = (e1 * aa + e2 * vt) / (e1 * bb + e2)
                pp_new = jnp.maximum(pp + neg_ew, kt)
                f1 = jnp.exp(pp - pp_new)
                f2 = jnp.exp(kt - pp_new)
                return ((f1 * aa + f2 * vt, f1 * bb + f2, pp_new), out)
            init = (jnp.zeros((Bb, Dd), k.dtype), jnp.zeros((Bb, Dd), k.dtype), jnp.full((Bb, Dd), -1e+38, k.dtype))
            kT = jnp.swapaxes(k, 0, 1)
            vT = jnp.swapaxes(v, 0, 1)
            _, outT = jax.lax.scan(step, init, (kT, vT))
            return jnp.swapaxes(outT, 0, 1)
        xs = jnp.pad(x, ((0, 0), (1, 0), (0, 0)))[:, :-1, :]
        xk = x * tm_k + xs * (1.0 - tm_k)
        xv = x * tm_v + xs * (1.0 - tm_v)
        xr = x * tm_r + xs * (1.0 - tm_r)
        k = jnp.einsum('btd,ed->bte', xk, Wk)
        v = jnp.einsum('btd,ed->bte', xv, Wv)
        r = jax.nn.sigmoid(jnp.einsum('btd,ed->bte', xr, Wr))
        wkv = _wkv(time_decay, time_first, k, v)
        mu = jnp.mean(wkv, axis=-1, keepdims=True)
        var = jnp.mean(jnp.square(wkv - mu), axis=-1, keepdims=True)
        ln = (wkv - mu) * jax.lax.rsqrt(var + LN_EPS) * ln_g + ln_b
        rwkv = r * ln
        return jnp.einsum('btd,ed->bte', rwkv, Wo)

    def _L0_ffn_ref(hidden_states, gate_w, w_gate, w_up, w_down):
        import jax, jax.numpy as jnp
        import numpy as np
        B, S, D, FF, E = (4, 512, 512, 2048, 2)
        b, s, d = hidden_states.shape
        x = hidden_states.reshape(-1, d)
        logits = x @ gate_w.T
        probs = jax.nn.softmax(logits.astype(jnp.float32), axis=-1)
        sel = jnp.argmax(probs, axis=-1)
        top_w = jnp.take_along_axis(probs, sel[:, None], axis=-1)
        onehot = jax.nn.one_hot(sel, gate_w.shape[0], dtype=x.dtype)
        g = jnp.einsum('td,efd->etf', x, w_gate)
        u = jnp.einsum('td,efd->etf', x, w_up)
        h = jax.nn.silu(g) * u
        y = jnp.einsum('etf,edf->etd', h, w_down)
        out = jnp.einsum('etd,te->td', y, onehot * top_w)
        return out.reshape(b, s, d)

    def _L1_attn_ref(x, Wq_sem, Wk_sem, Wq_geo, Wk_geo, Wv, Wo, logit_scale):
        import jax, jax.numpy as jnp
        import numpy as np
        D_MODEL = 512
        H = 16
        HKV = 4
        DS = 32
        DG = 32
        DV = 64
        B, T = (2, 1024)
        MB = 64
        LW = 256
        ROPE_BASE = 10000.0
        NEG_INF = -1000000000.0

        def _rope(x, pos, base):
            d = x.shape[-1]
            inv_freq = 1.0 / base ** (jnp.arange(0, d, 2, dtype=jnp.float32) / d)
            ang = pos.astype(jnp.float32)[:, None] * inv_freq
            cos, sin = (jnp.cos(ang), jnp.sin(ang))
            x1, x2 = jnp.split(x, 2, axis=-1)
            return jnp.concatenate([x1 * cos - x2 * sin, x2 * cos + x1 * sin], axis=-1)
        Bq, Tq = (x.shape[0], x.shape[1])
        split = lambda y, h, d: y.reshape(Bq, Tq, h, d).transpose(0, 2, 1, 3)
        q_sem = split(x @ Wq_sem, H, DS)
        k_sem = split(x @ Wk_sem, HKV, DS)
        q_geo = split(x @ Wq_geo, H, DG)
        k_geo = split(x @ Wk_geo, HKV, DG)
        v = split(x @ Wv, HKV, DV)
        pos = jnp.arange(Tq)
        q_geo = _rope(q_geo, pos, ROPE_BASE)
        k_geo = _rope(k_geo, pos, ROPE_BASE)
        remote = Tq - LW
        nblk = remote // MB
        pool = lambda a: jnp.concatenate([a[:, :, :remote].reshape(Bq, HKV, nblk, MB, a.shape[-1]).mean(axis=3), a[:, :, remote:]], axis=2)
        k_sem2, k_geo2, v2 = (pool(k_sem), pool(k_geo), pool(v))
        k_pos = jnp.concatenate([jnp.arange(nblk) * MB + (MB - 1), jnp.arange(remote, Tq)])
        rep = lambda a: jnp.repeat(a, H // HKV, axis=1)
        k_sem2, k_geo2, v2 = (rep(k_sem2), rep(k_geo2), rep(v2))
        scores = jnp.einsum('bhqd,bhkd->bhqk', q_sem, k_sem2) * (1.0 / jnp.sqrt(float(DS))) + jnp.einsum('bhqd,bhkd->bhqk', q_geo, k_geo2) * (1.0 / jnp.sqrt(float(DG)))
        scores = scores * jnp.exp(logit_scale)[None, :, None, None]
        mask = k_pos[None, :] <= pos[:, None]
        scores = jnp.where(mask[None, None], scores, NEG_INF)
        probs = jax.nn.softmax(scores, axis=-1)
        out = jnp.einsum('bhqk,bhkd->bhqd', probs, v2)
        out = out.transpose(0, 2, 1, 3).reshape(Bq, Tq, H * DV)
        return out @ Wo

    def _L1_ffn_ref(u, shared_w1, shared_b1, shared_w2, shared_b2, routed_w1, routed_b1, routed_w2, routed_b2, centroids, bias):
        import jax, jax.numpy as jnp
        import numpy as np
        D_MODEL, D_FF, NS, NR, KR = (512, 352, 2, 16, 4)
        B, S = (4, 512)

        def _moe_forward(u, shared_w1, shared_b1, shared_w2, shared_b2, routed_w1, routed_b1, routed_w2, routed_b2, centroids, bias):
            b, s, d = u.shape
            flat = u.reshape(-1, d)
            T = flat.shape[0]
            h = jax.nn.relu(jnp.einsum('td,ndf->ntf', flat, shared_w1) + shared_b1[:, None, :])
            shared_out = jnp.einsum('ntf,nfd->td', h, shared_w2) + shared_b2.sum(0)
            out = flat + shared_out
            scores = jax.nn.sigmoid(flat @ centroids.T) + bias
            vals, idx = jax.lax.top_k(scores, KR)
            gating = jnp.zeros_like(scores).at[jnp.arange(T)[:, None], idx].set(vals)
            gating = gating / jnp.clip(gating.sum(-1, keepdims=True), 1e-08)

            def step(acc, ew):
                w1, b1, w2, b2, g = ew
                hj = jax.nn.relu(flat @ w1 + b1)
                yj = hj @ w2 + b2
                return (acc + yj * g[:, None], None)
            rout0 = jnp.zeros_like(flat)
            rout, _ = jax.lax.scan(step, rout0, (routed_w1, routed_b1, routed_w2, routed_b2, gating.T))
            return (out + rout).reshape(b, s, d)
        return _moe_forward(u, shared_w1, shared_b1, shared_w2, shared_b2, routed_w1, routed_b1, routed_w2, routed_b2, centroids, bias)
    x = L0_attn_x
    xn = _layernorm(x, axis=-1)
    s = _L0_attn_ref(xn, L0_attn_Wk, L0_attn_Wv, L0_attn_Wr, L0_attn_Wo, L0_attn_tm_k, L0_attn_tm_v, L0_attn_tm_r, L0_attn_time_decay, L0_attn_time_first, L0_attn_ln_g, L0_attn_ln_b)
    g = _silu(_L0_ffn_ref(xn, L0_ffn_gate_w, L0_ffn_w_gate, L0_ffn_w_up, L0_ffn_w_down))
    x = x + s * g
    xn = _layernorm(x, axis=-1)
    s = _L1_attn_ref(xn, L1_attn_Wq_sem, L1_attn_Wk_sem, L1_attn_Wq_geo, L1_attn_Wk_geo, L1_attn_Wv, L1_attn_Wo, L1_attn_logit_scale)
    g = _silu(_L1_ffn_ref(xn, L1_ffn_shared_w1, L1_ffn_shared_b1, L1_ffn_shared_w2, L1_ffn_shared_b2, L1_ffn_routed_w1, L1_ffn_routed_b1, L1_ffn_routed_w2, L1_ffn_routed_b2, L1_ffn_centroids, L1_ffn_bias))
    x = x + s * g
    return x

_drawn_inputs = setup_inputs


def setup_inputs(seed=0):
    import zlib

    import numpy as np

    out = dict(_drawn_inputs(seed))
    spreads = {'L0_attn_ln_g': (1.0, 0.2),
     'L0_attn_ln_b': (0.0, 0.1),
     'L1_attn_logit_scale': (0.0, 0.1),
     'L1_ffn_shared_b1': (0.0, 0.1),
     'L1_ffn_shared_b2': (0.0, 0.1),
     'L1_ffn_routed_b1': (0.0, 0.1),
     'L1_ffn_routed_b2': (0.0, 0.1),
     'L1_ffn_bias': (0.0, 0.1)}
    factors = {}
    for name, (base, spread) in spreads.items():
        noise = np.random.default_rng([zlib.crc32(name.encode()), seed]).standard_normal(out[name].shape)
        drawn = base * np.exp(spread * noise) if base else spread * noise
        out[name] = jnp.asarray(drawn.astype(out[name].dtype))
    for name, factor in factors.items():
        out[name] = (out[name] * factor).astype(out[name].dtype)
    return out
```

```python
from contextlib import ExitStack

import concourse.bass as bass
from concourse import mybir

F32 = mybir.dt.float32
F32R = mybir.dt.float32r
ALU = mybir.AluOpType
ACT = mybir.ActivationFunctionType
AX = mybir.AxisListType

P = 128
D = 512
KC = D // P
T = 2048
NT = T // P
TB = 4
BLK = T // TB
TPB = BLK // P
WCOLS = 3072

HI, LO = 0, 1
PASSES = [(HI, HI), (HI, LO), (LO, HI)]


def f32(ap):
    return ap.bitcast(F32)


class Pools:

    def __init__(self, nc, ctx, tag):
        self.nc, self.ctx, self.tag, self.sems = nc, ctx, tag, []
        ctx.callback(self.give_back)

    def sb(self, name, shape, dt=F32):
        return self.ctx.enter_context(self.nc.sbuf_tensor(f"{self.tag}_{name}", shape, dt))

    def ps(self, name, shape, dt=F32):
        return self.ctx.enter_context(self.nc.psum_tensor(f"{self.tag}_ps_{name}", shape, dt))

    def sem(self, name):
        self.sems.append(self.nc.alloc_semaphore(f"{self.tag}_{name}"))
        return self.sems[-1]

    def give_back(self):
        self.nc.clear_and_free_semaphores(self.sems)
        self.nc.all_engine_barrier()


class Chain:

    def __init__(self, eng, sem, base=0):
        self.eng, self.sem, self.n = eng, sem, base

    def __call__(self, ins):
        self.n = self.n + 1
        ins.then_inc(self.sem, 1)
        self.eng.wait_ge(self.sem, self.n)


def layernorm_stage(nc, tag, x_dram, ident_dram, keep, xT_dram=None):
    with ExitStack() as ctx:
        a = Pools(nc, ctx, tag)
        ident = a.sb("ident", [P, P])
        stats = a.sb("stats", [P, NT, 6])
        mv = a.sb("mv", [P, NT, 2])
        rstd = a.sb("rstd", [P, NT])
        eps = a.sb("eps", [P, 1])
        whole = [a.sb(f"whole{i}", [P, KC, BLK]) for i in range(2)] if xT_dram is not None else None
        banks = [a.ps(f"xT{i}", [P, KC, P]) for i in range(8)]
        s_wh = a.sem("whole_ready")
        s_st2 = [a.sem(f"whole_stored{i}") for i in range(2)]
        s_x = [a.sem(f"x_loaded{t}") for t in range(4)]
        s_id = a.sem("ident_loaded")
        s_eps = a.sem("eps_set")
        s_st = a.sem("stats_step")
        s_var = a.sem("var_ready")
        s_std = a.sem("std_ready")
        s_n = a.sem("norm_step")
        s_xn = a.sem("xn_ready")
        s_tr = a.sem("transposed")
        s_hi = a.sem("hi_ready")
        s_lo = a.sem("lo_ready")
        block = ctx.enter_context(nc.Block())
        y, xn = keep.y, keep.xn

        @block.sync
        def _(sp):
            sp.dma_start(ident[:], ident_dram).then_inc(s_id, 16)
            for b in range(4):
                sp.dma_start(y[:, 4 * b:4 * b + 4, :], x_dram[512 * b:512 * b + 512, :]
                             .rearrange("(t p) d -> p t d", p=P)).then_inc(s_x[b], 16)
            if whole:
                for b in range(4):
                    sp.wait_ge(s_wh, 4 * b + 4)
                    sp.dma_start(xT_dram[:, :, b * BLK:(b + 1) * BLK], whole[b % 2][:]).then_inc(s_st2[b % 2], 16)
                for i in range(2):
                    sp.wait_ge(s_st2[i], 32)

        @block.vector
        def _(dve):
            nc.vector.memset(eps[:], 1e-5).then_inc(s_eps, 1)
            for t in range(NT):
                if t % 4 == 0:
                    dve.wait_ge(s_x[t // 4], 16)
                nc.vector.bn_stats(stats[:, t, :], y[:, t, :]).then_inc(s_st, 1)
            for t in range(NT):
                dve.wait_ge(s_st, t + 1)
                nc.vector.bn_aggr(mv[:, t, :], stats[:, t, :]).then_inc(s_var, 1)
            dve.wait_ge(s_std, 1)
            nc.vector.reciprocal(rstd[:], rstd[:]).then_inc(s_n, 1)
            dve.wait_ge(s_n, 1)
            for t in range(NT):
                nc.vector.tensor_scalar(y[:, t, :], y[:, t, :], mv[:, t, 0:1], rstd[:, t:t + 1],
                                        ALU.subtract, ALU.mult).then_inc(s_xn, 1)
            for t in range(NT):
                dve.wait_ge(s_hi, t + 1)
                cols = slice(t * P, (t + 1) * P)
                if whole:
                    b = t // 4
                    if b >= 2:
                        dve.wait_ge(s_st2[b % 2], 16)
                    nc.vector.tensor_copy(whole[b % 2][:, :, (t % 4) * P:(t % 4 + 1) * P],
                                          banks[t % 8][:]).then_inc(s_wh, 1)
                nc.vector.tensor_tensor(xn[LO][:, :, cols], banks[t % 8][:], f32(xn[HI][:, :, cols]),
                                        ALU.subtract).then_inc(s_lo, 1)

        @block.scalar
        def _(act):
            act.wait_ge(s_eps, 1)
            act.wait_ge(s_var, NT)
            nc.scalar.activation(rstd[:], mv[:, :, 1], ACT.Sqrt, bias=eps[:]).then_inc(s_std, 1)
            for t in range(NT):
                act.wait_ge(s_tr, t + 1)
                nc.scalar.copy(xn[HI][:, :, t * P:(t + 1) * P], banks[t % 8][:]).then_inc(s_hi, 1)

        @block.tensor
        def _(pe):
            pe.wait_ge(s_id, 16)
            for t in range(NT):
                pe.wait_ge(s_xn, t + 1)
                if t >= 8:
                    pe.wait_ge(s_lo, t - 7)
                for c in range(KC):
                    last = nc.tensor.transpose(banks[t % 8][:, c, :], y[:, t, c * P:(c + 1) * P], ident[:])
                last.then_inc(s_tr, 1)


def expert_stage(nc, tag, w_dram, groups, gated, gate_of, router, keep, finish):
    FC = 2 if gated else 3
    MATS = 2 if gated else 1
    NB = FC * MATS
    HID = FC * P
    DOWN = MATS * KC * HID
    steps = groups * TB
    with ExitStack() as ctx:
        a = Pools(nc, ctx, tag)
        raw = a.sb("raw", [P, WCOLS])
        w = [[a.sb(f"w{j}{'hl'[s]}", [P, WCOLS], F32R) for s in (HI, LO)] for j in range(2)]
        h = [[a.sb(f"h{j}{'hl'[s]}", [P, FC, BLK], F32R) for s in (HI, LO)] for j in range(2)]
        h32 = [a.sb(f"h32_{f}", [P, BLK]) for f in range(FC)]
        sil = [a.sb(f"silu{f}", [P, BLK]) for f in range(FC)] if gated else None
        hb = [a.ps(f"hid{b}", [P, BLK]) for b in range(NB)]
        yb = [a.ps(f"y{b}", [P, D]) for b in range(TPB)]
        s_raw = a.sem("raw_loaded")
        s_whi = a.sem("w_hi_ready")
        s_w = a.sem("w_ready")
        s_hid = a.sem("hidden_summed")
        s_sil = a.sem("silu_ready")
        s_h32 = a.sem("h32_ready")
        s_hhi = a.sem("h_hi_ready")
        s_h = a.sem("h_ready")
        s_y = a.sem("y_summed")
        s_yadd = a.sem("y_added")
        s_bias = a.sem("bias_ready")
        bias = None if gated else a.sb("bias_now", [P, 2, FC])
        env = router(a, hb, yb)
        fin = finish(a, env, hb, yb, h, s_y, steps * TPB)
        block = ctx.enter_context(nc.Block())
        xn, y = keep.xn, keep.y

        def pairs(eng, body):
            body(0, True)
            with eng.Fori(1, groups // 2) as i:
                body(i, False)

        @block.sync
        def _(sp):
            env.sync(sp)

            def load(i, first):
                for j in range(2):
                    g = 2 * i + j
                    if not (first and j == 0):
                        sp.wait_ge(s_w, g)
                    sp.dma_start(raw[:], w_dram[g, :, :] if first else
                                 w_dram[bass.ds(g, 1), :, :].rearrange("g p n -> p (g n)")).then_inc(s_raw, 16)
            pairs(sp, load)
            fin.sync(sp)

        @block.gpsimd
        def _(pool):
            def weights_lo(g, j):
                pool.wait_ge(s_whi, g + 1)
                nc.gpsimd.tensor_tensor(w[j][LO][:], raw[:], f32(w[j][HI][:]), ALU.subtract).then_inc(s_w, 1)

            def hidden(i, first, last=False):
                for j in range(2):
                    for tb in range(TB):
                        k = (2 * i + j) * TB + tb
                        for f in range(FC):
                            pool.wait_ge(s_hhi, k * FC + f + 1)
                            nc.gpsimd.tensor_tensor(h[tb % 2][LO][:, f, :], h32[f][:], f32(h[tb % 2][HI][:, f, :]),
                                                    ALU.subtract).then_inc(s_h, 1)
                        if tb == 1 and j == 0:
                            weights_lo(2 * i + 1, 1)
                        if tb == 1 and j == 1 and not last:
                            weights_lo(2 * i + 2, 0)

            weights_lo(0, 0)
            hidden(0, True)
            with pool.Fori(1, groups // 2 - 1) as i:
                hidden(i, False)
            hidden(groups // 2 - 1, False, last=True)

        @block.scalar
        def _(act):
            def weights_hi(g, j, fresh):
                act.wait_ge(s_raw, 16 * g + 16)
                if not fresh:
                    act.wait_ge(s_y, TB * TPB * (g - 1))
                nc.scalar.copy(w[j][HI][:], raw[:]).then_inc(s_whi, 1)

            def hidden(i, first, last=False):
                for j in range(2):
                    g = 2 * i + j
                    if not gated:
                        src = env.b1[:, :, g] if first else env.b1[:, :, bass.ds(g, 1)].rearrange("p f g -> p (f g)")
                        nc.scalar.copy(bias[:, j, :], src).then_inc(s_bias, 1)
                    for tb in range(TB):
                        k = g * TB + tb
                        fresh = first and j == 0 and tb == 0
                        if gated:
                            for f in range(FC):
                                act.wait_ge(s_hid, k * NB + 2 * f + 1)
                                if not fresh:
                                    act.wait_ge(s_h32, (k - 1) * FC + f + 1)
                                nc.scalar.activation(sil[f][:], hb[2 * f][:], ACT.Silu).then_inc(s_sil, 1)
                        else:
                            for f in range(FC):
                                act.wait_ge(s_hid, k * NB + f + 1)
                                if not fresh:
                                    act.wait_ge(s_h, (k - 1) * FC + f + 1)
                                if tb == 0 and f == 0:
                                    act.wait_ge(s_bias, 2 * i + j + 1)
                                nc.scalar.activation(h32[f][:], hb[f][:], ACT.Relu, bias=bias[:, j, f:f + 1])\
                                  .then_inc(s_h32, 1)
                        for f in range(FC):
                            act.wait_ge(s_h32, k * FC + f + 1)
                            if f == 0 and not (first and j == 0 and tb < 2):
                                act.wait_ge(s_y, (k - 1) * TPB)
                            nc.scalar.copy(h[tb % 2][HI][:, f, :], h32[f][:]).then_inc(s_hhi, 1)
                        if tb == 1 and j == 0:
                            weights_hi(2 * i + 1, 1, first)
                        if tb == 1 and j == 1 and not last:
                            weights_hi(2 * i + 2, 0, False)

            weights_hi(0, 0, True)
            env.scalar(act)
            hidden(0, True)
            with act.Fori(1, groups // 2 - 1) as i:
                hidden(i, False)
            hidden(groups // 2 - 1, False, last=True)
            fin.scalar(act)

        @block.vector
        def _(dve):
            env.vector(dve)

            def add_y(g, k, tb, dyn):
                for tt in range(TPB):
                    tile = tb * TPB + tt
                    dve.wait_ge(s_y, k * TPB + tt + 1)
                    gate = gate_of(env, g, tile, dyn)
                    nc.vector.scalar_tensor_tensor(y[:, tile, :], yb[tt][:], gate, y[:, tile, :],
                                                   ALU.mult, ALU.add).then_inc(s_yadd, 1)

            def work(i, first):
                for j in range(2):
                    for tb in range(TB):
                        g = 2 * i + j
                        k = g * TB + tb
                        if gated:
                            for f in range(FC):
                                dve.wait_ge(s_sil, k * FC + f + 1)
                                dve.wait_ge(s_hid, k * NB + 2 * f + 2)
                                if not (first and j == 0 and tb == 0):
                                    dve.wait_ge(s_h, (k - 1) * FC + f + 1)
                                nc.vector.tensor_tensor(h32[f][:], hb[2 * f + 1][:], sil[f][:],
                                                        ALU.mult).then_inc(s_h32, 1)
                        if first and j == 0 and tb == 0:
                            continue
                        add_y(g if tb else g - 1, k - 1, (tb - 1) % TB, not first)
            pairs(dve, work)
            add_y(groups - 1, steps - 1, TB - 1, False)
            fin.vector(dve)

        @block.tensor
        def _(pe):
            env.tensor(pe)

            def hidden(j, tb, k, fresh):
                for f in range(FC):
                    for m in range(MATS):
                        b = f * MATS + m
                        if not fresh:
                            pe.wait_ge(s_h32, (k - 1) * FC + f + 1)
                        for c in range(KC):
                            col = (m * KC + c) * HID + f * P
                            for n, (p, q) in enumerate(PASSES):
                                last = nc.tensor.matmul(hb[b][:], w[j][p][:, col:col + P],
                                                        xn[q][:, c, tb * BLK:(tb + 1) * BLK],
                                                        start=(c == 0 and n == 0), stop=(c == KC - 1 and n == 2))
                        last.then_inc(s_hid, 1)

            def down(j, tb, k, fresh):
                pe.wait_ge(s_h, (k + 1) * FC)
                if fresh:
                    env.tensor_before_y(pe)
                for tt in range(TPB):
                    if not fresh:
                        pe.wait_ge(s_yadd, (k - 1) * TPB + tt + 1)
                    for f in range(FC):
                        for n, (p, q) in enumerate(PASSES):
                            last = nc.tensor.matmul(yb[tt][:], h[tb % 2][p][:, f, tt * P:(tt + 1) * P],
                                                    w[j][q][:, DOWN + f * D:DOWN + (f + 1) * D],
                                                    start=(f == 0 and n == 0), stop=(f == FC - 1 and n == 2))
                    last.then_inc(s_y, 1)

            def work(i, first):
                for j in range(2):
                    g = 2 * i + j
                    pe.wait_ge(s_w, g + 1)
                    for tb in range(TB):
                        k = g * TB + tb
                        fresh = first and j == 0
                        hidden(j, tb, k, fresh and tb == 0)
                        if fresh and tb == 0:
                            continue
                        down(j if tb else 1 - j, (tb - 1) % TB, k - 1, fresh and tb == 1)
            pairs(pe, work)
            down(1, TB - 1, steps - 1, False)
            fin.tensor(pe)


class Stage:

    def sync(self, eng): pass
    def scalar(self, eng): pass
    def vector(self, eng): pass
    def tensor(self, eng): pass
    def tensor_before_y(self, eng): pass


def top1_router(nc, gw_dram, groups, keep):
    E = 2

    def router(a, hb, yb):
        env = Stage()
        raw = a.sb("gw_raw", [P, KC, E])
        gw = [a.sb(f"gw{'hl'[s]}", [P, KC, E], F32R) for s in (HI, LO)]
        lg = a.sb("logits", [P, NT, E])
        red = a.sb("red", [P, NT])
        pr = a.sb("probs", [P, E, NT])
        sel = a.sb("sel", [P, E, NT])
        env.gates = a.sb("gates", [P, groups, NT])
        ps = yb[0][:, 0:NT * E].rearrange("p (t e) -> p t e", e=E)
        s_in = a.sem("gw_loaded")
        s_c = a.sem("gate_chain")
        s_gw = a.sem("gw_ready")
        s_lg = a.sem("logits_summed")
        s_read = a.sem("logits_read")
        s_e = a.sem("gate_exp")
        s_d = a.sem("gate_shifted")

        def sync(sp):
            sp.dma_start(raw[:], gw_dram).then_inc(s_in, 16)

        def vector(dve):
            link = Chain(dve, s_c)
            dve.wait_ge(s_in, 16)
            link(nc.vector.tensor_copy(gw[HI][:], raw[:]))
            nc.vector.tensor_tensor(gw[LO][:], raw[:], f32(gw[HI][:]), ALU.subtract).then_inc(s_gw, 1)
            link(nc.vector.memset(keep.y[:], 0.0))
            dve.wait_ge(s_lg, 1)
            nc.vector.tensor_copy(lg[:], ps).then_inc(s_read, 1)
            dve.wait_ge(s_read, 1)
            link(nc.vector.tensor_reduce(red[:], lg[:], AX.X, ALU.max))
            nc.vector.tensor_tensor(lg[:], lg[:], red[:].unsqueeze(2).to_broadcast([P, NT, E]),
                                    ALU.subtract).then_inc(s_d, 1)
            dve.wait_ge(s_e, 1)
            link(nc.vector.tensor_reduce(red[:], lg[:], AX.X, ALU.add))
            link(nc.vector.reciprocal(red[:], red[:]))
            link(nc.vector.tensor_tensor(pr[:].rearrange("p e t -> p t e"), lg[:],
                                         red[:].unsqueeze(2).to_broadcast([P, NT, E]), ALU.mult))
            link(nc.vector.tensor_tensor(sel[:, 0, :], pr[:, 0, :], pr[:, 1, :], ALU.is_ge))
            link(nc.vector.tensor_scalar(sel[:, 1, :], sel[:, 0, :], -1.0, 1.0, ALU.mult, ALU.add))
            link(nc.vector.tensor_tensor(pr[:], pr[:], sel[:], ALU.mult))
            half = groups // E
            for e in range(E):
                link(nc.vector.tensor_copy(env.gates[:, e * half:(e + 1) * half, :],
                                           pr[:, e:e + 1, :].to_broadcast([P, half, NT])))

        def scalar(act):
            act.wait_ge(s_d, 1)
            nc.scalar.activation(lg[:], lg[:], ACT.Exp).then_inc(s_e, 1)

        def tensor(pe):
            pe.wait_ge(s_gw, 1)
            for t in range(NT):
                for c in range(KC):
                    for n, (p, q) in enumerate(PASSES):
                        last = nc.tensor.matmul(ps[:, t, :], keep.xn[p][:, c, t * P:(t + 1) * P], gw[q][:, c, :],
                                                start=(c == 0 and n == 0), stop=(c == KC - 1 and n == 2))
            last.then_inc(s_lg, 1)

        env.sync, env.vector, env.scalar, env.tensor = sync, vector, scalar, tensor
        env.tensor_before_y = lambda pe: pe.wait_ge(s_read, 1)
        return env

    return router


def silu_out(nc, out_dram, keep):
    def finish(a, env, hb, yb, h, s_y, y_all):
        fin = Stage()
        s_g = a.sem("silu_y_ready")
        s_out = a.sem("silu_y_stored")
        s_last = a.sem("y_final")

        def vector(dve):
            nc.vector.drain().then_inc(s_last, 1)

        def scalar(act):
            act.wait_ge(s_last, 1)
            for t in range(NT):
                nc.scalar.activation(keep.y[:, t, :], keep.y[:, t, :], ACT.Silu).then_inc(s_g, 1)

        def sync(sp):
            for b in range(4):
                sp.wait_ge(s_g, 4 * b + 4)
                sp.dma_start(out_dram[512 * b:512 * b + 512, :].rearrange("(t p) d -> p t d", p=P),
                             keep.y[:, 4 * b:4 * b + 4, :]).then_inc(s_out, 16)
            sp.wait_ge(s_out, 64)

        fin.vector, fin.scalar, fin.sync = vector, scalar, sync
        return fin
    return finish


def time_mix_stage(nc, w_dram, vec_dram, xT_dram, x_dram, g_dram, x1_dram):
    TM_K, TM_V, TM_R, DECAY, FIRST, LN_G, LN_B = range(7)
    K_, V_, R_, O_ = range(4)
    with ExitStack() as ctx:
        a = Pools(nc, ctx, "mix")
        x = a.sb("x", [P, KC, T])
        low = a.sb("low", [P, 16, BLK]) 
        w = [[a.sb(f"w{m}{'hl'[s]}", [P, KC, D], F32R) for s in (HI, LO)] for m in range(4)]
        mix = [[a.sb(f"mix{m}{'hl'[s]}", [P, KC, BLK], F32R) for s in (HI, LO)] for m in range(3)]
        r, wk = low[:, 0:4, :], low[:, 4:8, :]
        d = [low[:, 8 + i, :] for i in range(2)]
        xm = [low[:, 10 + i, :] for i in range(2)]
        e_sep = a.sb("e1", [P, 4, BLK])
        E = [low[:, 12:16, :], e_sep[:]]
        ks = [a.sb(f"k{i}", [P, BLK]) for i in range(2)]
        vs = [a.sb(f"v{i}", [P, BLK]) for i in range(2)]
        pp = [a.sb(f"pp{i}", [P, BLK + 1]) for i in range(2)]
        aa = a.sb("aa", [P, BLK + 1])
        bb = a.sb("bb", [P, BLK + 1])
        q = [a.sb(f"q{i}", [P, BLK]) for i in range(2)]
        f2v = a.sb("f2v", [P, BLK])
        vec = a.sb("vec", [P, 7, KC])
        negew = a.sb("negew", [P, KC])
        carry = a.sb("carry", [P, 3, KC])
        mean_w = a.sb("mean_w", [P, P], F32R)
        eps = a.sb("eps", [P, 1])
        kp = [a.ps(f"k{i}", [P, BLK]) for i in range(2)]
        vp = [a.ps(f"v{i}", [P, BLK]) for i in range(2)]
        rp = [a.ps(f"r{i}", [P, BLK]) for i in range(2)]
        mp = a.ps("mean", [P, BLK])
        qp = a.ps("var", [P, BLK])
        sp_banks = [kp[0], vp[0], kp[1], vp[1]]

        names = """const w_loaded w_hi w_split x_whole consts diff mixed mix_hi mix_lo k_sum v_sum r_sum kv_read
            pp_scan carry shifts q e2_arg exps f2v scans den num wkv r_read r_gate w_hi_part w_lo_part mean_sum
            centred square sq_hi sq_lo var_sum std rstd normed affine gated g_hi g_lo s_sum scaled x1
            negew one""".split()
        S = {n: a.sem(n) for n in names}
        tiles_in = [a.sem(f"tiles_loaded{i}") for i in range(2)]
        stored = [a.sem(f"x1_stored{i}") for i in range(2)]
        block = ctx.enter_context(nc.Block())

        def blocks(eng, body):
            body(0, True)
            with eng.Fori(1, TB) as tb:
                body(tb, False)

        @block.sync
        def _(sp):
            sp.dma_start(vec[:], vec_dram).then_inc(S["const"], 16)
            for b in range(TB):
                sp.dma_start(x[:, :, b * BLK:(b + 1) * BLK], xT_dram[:, :, b * BLK:(b + 1) * BLK])\
                  .then_inc(S["x_whole"], 16)
            for m in range(4):
                if m:
                    sp.wait_ge(S["w_split"], m)
                sp.dma_start(e_sep[:], w_dram[m, :, :, :]).then_inc(S["w_loaded"], 16)

            def tiles(tb, first):
                for tt in range(TPB):
                    n = TPB * tb + tt
                    row = n * P
                    rows = (lambda t: t[row:row + P, :]) if first else (lambda t: t[bass.ds(row, P), :])
                    if tt < 2:
                        sp.wait_ge(S["num"], 12 * tb + 12)
                    else:
                        sp.wait_ge(stored[tt % 2], 16 * (2 * tb + tt // 2))
                    sp.dma_start(ks[tt % 2][:], rows(g_dram)).then_inc(tiles_in[tt % 2], 16)
                    sp.dma_start(vs[tt % 2][:], rows(x_dram)).then_inc(tiles_in[tt % 2], 16)
                    if tt >= 1:
                        store(tb, tt - 1, first)
                store(tb, 3, first)

            def store(tb, tt, first):
                n = TPB * tb + tt
                row = n * P
                dst = x1_dram[row:row + P, :] if first else x1_dram[bass.ds(row, P), :]
                sp.wait_ge(S["x1"], n + 1)
                sp.dma_start(dst, ks[tt % 2][:]).then_inc(stored[tt % 2], 16)
            blocks(sp, tiles)
            for i in range(2):
                sp.wait_ge(stored[i], 32 * TB)

        def shifted(tb, c, first):
            return x[:, c, 0:BLK - 1] if first else x[:, c, bass.ds(tb * BLK - 1, BLK)]

        def here(tb, c, first):
            return x[:, c, 0:BLK] if first else x[:, c, bass.ds(tb * BLK, BLK)]

        @block.gpsimd
        def _(pool):
            for m in range(4):
                pool.wait_ge(S["w_hi"], m + 1)
                nc.gpsimd.tensor_tensor(w[m][LO][:], e_sep[:], f32(w[m][HI][:]), ALU.subtract).then_inc(S["w_split"], 1)
            pool.wait_ge(S["x_whole"], 16 * TB)

            def front(tb, c):
                n = KC * tb + c
                j = c % 2
                e = E[j]
                if c >= 2:
                    pool.wait_ge(S["wkv"], n - 1)
                else:
                    pool.wait_ge(S["sq_lo"], KC * tb)
                pool.wait_ge(S["pp_scan"], n + 1)
                nc.gpsimd.tensor_tensor(e[:, 0, :], pp[j][:, 0:BLK], pp[j][:, 1:BLK + 1],
                                        ALU.subtract).then_inc(S["shifts"], 1)
                nc.gpsimd.tensor_tensor(e[:, 1, :], ks[j][:], pp[j][:, 1:BLK + 1], ALU.subtract).then_inc(S["shifts"], 1)
                pool.wait_ge(S["q"], n + 1)
                nc.gpsimd.tensor_tensor(e[:, 2, :], pp[j][:, 0:BLK], q[j][:], ALU.subtract).then_inc(S["shifts"], 1)

            def back(tb, c):
                n = KC * tb + c
                j = c % 2
                e = E[j]
                pool.wait_ge(S["exps"], n + 1)
                pool.wait_ge(S["scans"], 2 * n)
                nc.gpsimd.tensor_tensor(f2v[:], e[:, 1, :], vs[j][:], ALU.mult).then_inc(S["f2v"], 1)
                pool.wait_ge(S["scans"], 2 * n + 2)
                nc.gpsimd.tensor_tensor(e[:, 0, :], e[:, 2, :], aa[:, 0:BLK], ALU.mult).then_inc(S["num"], 1)
                nc.gpsimd.tensor_tensor(e[:, 1, :], e[:, 3, :], vs[j][:], ALU.mult).then_inc(S["num"], 1)
                pool.wait_ge(S["num"], 3 * n + 2)
                nc.gpsimd.tensor_tensor(e[:, 0, :], e[:, 0, :], e[:, 1, :], ALU.add).then_inc(S["num"], 1)

            def body(tb, first):
                for c in range(KC):
                    n = KC * tb + c
                    if c < 2:
                        if not first:
                            pool.wait_ge(S["mixed"], 12 * tb)
                    else:
                        pool.wait_ge(S["mixed"], 12 * tb + 3 * (c - 1))
                    if first:
                        nc.gpsimd.tensor_copy(d[c % 2][:, 0:1], x[:, c, 0:1])
                        nc.gpsimd.tensor_tensor(d[c % 2][:, 1:BLK], x[:, c, 1:BLK], shifted(tb, c, True),
                                                ALU.subtract).then_inc(S["diff"], 1)
                    else:
                        nc.gpsimd.tensor_tensor(d[c % 2][:], here(tb, c, False), shifted(tb, c, False),
                                                ALU.subtract).then_inc(S["diff"], 1)
                    for m in range(3):
                        i = 12 * tb + 3 * c + m
                        pool.wait_ge(S["mix_hi"], i + 1)
                        nc.gpsimd.tensor_tensor(mix[m][LO][:, c, :], xm[(3 * c + m) % 2][:], f32(mix[m][HI][:, c, :]),
                                                ALU.subtract).then_inc(S["mix_lo"], 1)
                front(tb, 0)
                front(tb, 1)
                for c in range(KC):
                    back(tb, c)
                    if c + 2 < KC:
                        front(tb, c + 2)
                for c in range(KC):
                    pool.wait_ge(S["w_hi_part"], KC * tb + c + 1)
                    nc.gpsimd.tensor_tensor(mix[0][LO][:, c, :], wk[:, c, :], f32(mix[0][HI][:, c, :]),
                                            ALU.subtract).then_inc(S["w_lo_part"], 1)
                for c in range(KC):
                    pool.wait_ge(S["sq_hi"], KC * tb + c + 1)
                    nc.gpsimd.tensor_tensor(mix[0][LO][:, c, :], e_sep[:, c, :], f32(mix[0][HI][:, c, :]),
                                            ALU.subtract).then_inc(S["sq_lo"], 1)
                for c in range(KC):
                    pool.wait_ge(S["affine"], KC * tb + c + 1)
                    nc.gpsimd.tensor_tensor(wk[:, c, :], wk[:, c, :], r[:, c, :], ALU.mult).then_inc(S["gated"], 1)
                for c in range(KC):
                    pool.wait_ge(S["g_hi"], KC * tb + c + 1)
                    nc.gpsimd.tensor_tensor(mix[0][LO][:, c, :], wk[:, c, :], f32(mix[0][HI][:, c, :]),
                                            ALU.subtract).then_inc(S["g_lo"], 1)
            blocks(pool, body)

        @block.vector
        def _(dve):
            nc.vector.memset(f32(mean_w[:]), 1.0 / D).then_inc(S["consts"], 1)
            nc.vector.memset(eps[:], 1e-5).then_inc(S["consts"], 1)
            nc.vector.memset(carry[:, 0, :], -1e38).then_inc(S["consts"], 1)
            nc.vector.memset(carry[:, 1:3, :], 0.0).then_inc(S["consts"], 1)
            dve.wait_ge(S["negew"], 1)
            nc.vector.tensor_scalar_mul(negew[:], negew[:], -1.0).then_inc(S["consts"], 1)
            dve.wait_ge(S["consts"], 5)
            dve.wait_ge(S["x_whole"], 16 * TB)

            def front(tb, c, carried):
                n = KC * tb + c
                j = c % 2
                carried(nc.vector.tensor_copy(pp[j][:, 0:1], carry[:, 0, c:c + 1]))
                dve.wait_ge(S["kv_read"], 2 * n + 2)
                nc.vector.tensor_tensor_scan(pp[j][:, 1:BLK + 1], negew[:, c:c + 1].to_broadcast([P, BLK]), ks[j][:],
                                             carry[:, 0, c:c + 1], ALU.add, ALU.max).then_inc(S["pp_scan"], 1)
                dve.wait_ge(S["pp_scan"], n + 1)
                carried(nc.vector.tensor_copy(carry[:, 0, c:c + 1], pp[j][:, BLK:BLK + 1]))
                nc.vector.scalar_tensor_tensor(q[j][:], ks[j][:], vec[:, FIRST, c:c + 1], pp[j][:, 0:BLK],
                                               ALU.add, ALU.max).then_inc(S["q"], 1)
                dve.wait_ge(S["q"], n + 1)
                if c < 2:
                    dve.wait_ge(S["sq_lo"], KC * tb)
                nc.vector.scalar_tensor_tensor(E[j][:, 3, :], ks[j][:], vec[:, FIRST, c:c + 1], q[j][:],
                                               ALU.add, ALU.subtract).then_inc(S["e2_arg"], 1)

            def back(tb, c, carried):
                n = KC * tb + c
                j = c % 2
                e = E[j]
                if c:
                    dve.wait_ge(S["num"], 3 * n)
                elif not (isinstance(tb, int) and tb == 0):
                    dve.wait_ge(S["num"], 3 * n)
                carried(nc.vector.tensor_copy(aa[:, 0:1], carry[:, 1, c:c + 1]))
                carried(nc.vector.tensor_copy(bb[:, 0:1], carry[:, 2, c:c + 1]))
                dve.wait_ge(S["f2v"], n + 1)
                nc.vector.tensor_tensor_scan(aa[:, 1:BLK + 1], e[:, 0, :], f2v[:], carry[:, 1, c:c + 1],
                                             ALU.mult, ALU.add).then_inc(S["scans"], 1)
                nc.vector.tensor_tensor_scan(bb[:, 1:BLK + 1], e[:, 0, :], e[:, 1, :], carry[:, 2, c:c + 1],
                                             ALU.mult, ALU.add).then_inc(S["scans"], 1)
                dve.wait_ge(S["scans"], 2 * n + 2)
                carried(nc.vector.tensor_copy(carry[:, 1, c:c + 1], aa[:, BLK:BLK + 1]))
                carried(nc.vector.tensor_copy(carry[:, 2, c:c + 1], bb[:, BLK:BLK + 1]))
                nc.vector.tensor_tensor(q[j][:], e[:, 2, :], bb[:, 0:BLK], ALU.mult).then_inc(S["den"], 1)
                dve.wait_ge(S["den"], 3 * n + 1)
                nc.vector.tensor_tensor(q[j][:], q[j][:], e[:, 3, :], ALU.add).then_inc(S["den"], 1)
                dve.wait_ge(S["den"], 3 * n + 2)
                nc.vector.reciprocal(q[j][:], q[j][:]).then_inc(S["den"], 1)
                dve.wait_ge(S["den"], 3 * n + 3)
                dve.wait_ge(S["num"], 3 * n + 3)
                nc.vector.tensor_tensor(wk[:, c, :], e[:, 0, :], q[j][:], ALU.mult).then_inc(S["wkv"], 1)

            def body(tb, first):
                for c in range(KC):
                    dve.wait_ge(S["diff"], KC * tb + c + 1)
                    for m in range(3):
                        i = 3 * c + m
                        if not (first and i < 2):
                            dve.wait_ge(S["mix_lo"], 12 * tb + i - 1)
                        o, s = xm[i % 2], vec[:, TM_K + m, c:c + 1]
                        if first:
                            nc.vector.tensor_scalar(o[:, 0:1], d[c % 2][:, 0:1], s, None, ALU.mult)
                            nc.vector.scalar_tensor_tensor(o[:, 1:BLK], d[c % 2][:, 1:BLK], s, shifted(tb, c, True),
                                                           ALU.mult, ALU.add).then_inc(S["mixed"], 1)
                        else:
                            nc.vector.scalar_tensor_tensor(o[:], d[c % 2][:], s, shifted(tb, c, False),
                                                           ALU.mult, ALU.add).then_inc(S["mixed"], 1)
                carried = Chain(dve, S["carry"], 6 * KC * tb)
                front(tb, 0, carried)
                front(tb, 1, carried)
                for c in range(KC):
                    back(tb, c, carried)
                    if c + 2 < KC:
                        front(tb, c + 2, carried)
                dve.wait_ge(S["mean_sum"], tb + 1)
                for c in range(KC):
                    nc.vector.tensor_tensor(wk[:, c, :], wk[:, c, :], mp[:], ALU.subtract).then_inc(S["centred"], 1)
                dve.wait_ge(S["std"], tb + 1)
                nc.vector.reciprocal(q[0][:], q[0][:]).then_inc(S["rstd"], 1)
                dve.wait_ge(S["rstd"], tb + 1)
                for c in range(KC):
                    nc.vector.tensor_tensor(wk[:, c, :], wk[:, c, :], q[0][:], ALU.mult).then_inc(S["normed"], 1)
                for tt in range(TPB):
                    n = TPB * tb + tt
                    dve.wait_ge(S["s_sum"], n + 1)
                    dve.wait_ge(tiles_in[tt % 2], 32 * (2 * tb + tt // 2 + 1))
                    nc.vector.tensor_tensor(ks[tt % 2][:], sp_banks[tt][:], ks[tt % 2][:], ALU.mult).then_inc(S["scaled"], 1)
                    dve.wait_ge(S["scaled"], n + 1)
                    nc.vector.tensor_tensor(ks[tt % 2][:], ks[tt % 2][:], vs[tt % 2][:], ALU.add).then_inc(S["x1"], 1)
            blocks(dve, body)

        @block.scalar
        def _(act):
            act.wait_ge(S["const"], 16)
            nc.scalar.activation(negew[:], vec[:, DECAY, :], ACT.Exp).then_inc(S["negew"], 1)
            for m in range(4):
                act.wait_ge(S["w_loaded"], 16 * m + 16)
                nc.scalar.copy(w[m][HI][:], e_sep[:]).then_inc(S["w_hi"], 1)
            act.wait_ge(S["w_split"], 4)
            act.wait_ge(S["consts"], 5)

            def read_kv(tb, c):
                n = KC * tb + c
                j = c % 2
                if c >= 2:
                    act.wait_ge(S["num"], 3 * (n - 1))
                elif not (isinstance(tb, int) and tb == 0):
                    for i in range(2):
                        act.wait_ge(stored[i], 32 * tb)
                act.wait_ge(S["k_sum"], n + 1)
                nc.scalar.copy(ks[j][:], kp[j][:]).then_inc(S["kv_read"], 1)
                act.wait_ge(S["v_sum"], n + 1)
                nc.scalar.copy(vs[j][:], vp[j][:]).then_inc(S["kv_read"], 1)

            def exps(tb, c):
                n = KC * tb + c
                act.wait_ge(S["shifts"], 3 * n + 3)
                act.wait_ge(S["e2_arg"], n + 1)
                nc.scalar.activation(E[c % 2], E[c % 2], ACT.Exp).then_inc(S["exps"], 1)

            def body(tb, first):
                for c in range(KC):
                    for m in range(3):
                        i = 3 * c + m
                        act.wait_ge(S["mixed"], 12 * tb + i + 1)
                        if not first and c == 0:
                            if m == 0:
                                act.wait_ge(S["s_sum"], TPB * tb)
                            if m == 1:
                                act.wait_ge(S["v_sum"], KC * tb)
                            if m == 2:
                                act.wait_ge(S["r_sum"], KC * tb)
                        nc.scalar.copy(mix[m][HI][:, c, :], xm[i % 2][:]).then_inc(S["mix_hi"], 1)
                read_kv(tb, 0)
                read_kv(tb, 1)
                exps(tb, 0)
                read_kv(tb, 2)
                exps(tb, 1)
                read_kv(tb, 3)
                exps(tb, 2)
                exps(tb, 3)
                for c in range(KC):
                    act.wait_ge(S["r_sum"], KC * tb + c + 1)
                    nc.scalar.activation(r[:, c, :], rp[c % 2][:], ACT.Sigmoid).then_inc(S["r_gate"], 1)
                act.wait_ge(S["k_sum"], KC * tb + KC)
                for c in range(KC):
                    act.wait_ge(S["wkv"], KC * tb + c + 1)
                    nc.scalar.copy(mix[0][HI][:, c, :], wk[:, c, :]).then_inc(S["w_hi_part"], 1)
                for c in range(KC):
                    act.wait_ge(S["centred"], KC * tb + c + 1)
                    nc.scalar.activation(e_sep[:, c, :], wk[:, c, :], ACT.Square).then_inc(S["square"], 1)
                for c in range(KC):
                    act.wait_ge(S["square"], KC * tb + c + 1)
                    nc.scalar.copy(mix[0][HI][:, c, :], e_sep[:, c, :]).then_inc(S["sq_hi"], 1)
                act.wait_ge(S["var_sum"], tb + 1)
                nc.scalar.activation(q[0][:], qp[:], ACT.Sqrt, bias=eps[:]).then_inc(S["std"], 1)
                for c in range(KC):
                    act.wait_ge(S["normed"], KC * tb + c + 1)
                    nc.scalar.activation(wk[:, c, :], wk[:, c, :], ACT.Identity, bias=vec[:, LN_B, c:c + 1],
                                         scale=vec[:, LN_G, c:c + 1]).then_inc(S["affine"], 1)
                for c in range(KC):
                    act.wait_ge(S["gated"], KC * tb + c + 1)
                    nc.scalar.copy(mix[0][HI][:, c, :], wk[:, c, :]).then_inc(S["g_hi"], 1)
            blocks(act, body)

        @block.tensor
        def _(pe):
            pe.wait_ge(S["consts"], 5)

            def project(bank, m, src, c, sem):
                for k in range(KC):
                    for n, (p_, q_) in enumerate(PASSES):
                        last = nc.tensor.matmul(bank[:], w[m][p_][:, k, c * P:(c + 1) * P], mix[src][q_][:, k, :],
                                                start=(k == 0 and n == 0), stop=(k == KC - 1 and n == 2))
                last.then_inc(S[sem], 1)

            def average(bank, sem):
                for k in range(KC):
                    for s in (HI, LO):
                        last = nc.tensor.matmul(bank[:], mean_w[:], mix[0][s][:, k, :],
                                                start=(k == 0 and s == HI), stop=(k == KC - 1 and s == LO))
                last.then_inc(S[sem], 1)

            def body(tb, first):
                pe.wait_ge(S["w_split"], 4)
                pe.wait_ge(S["mix_lo"], 12 * tb + 12)
                for c in range(KC):
                    n = KC * tb + c
                    if c >= 2:
                        pe.wait_ge(S["kv_read"], 2 * (n - 1))
                    elif not first:
                        pe.wait_ge(S["scaled"], TPB * tb)
                    project(kp[c % 2], K_, 0, c, "k_sum")
                    project(vp[c % 2], V_, 1, c, "v_sum")
                for c in range(KC):
                    n = KC * tb + c
                    if not (first and c < 2):
                        pe.wait_ge(S["r_gate"], n - 1)
                    project(rp[c % 2], R_, 2, c, "r_sum")
                pe.wait_ge(S["w_lo_part"], KC * tb + KC)
                average(mp, "mean_sum")
                pe.wait_ge(S["sq_lo"], KC * tb + KC)
                average(qp, "var_sum")
                pe.wait_ge(S["g_lo"], KC * tb + KC)
                for tt in range(TPB):
                    for k in range(KC):
                        for n, (p_, q_) in enumerate(PASSES):
                            last = nc.tensor.matmul(sp_banks[tt][:], mix[0][p_][:, k, tt * P:(tt + 1) * P],
                                                    w[O_][q_][:, k, :],
                                                    start=(k == 0 and n == 0), stop=(k == KC - 1 and n == 2))
                    last.then_inc(S["s_sum"], 1)
            blocks(pe, body)



def top4_router(nc, A, keep):
    E, SH, TOP = 16, 2, 4
    G = E + SH

    def router(a, hb, yb):
        env = Stage()
        env.b1 = a.sb("b1", [P, 3, G])
        env.gates = a.sb("gates", [P, G, NT])
        env.b2 = a.sb("b2", [G, D])
        env.ident = a.sb("ident", [P, P])
        raw = a.sb("cen_raw", [P, KC, E])
        cen = [a.sb(f"cen{'hl'[s]}", [P, KC, E], F32R) for s in (HI, LO)]
        bias = a.sb("bias", [P, E])
        lower = a.sb("lower", [P, E, E])
        sc = a.sb("scores", [P, NT, E])
        rank = a.sb("rank", [P, NT, E])
        red = a.sb("red", [P, NT])
        gt = a.sb("greater", [P, 4, E * E])
        eq = a.sb("equal", [P, 4, E * E])
        ps = yb[0][:, 0:NT * E].rearrange("p (t e) -> p t e", e=E)
        s_in = a.sem("router_loaded")
        s_c = a.sem("router_chain")
        s_cen = a.sem("centroids_ready")
        s_lg = a.sem("logits_summed")
        s_sg = a.sem("sigmoid")
        env.s_in = s_in

        def sync(sp):
            for dst, src in ((env.b1, A["moe_b1"]), (env.b2, A["moe_b2"]), (env.ident, A["ident"]),
                             (raw, A["moe_cen"]), (bias, A["moe_bias"]), (lower, A["moe_lower"])):
                sp.dma_start(dst[:], src).then_inc(s_in, 16)

        def vector(dve):
            link = Chain(dve, s_c)
            dve.wait_ge(s_in, 16 * 6)
            link(nc.vector.tensor_copy(cen[HI][:], raw[:]))
            nc.vector.tensor_tensor(cen[LO][:], raw[:], f32(cen[HI][:]), ALU.subtract).then_inc(s_cen, 1)
            link(nc.vector.memset(env.gates[:, 0:SH, :], 1.0))
            dve.wait_ge(s_sg, 1)
            link(nc.vector.tensor_tensor(sc[:], sc[:], bias[:].unsqueeze(1).to_broadcast([P, NT, E]), ALU.add))
            for b in range(4):
                part = sc[:, 4 * b:4 * b + 4, :]
                g4, e4 = (m[:].rearrange("p t (i j) -> p t i j", j=E) for m in (gt, eq))
                other = part.unsqueeze(2).to_broadcast([P, 4, E, E])
                own = part.unsqueeze(3).to_broadcast([P, 4, E, E])
                link(nc.vector.tensor_tensor(g4, other, own, ALU.is_gt))
                link(nc.vector.tensor_tensor(e4, other, own, ALU.is_equal))
                link(nc.vector.tensor_tensor(eq[:], eq[:], lower[:].rearrange("p i j -> p (i j)").unsqueeze(1)
                                             .to_broadcast([P, 4, E * E]), ALU.mult))
                link(nc.vector.tensor_tensor(gt[:], gt[:], eq[:], ALU.add))
                link(nc.vector.tensor_reduce(rank[:, 4 * b:4 * b + 4, :], g4, AX.X, ALU.add))
            link(nc.vector.tensor_scalar(rank[:], rank[:], float(TOP), None, ALU.is_lt))
            link(nc.vector.tensor_tensor(sc[:], sc[:], rank[:], ALU.mult))
            link(nc.vector.tensor_reduce(red[:], sc[:], AX.X, ALU.add))
            link(nc.vector.tensor_scalar(red[:], red[:], 1e-8, None, ALU.max))
            link(nc.vector.reciprocal(red[:], red[:]))
            link(nc.vector.tensor_tensor(env.gates[:, SH:G, :].rearrange("p e t -> p t e"), sc[:],
                                         red[:].unsqueeze(2).to_broadcast([P, NT, E]), ALU.mult))

        def scalar(act):
            act.wait_ge(s_in, 16 * 6)
            act.wait_ge(s_lg, 1)
            nc.scalar.activation(sc[:], ps, ACT.Sigmoid).then_inc(s_sg, 1)

        def tensor(pe):
            pe.wait_ge(s_cen, 1)
            for t in range(NT):
                for c in range(KC):
                    for n, (p, q) in enumerate(PASSES):
                        last = nc.tensor.matmul(ps[:, t, :], keep.xn[p][:, c, t * P:(t + 1) * P], cen[q][:, c, :],
                                                start=(c == 0 and n == 0), stop=(c == KC - 1 and n == 2))
            last.then_inc(s_lg, 1)

        env.sync, env.vector, env.scalar, env.tensor = sync, vector, scalar, tensor
        env.tensor_before_y = lambda pe: pe.wait_ge(s_sg, 1)
        return env

    return router


def output_biases(nc, out_dram, keep):
    G = 18

    def finish(a, env, hb, yb, h, s_y, y_all):
        fin = silu_out(nc, out_dram, keep)(a, env, hb, yb, h, s_y, y_all)
        gT = [h[0][s][0:G, 0, :] for s in (HI, LO)]
        b2 = [h[1][s][0:G, 0, :] for s in (HI, LO)]
        s_b2h = a.sem("b2_hi_ready")
        s_b2 = a.sem("b2_ready")
        s_t = a.sem("gates_transposed")
        s_gh = a.sem("gT_hi_ready")
        s_gl = a.sem("gT_lo_ready")
        s_bs = a.sem("bias_summed")
        s_ba = a.sem("bias_added")
        s_done = a.sem("hidden_done")
        silu_vector, silu_scalar = fin.vector, fin.scalar

        def tensor(pe):
            pe.wait_ge(s_b2, 1)
            pe.wait_ge(s_done, 1)
            for b in range(TB):
                if b >= 1:
                    pe.wait_ge(s_gl, b)
                for tt in range(TPB):
                    last = nc.tensor.transpose(hb[0][0:G, tt * P:(tt + 1) * P], env.gates[:, :, b * TPB + tt], env.ident[:])
                last.then_inc(s_t, 1)
                pe.wait_ge(s_gl, b + 1)
                for tt in range(TPB):
                    if b:
                        pe.wait_ge(s_ba, (b - 1) * TPB + tt + 1)
                    for n, (p, q) in enumerate(PASSES):
                        last = nc.tensor.matmul(yb[tt][:], gT[p][:, tt * P:(tt + 1) * P], b2[q],
                                                start=(n == 0), stop=(n == 2))
                    last.then_inc(s_bs, 1)

        def scalar(act):
            act.wait_ge(s_y, y_all)
            nc.scalar.copy(b2[HI], env.b2[:]).then_inc(s_b2h, 1)
            for b in range(TB):
                act.wait_ge(s_t, b + 1)
                nc.scalar.copy(gT[HI], hb[0][0:G, :]).then_inc(s_gh, 1)
            silu_scalar(act)

        def vector(dve):
            dve.wait_ge(s_b2h, 1)
            nc.vector.tensor_tensor(b2[LO], env.b2[:], f32(b2[HI]), ALU.subtract).then_inc(s_b2, 1)
            nc.vector.drain().then_inc(s_done, 1)
            for b in range(TB):
                dve.wait_ge(s_gh, b + 1)
                nc.vector.tensor_tensor(gT[LO], hb[0][0:G, :], f32(gT[HI]), ALU.subtract).then_inc(s_gl, 1)
                for tt in range(TPB):
                    t = b * TPB + tt
                    dve.wait_ge(s_bs, t + 1)
                    nc.vector.tensor_tensor(keep.y[:, t, :], yb[tt][:], keep.y[:, t, :], ALU.add).then_inc(s_ba, 1)
            silu_vector(dve)

        fin.tensor, fin.scalar, fin.vector = tensor, scalar, vector
        return fin
    return finish


H, HKV, DH, DV = 16, 4, 64, 64
MBLK, NPOOL, WIN = 64, 28, 256
WQ, WK, WV, WOUT = 0, 1024, 1536, 1792
AW = 2816


def attention_stage(nc, A, x1_dram, g_dram, out_dram, keep):
    HALF = AW // 2
    with ExitStack() as ctx:
        a = Pools(nc, ctx, "att")
        xn = keep.xn
        raw = a.sb("raw", [P, HALF])
        w = [a.sb(f"w{'hl'[s]}", [P, AW], F32R) for s in (HI, LO)]
        s_acc = a.sb("s_acc", [P, NT, D])
        rope = [a.sb(f"rope{i}", [P, 2, BLK]) for i in range(2)]
        q32 = [a.sb(f"q32_{i}", [P, BLK]) for i in range(2)]
        qp = [[a.sb(f"q{i}{'hl'[s]}", [P, BLK], F32R) for s in (HI, LO)] for i in range(2)]
        t1 = [a.sb(f"t1_{i}", [P, BLK]) for i in range(2)]
        rot = [a.sb(f"rot{i}", [P, BLK]) for i in range(2)]
        qr = [a.sb(f"qr{'hl'[s]}", [P, 2, BLK], F32R) for s in (HI, LO)]
        sm = [a.sb(f"sm{i}", [P, TPB, 4, 32]) for i in range(2)]
        sw = a.sb("sw", [P, 2, 4, WIN])
        pT = [a.sb(f"pT{'hl'[s]}", [P, BLK], F32R) for s in (HI, LO)]
        pw = [a.sb(f"pw{'hl'[s]}", [P, 2, WIN], F32R) for s in (HI, LO)]
        oT = [a.sb(f"oT{'hl'[s]}", [P, 2, BLK], F32R) for s in (HI, LO)]
        kbd = [a.sb(f"kbd{'hl'[s]}", [P, 2, 32], F32R) for s in (HI, LO)]
        kwin = [a.sb(f"kwin{'hl'[s]}", [P, 2, WIN], F32R) for s in (HI, LO)]
        vbd = [a.sb(f"vbd{'hl'[s]}", [P, 2, 2, DV], F32R) for s in (HI, LO)]
        vwin = [a.sb(f"vwin{'hl'[s]}", [P, 2, 3, DV], F32R) for s in (HI, LO)]
        xbar = [a.sb(f"xbar{'hl'[s]}", [P, KC, 4, 32], F32R) for s in (HI, LO)]
        pool_s = [sm[0][:, :, i, :] for i in range(2)]
        kpool = a.sb("kpool", [P, 32])
        ident = a.sb("ident", [P, P])
        perm = a.sb("perm", [P, P], F32R)
        madd = a.sb("madd", [P, NT, 32])
        mmul = a.sb("mmul", [P, 4, 32])
        extra = a.sb("extra", [P, 32])
        wmask = a.sb("wmask", [P, 2, WIN])
        scale = a.sb("scale", [P, 2 * HKV])
        scale_now = a.sb("scale_now", [P, 2])
        mx = a.sb("mx", [P, TPB * 4])
        mw = a.sb("mw", [P, 8])
        bA = [a.ps(f"qsum{i}", [P, BLK]) for i in range(2)]
        bB = a.ps("swapped", [P, BLK])
        bS = a.ps("scores", [P, TPB, 2, 2, 32])
        bT = a.ps("pT", [P, BLK])
        bP = a.ps("pv", [P, BLK])
        bO = [a.ps(f"o{i}", [P, D]) for i in range(2)]
        N = dict(q_sum=12, q32=12, q_hi=12, q_lo=12, t1=12, swapped=12, t2=12, rotated=12, qr_hi=8, qr_lo=8,
                 k_pool=4, kp_mean=1, k_hi=4, k_lo=4, v_sum=3, v_hi=6, v_lo=6, scores=4, masked=4, max=4, shifted=4,
                 exps=4, prob=4, sums=4, inv=4, pT_sum=4, pT_hi=4, pT_lo=4, pv=8, o_hi=8, o_lo=8, s_sum=16, s_add=16,
                 win_s=4, win_m=4, win_max=1, win_mx=1, win_sh=2, win_e=2, win_sum=1, win_tot=1, win_p=2,
                 win_T=4, win_hi=4, win_lo=4, w_hi=2, w_lo=2, m_mul=1, m_fix=1, scale=1)
        S = {n: a.sem(n) for n in N}
        s_raw = a.sem("raw_loaded")
        s_rope = [a.sem(f"rope_loaded{i}") for i in range(2)]
        s_const = a.sem("const_loaded")
        s_zero = a.sem("zeroed")
        s_xb = a.sem("xbar_step")
        s_xbr = a.sem("xbar_ready")
        s_perm = a.sem("perm_ready")
        s_sc = a.sem("scale_step")
        s_tile = [a.sem(f"tiles_loaded{i}") for i in range(2)]
        s_st = [a.sem(f"stored{i}") for i in range(2)]
        s_fin = a.sem("final_step")
        s_res = a.sem("result")
        block = ctx.enter_context(nc.Block())

        def waiter(eng, g):
            def wait(name, n):
                v = N[name] * g + n
                if not (isinstance(v, int) and v <= 0):
                    eng.wait_ge(S[name], v)
            return wait

        def groups(eng, body):
            body(0)
            with eng.Fori(1, HKV) as g:
                body(g)

        def order(start, finish, values, scores, attend):
            start(0)
            start(1)
            finish(0)
            start(2)
            finish(1)
            start(3)
            finish(2)
            for t in range(6):
                if t < 4:
                    start(4 + 2 * t)
                if t < 5:
                    finish(3 + 2 * t)
                if t < 4:
                    start(5 + 2 * t)
                if t == 0:
                    values()
                if 1 <= t <= 4:
                    scores(t - 1)
                if t < 4:
                    finish(4 + 2 * t)
                if t >= 2:
                    attend(t - 2)

        def block_of(u):
            return u if u < 4 else (u - 4) // 2

        USES = [0, 1, 2, 3, 0, 1, 2, 3]

        def slot_of(u):
            return u if u < 4 else 4 + (u - 4) // 2

        @block.sync
        def _(sp):
            for dst, src in ((ident, A["ident"]), (madd, A["att_madd"]), (mmul, A["att_mmul"]),
                             (extra, A["att_extra"]), (wmask, A["att_wmask"]), (scale, A["att_scale"]),
                             (t1[0], A["att_perm"])):
                sp.dma_start(dst[:, 0:P] if dst is t1[0] else dst[:], src).then_inc(s_const, 16)

            def body(g):
                wait = waiter(sp, g)
                for half in range(2):
                    wait("w_lo", half)
                    src = A["att_w"][g, half, :, :] if isinstance(g, int) else \
                        A["att_w"][bass.ds(g, 1), half, :, :].rearrange("g p n -> p (g n)")
                    sp.dma_start(raw[:], src).then_inc(s_raw, 16)
                for i, b in enumerate(USES):
                    wait("rotated", {0: -2, 1: 0, 2: 1, 3: 2, 4: 3, 5: 4, 6: 6, 7: 8}[i])
                    sp.dma_start(rope[i % 2][:], A["att_rope"][b, :, :, :]).then_inc(s_rope[i % 2], 16)
            groups(sp, body)
            for t in range(NT):
                if t == 0:
                    sp.wait_ge(S["s_add"], N["s_add"] * HKV)
                if t >= 2:
                    sp.wait_ge(s_st[t % 2], 16 * (t // 2))
                sp.dma_start(sw[:, t % 2, 0:2, :], x1_dram[t * P:(t + 1) * P, :]
                             .rearrange("p (a n) -> p a n", a=2)).then_inc(s_tile[t % 2], 16)
                sp.dma_start(sw[:, t % 2, 2:4, :], g_dram[t * P:(t + 1) * P, :]
                             .rearrange("p (a n) -> p a n", a=2)).then_inc(s_tile[t % 2], 16)
                if t >= 1:
                    sp.wait_ge(s_res, t)
                    sp.dma_start(out_dram[(t - 1) * P:t * P, :], s_acc[:, t - 1, :]).then_inc(s_st[(t - 1) % 2], 16)
            sp.wait_ge(s_res, NT)
            sp.dma_start(out_dram[(NT - 1) * P:NT * P, :], s_acc[:, NT - 1, :]).then_inc(s_st[1], 16)
            for i in range(2):
                sp.wait_ge(s_st[i], 16 * NT // 2)

        @block.gpsimd
        def _(pool):
            for m in (*kbd, *kwin, *vbd, *vwin):
                nc.gpsimd.memset(f32(m[:]), 0.0).then_inc(s_zero, 1)

            def body(g):
                wait = waiter(pool, g)
                for half in range(2):
                    wait("w_hi", half + 1)
                    cols = slice(half * HALF, (half + 1) * HALF)
                    nc.gpsimd.tensor_tensor(w[LO][:, cols], raw[:], f32(w[HI][:, cols]), ALU.subtract)\
                      .then_inc(S["w_lo"], 1)

                def start(u):
                    j = u % 2
                    wait("q_hi", u + 1)
                    nc.gpsimd.tensor_tensor(qp[j][LO][:], q32[j][:], f32(qp[j][HI][:]), ALU.subtract).then_inc(S["q_lo"], 1)
                    i = slot_of(u)
                    pool.wait_ge(s_rope[i % 2], 16 * (4 * g + i // 2 + 1))
                    wait("rotated", u - 1)
                    nc.gpsimd.tensor_tensor(t1[j][:], q32[j][:], rope[i % 2][:, 0, :], ALU.mult).then_inc(S["t1"], 1)

                def finish(u):
                    if u >= 4:
                        n = u - 4
                        wait("qr_hi", n + 1)
                        nc.gpsimd.tensor_tensor(qr[LO][:, n % 2, :], rot[u % 2][:], f32(qr[HI][:, n % 2, :]),
                                                ALU.subtract).then_inc(S["qr_lo"], 1)

                def scores(tb):
                    if tb == 0:
                        wait("m_mul", 1)
                        nc.gpsimd.tensor_tensor(sm[0][:], sm[0][:], madd[:, 0:4, :].unsqueeze(2).to_broadcast([P, 4, 4, 32]),
                                                ALU.add).then_inc(S["masked"], 1)
                        wait("exps", 1)
                        nc.gpsimd.tensor_tensor(sm[0][:, 0, :, :], sm[0][:, 0, :, :],
                                                extra[:].unsqueeze(1).to_broadcast([P, 4, 32]), ALU.add)\
                          .then_inc(S["m_fix"], 1)

                def nothing(*_):
                    pass
                order(start, finish, nothing, scores, nothing)
            groups(pool, body)

        @block.scalar
        def _(act):
            act.wait_ge(s_const, 16 * 7)
            nc.scalar.activation(scale[:], scale[:], ACT.Exp).then_inc(s_sc, 1)
            act.wait_ge(s_sc, 1)
            nc.scalar.mul(scale[:], scale[:], float(32.0 ** -0.5)).then_inc(s_sc, 1)
            nc.scalar.copy(perm[:], t1[0][:, 0:P]).then_inc(s_perm, 1)
            act.wait_ge(s_sc, 2)
            act.wait_ge(s_zero, 8)

            def body(g):
                wait = waiter(act, g)
                nc.scalar.copy(scale_now[:], scale[:, 2 * g:2 * g + 2] if isinstance(g, int) else
                               scale[:, bass.ds(2 * g, 2)]).then_inc(S["scale"], 1)
                for half in range(2):
                    act.wait_ge(s_raw, 32 * g + 16 * half + 16)
                    wait("s_sum", 0)
                    nc.scalar.copy(w[HI][:, half * HALF:(half + 1) * HALF], raw[:]).then_inc(S["w_hi"], 1)

                def start(u):
                    j = u % 2
                    wait("q_sum", u + 1)
                    wait("t1", u - 1)
                    if u < 4:
                        nc.scalar.copy(q32[j][:], bA[j][:]).then_inc(S["q32"], 1)
                    else:
                        c = (u - 4) % 2
                        wait("scale", 1)
                        nc.scalar.activation(q32[j][:], bA[j][:], ACT.Copy, scale=scale_now[:, c:c + 1])\
                          .then_inc(S["q32"], 1)
                    wait("q32", u + 1)
                    wait("swapped", u - 1)
                    nc.scalar.copy(qp[j][HI][:], q32[j][:]).then_inc(S["q_hi"], 1)

                def finish(u):
                    wait("rotated", u + 1)
                    if u >= 4:
                        n = u - 4
                        wait("scores", n // 2)
                        if n < 2:
                            wait("win_s", 0)
                        nc.scalar.copy(qr[HI][:, n % 2, :], rot[u % 2][:]).then_inc(S["qr_hi"], 1)
                    elif u == 3:
                        for e in range(2):
                            rows = slice(64 * e, 64 * e + 64)
                            nc.scalar.copy(kwin[HI][rows, e, :], rot[1][rows, BLK - WIN:BLK]).then_inc(S["k_hi"], 1)
                        wait("kp_mean", 1)
                        for e in range(2):
                            rows = slice(64 * e, 64 * e + 64)
                            nc.scalar.copy(kbd[HI][rows, e, 0:NPOOL], kpool[rows, 0:NPOOL]).then_inc(S["k_hi"], 1)

                def values():
                    wait("v_sum", 1)
                    for h in range(4):
                        rows = slice(32 * h, 32 * h + 32)
                        nc.scalar.copy(vbd[HI][rows, h // 2, h % 2, :], bT[rows, 0:DV]).then_inc(S["v_hi"], 1)
                    for kt in range(2):
                        wait("v_sum", kt + 2)
                        nc.scalar.copy(vwin[HI][:, kt, 1, :], bO[kt][:, 0:DV]).then_inc(S["v_hi"], 1)

                def scores(tb):
                    wait("shifted", tb + 1)
                    nc.scalar.activation(sm[tb % 2][:], sm[tb % 2][:], ACT.Exp).then_inc(S["exps"], 1)
                    if tb == 3:
                        for i in range(2):
                            wait("win_sh", i + 1)
                            nc.scalar.activation(sw[:, i], sw[:, i], ACT.Exp).then_inc(S["win_e"], 1)

                def attend(tb):
                    wait("pT_sum", tb + 1)
                    nc.scalar.copy(pT[HI][:], bT[:]).then_inc(S["pT_hi"], 1)
                    for p in range(2):
                        if tb == 3:
                            for h in (2 * p, 2 * p + 1):
                                wait("win_T", h + 1)
                                nc.scalar.copy(pw[HI][:].rearrange("p a n -> p (a n)"), bA[h % 2][:])\
                                  .then_inc(S["win_hi"], 1)
                        wait("pv", 2 * tb + p + 1)
                        if p == 0:
                            wait("s_sum", 4 * tb)
                        nc.scalar.copy(oT[HI][:, p, :], bP[:]).then_inc(S["o_hi"], 1)
                order(start, finish, values, scores, attend)
            groups(act, body)

        @block.vector
        def _(dve):
            link = Chain(dve, s_xb)
            for s in (HI, LO):
                for c in range(KC):
                    nc.vector.tensor_reduce(pool_s[s][:, c, 0:NPOOL], f32(xn[s][:, c, 0:NPOOL * MBLK])
                                            .rearrange("p (b m) -> p b m", m=MBLK), AX.X, ALU.add)
                    link(nc.vector.tensor_reduce(pool_s[s][:, c, NPOOL:NPOOL + 1], f32(xn[s][:, c, T - WIN:T]),
                                                 AX.X, ALU.add))
            link(nc.vector.tensor_tensor(pool_s[0][:, :, 0:29], pool_s[0][:, :, 0:29], pool_s[1][:, :, 0:29], ALU.add))
            link(nc.vector.memset(pool_s[0][:, :, 29:32], 0.0))
            link(nc.vector.tensor_scalar_mul(pool_s[0][:, :, 0:NPOOL], pool_s[0][:, :, 0:NPOOL], 1.0 / MBLK))
            link(nc.vector.tensor_scalar_mul(pool_s[0][:, :, NPOOL:NPOOL + 1], pool_s[0][:, :, NPOOL:NPOOL + 1], 1.0 / WIN))
            for h in range(4):
                link(nc.vector.tensor_copy(xbar[HI][:, :, h, :], pool_s[0]))
            for h in range(4):
                nc.vector.tensor_tensor(xbar[LO][:, :, h, :], pool_s[0], f32(xbar[HI][:, :, h, :]), ALU.subtract)\
                  .then_inc(s_xbr, 1)
            link(nc.vector.memset(s_acc[:], 0.0))
            dve.wait_ge(s_xbr, 4)
            dve.wait_ge(s_zero, 8)
            dve.wait_ge(s_const, 16 * 7)

            def body(g):
                wait = waiter(dve, g)

                def start(u):
                    pass

                def finish(u):
                    j = u % 2
                    i = slot_of(u)
                    wait("swapped", u + 1)
                    dve.wait_ge(s_rope[i % 2], 16 * (4 * g + i // 2 + 1))
                    wait("qr_lo", u - 5)
                    nc.vector.tensor_tensor(rot[j][:], bB[:], rope[i % 2][:, 1, :], ALU.mult).then_inc(S["t2"], 1)
                    wait("t2", u + 1)
                    wait("t1", u + 1)
                    nc.vector.tensor_tensor(rot[j][:], rot[j][:], t1[j][:], ALU.add).then_inc(S["rotated"], 1)
                    if u < 4:
                        wait("rotated", u + 1)
                        nb = 8 if u < 3 else 4
                        nc.vector.tensor_reduce(kpool[:, 8 * u:8 * u + nb], rot[j][:, 0:nb * MBLK]
                                                .rearrange("p (b m) -> p b m", m=MBLK), AX.X, ALU.add)\
                          .then_inc(S["k_pool"], 1)
                    if u == 3:
                        wait("k_pool", 4)
                        nc.vector.tensor_scalar_mul(kpool[:, 0:NPOOL], kpool[:, 0:NPOOL], 1.0 / MBLK)\
                          .then_inc(S["kp_mean"], 1)
                        wait("kp_mean", 1)
                        for e in range(2):
                            rows = slice(64 * e, 64 * e + 64)
                            wait("k_hi", e + 1)
                            nc.vector.tensor_tensor(kwin[LO][rows, e, :], rot[1][rows, BLK - WIN:BLK],
                                                    f32(kwin[HI][rows, e, :]), ALU.subtract).then_inc(S["k_lo"], 1)
                        for e in range(2):
                            rows = slice(64 * e, 64 * e + 64)
                            wait("k_hi", e + 3)
                            nc.vector.tensor_tensor(kbd[LO][rows, e, 0:NPOOL], kpool[rows, 0:NPOOL],
                                                    f32(kbd[HI][rows, e, 0:NPOOL]), ALU.subtract).then_inc(S["k_lo"], 1)

                def values():
                    for h in range(4):
                        rows = slice(32 * h, 32 * h + 32)
                        wait("v_hi", h + 1)
                        nc.vector.tensor_tensor(vbd[LO][rows, h // 2, h % 2, :], bT[rows, 0:DV],
                                                f32(vbd[HI][rows, h // 2, h % 2, :]), ALU.subtract).then_inc(S["v_lo"], 1)
                    for kt in range(2):
                        wait("v_hi", kt + 5)
                        nc.vector.tensor_tensor(vwin[LO][:, kt, 1, :], bO[kt][:, 0:DV], f32(vwin[HI][:, kt, 1, :]),
                                                ALU.subtract).then_inc(S["v_lo"], 1)

                def scores(tb):
                    m = sm[tb % 2]
                    sc = bS[:].rearrange("p t c h k -> p t (c h) k")
                    wait("scores", tb + 1)
                    wait("pT_sum", tb - 1)
                    if tb == 0:
                        nc.vector.tensor_tensor(m[:], sc, mmul[:].unsqueeze(2).to_broadcast([P, 4, 4, 32]),
                                                ALU.mult).then_inc(S["m_mul"], 1)
                    else:
                        nc.vector.tensor_tensor(m[:], sc, madd[:, 4 * tb:4 * tb + 4, :].unsqueeze(2)
                                                .to_broadcast([P, 4, 4, 32]), ALU.add).then_inc(S["masked"], 1)
                    if tb == 3:
                        wait("win_T", 0)
                        for i in range(2):
                            for c in range(2):
                                n = 2 * i + c
                                wait("win_s", n + 1)
                                nc.vector.tensor_tensor(sw[:, i, 2 * c:2 * c + 2, :], bA[c][:]
                                                        .rearrange("p (h k) -> p h k", h=2),
                                                        wmask[:, i:i + 1, :].to_broadcast([P, 2, WIN]), ALU.add)\
                                  .then_inc(S["win_m"], 1)
                    wait("masked", tb + 1)
                    nc.vector.tensor_reduce(mx[:], m[:].rearrange("p t h k -> p (t h) k"), AX.X, ALU.max)\
                      .then_inc(S["max"], 1)
                    wait("max", tb + 1)
                    if tb == 3:
                        wait("win_m", 4)
                        nc.vector.tensor_reduce(mw[:], sw[:].rearrange("p t h k -> p (t h) k"), AX.X, ALU.max)\
                          .then_inc(S["win_max"], 1)
                        wait("win_max", 1)
                        nc.vector.tensor_tensor(mx[:, 8:16], mx[:, 8:16], mw[:], ALU.max).then_inc(S["win_mx"], 1)
                        wait("win_mx", 1)
                    nc.vector.tensor_tensor(m[:], m[:], mx[:].rearrange("p (t h) -> p t h", h=4).unsqueeze(3)
                                            .to_broadcast([P, 4, 4, 32]), ALU.subtract).then_inc(S["shifted"], 1)
                    if tb == 3:
                        for i in range(2):
                            nc.vector.tensor_tensor(sw[:, i], sw[:, i], mx[:, 8 + 4 * i:12 + 4 * i].unsqueeze(2)
                                                    .to_broadcast([P, 4, WIN]), ALU.subtract).then_inc(S["win_sh"], 1)
                    wait("exps", tb + 1)
                    if tb == 0:
                        wait("m_fix", 1)
                    if tb == 3:
                        wait("win_sh", 2)
                    nc.vector.tensor_reduce(mx[:], m[:].rearrange("p t h k -> p (t h) k"), AX.X, ALU.add)\
                      .then_inc(S["sums"], 1)
                    wait("sums", tb + 1)
                    if tb == 3:
                        wait("win_e", 2)
                        nc.vector.tensor_reduce(mw[:], sw[:].rearrange("p t h k -> p (t h) k"), AX.X, ALU.add)\
                          .then_inc(S["win_sum"], 1)
                        wait("win_sum", 1)
                        nc.vector.tensor_tensor(mx[:, 8:16], mx[:, 8:16], mw[:], ALU.add).then_inc(S["win_tot"], 1)
                        wait("win_tot", 1)
                    nc.vector.reciprocal(mx[:], mx[:]).then_inc(S["inv"], 1)
                    wait("inv", tb + 1)
                    wait("sums", tb + 1)
                    nc.vector.tensor_tensor(m[:], m[:], mx[:].rearrange("p (t h) -> p t h", h=4).unsqueeze(3)
                                            .to_broadcast([P, 4, 4, 32]), ALU.mult).then_inc(S["prob"], 1)
                    if tb == 3:
                        for i in range(2):
                            nc.vector.tensor_tensor(sw[:, i], sw[:, i], mx[:, 8 + 4 * i:12 + 4 * i].unsqueeze(2)
                                                    .to_broadcast([P, 4, WIN]), ALU.mult).then_inc(S["win_p"], 1)

                def attend(tb):
                    wait("pT_hi", tb + 1)
                    nc.vector.tensor_tensor(pT[LO][:], bT[:], f32(pT[HI][:]), ALU.subtract).then_inc(S["pT_lo"], 1)
                    for p in range(2):
                        if tb == 3:
                            for h in (2 * p, 2 * p + 1):
                                wait("win_hi", h + 1)
                                nc.vector.tensor_tensor(pw[LO][:].rearrange("p a n -> p (a n)"), bA[h % 2][:],
                                                        f32(pw[HI][:]).rearrange("p a n -> p (a n)"), ALU.subtract)\
                                  .then_inc(S["win_lo"], 1)
                        wait("o_hi", 2 * tb + p + 1)
                        nc.vector.tensor_tensor(oT[LO][:, p, :], bP[:], f32(oT[HI][:, p, :]), ALU.subtract)\
                          .then_inc(S["o_lo"], 1)
                    for tt in range(TPB):
                        wait("s_sum", 4 * tb + tt + 1)
                        t = 4 * tb + tt
                        nc.vector.tensor_tensor(s_acc[:, t, :], bO[tt % 2][:], s_acc[:, t, :], ALU.add)\
                          .then_inc(S["s_add"], 1)

                order(start, finish, values, scores, attend)
            groups(dve, body)
            fin = Chain(dve, s_fin)
            for t in range(NT):
                dve.wait_ge(s_tile[t % 2], 32 * (t // 2 + 1))
                fin(nc.vector.tensor_tensor(s_acc[:, t, :], s_acc[:, t, :], sw[:, t % 2, 2:4, :]
                                            .rearrange("p a n -> p (a n)"), ALU.mult))
                nc.vector.tensor_tensor(s_acc[:, t, :], s_acc[:, t, :], sw[:, t % 2, 0:2, :]
                                        .rearrange("p a n -> p (a n)"), ALU.add).then_inc(s_res, 1)

        @block.tensor
        def _(pe):
            pe.wait_ge(s_perm, 1)
            pe.wait_ge(s_xbr, 4)
            pe.wait_ge(s_zero, 8)

            def body(g):
                wait = waiter(pe, g)
                wait("w_lo", 2)

                def start(u):
                    j = u % 2
                    tb = block_of(u)
                    wait("q32", u - 1)
                    if u < 2:
                        wait("win_lo", 0)
                    cols = tb * BLK
                    for c in range(KC):
                        col = (WK + c * P) if u < 4 else (WQ + c * 256 + (u - 4) % 2 * P)
                        for n, (p, q) in enumerate(PASSES):
                            last = nc.tensor.matmul(bA[j][:], w[p][:, col:col + P], xn[q][:, c, cols:cols + BLK],
                                                    start=(c == 0 and n == 0), stop=(c == KC - 1 and n == 2))
                    last.then_inc(S["q_sum"], 1)

                def finish(u):
                    j = u % 2
                    wait("q_lo", u + 1)
                    wait("t2", u)
                    for s in (HI, LO):
                        last = nc.tensor.matmul(bB[:], perm[:], qp[j][s][:], start=(s == HI), stop=(s == LO))
                    last.then_inc(S["swapped"], 1)

                def values():
                    wait("pT_lo", 0)
                    for c in range(KC):
                        for n, (p, q) in enumerate(PASSES):
                            last = nc.tensor.matmul(bT[:, 0:DV], xbar[p][:, c].rearrange("p h k -> p (h k)"),
                                                    w[q][:, WV + c * DV:WV + (c + 1) * DV],
                                                    start=(c == 0 and n == 0), stop=(c == KC - 1 and n == 2))
                    last.then_inc(S["v_sum"], 1)
                    for kt in range(2):
                        wait("s_add", kt - 1)
                        k0 = T - WIN + kt * P
                        for c in range(KC):
                            for n, (p, q) in enumerate(PASSES):
                                last = nc.tensor.matmul(bO[kt][:, 0:DV], xn[p][:, c, k0:k0 + P],
                                                        w[q][:, WV + c * DV:WV + (c + 1) * DV],
                                                        start=(c == 0 and n == 0), stop=(c == KC - 1 and n == 2))
                        last.then_inc(S["v_sum"], 1)

                def scores(tb):
                    wait("k_lo", 4)
                    wait("qr_lo", 2 * tb + 2)
                    if tb == 1:
                        wait("m_mul", 1)
                    else:
                        wait("masked", tb)
                    for tt in range(TPB):
                        for c in range(2):
                            for n, (p, q) in enumerate(PASSES):
                                last = nc.tensor.matmul(bS[:, tt, c].rearrange("p h k -> p (h k)"),
                                                        qr[p][:, c, tt * P:(tt + 1) * P],
                                                        kbd[q][:].rearrange("p h k -> p (h k)"),
                                                        start=(n == 0), stop=(n == 2))
                    last.then_inc(S["scores"], 1)
                    if tb < 3:
                        return
                    wait("q32", 12)
                    for i in range(2):
                        for c in range(2):
                            if i:
                                wait("win_m", c + 1)
                            for n, (p, q) in enumerate(PASSES):
                                last = nc.tensor.matmul(bA[c][:], qr[p][:, c, (2 + i) * P:(3 + i) * P],
                                                        kwin[q][:].rearrange("p h k -> p (h k)"),
                                                        start=(n == 0), stop=(n == 2))
                            last.then_inc(S["win_s"], 1)

                def attend(tb):
                    wait("prob", tb + 1)
                    if tb == 0:
                        wait("v_lo", 6)
                    else:
                        wait("pT_lo", tb)
                    for tt in range(TPB):
                        last = nc.tensor.transpose(bT[:, tt * P:(tt + 1) * P],
                                                   sm[tb % 2][:, tt].rearrange("p h k -> p (h k)"), ident[:])
                    last.then_inc(S["pT_sum"], 1)
                    wait("pT_lo", tb + 1)
                    for p_ in range(2):
                        wait("o_lo", 2 * tb + p_)
                        for n, (p, q) in enumerate(PASSES):
                            last = nc.tensor.matmul(bP[:], vbd[p][:, p_].rearrange("p h d -> p (h d)"), pT[q][:],
                                                    start=(n == 0), stop=(n == 2 and tb < 3))
                        if tb == 3:
                            for h in (2 * p_, 2 * p_ + 1):
                                wait("win_p", 2)
                                wait("win_m", 4)
                                if h >= 2:
                                    wait("win_lo", h - 1)
                                for kt in range(2):
                                    for i in range(2):
                                        last = nc.tensor.transpose(bA[h % 2][:, kt * WIN + i * P:kt * WIN + (i + 1) * P],
                                                                   sw[:, i, h, kt * P:(kt + 1) * P], ident[:])
                                last.then_inc(S["win_T"], 1)
                                wait("win_lo", h + 1)
                                e = h % 2
                                for kt in range(2):
                                    for n, (p, q) in enumerate(PASSES):
                                        vv = vwin[p][:, kt, 1 - e:3 - e, :].rearrange("p a d -> p (a d)")
                                        last = nc.tensor.matmul(bP[:, WIN:BLK], vv, pw[q][:, kt, :], start=False,
                                                                stop=(e == 1 and kt == 1 and n == 2))
                        last.then_inc(S["pv"], 1)
                    wait("o_lo", 2 * tb + 2)
                    for tt in range(TPB):
                        wait("s_add", 4 * tb + tt - 1)
                        for c in range(2):
                            for n, (p, q) in enumerate(PASSES):
                                col = WOUT + c * D
                                last = nc.tensor.matmul(bO[tt % 2][:], oT[p][:, c, tt * P:(tt + 1) * P],
                                                        w[q][:, col:col + D], start=(c == 0 and n == 0),
                                                        stop=(c == 1 and n == 2))
                        last.then_inc(S["s_sum"], 1)
                order(start, finish, values, scores, attend)
            groups(pe, body)


class Keep:
    pass


def gate_of(env, g, tile, dynamic):
    return env.gates[:, bass.ds(g, 1), tile] if dynamic else env.gates[:, g, tile:tile + 1]


def program(nc, A, out):
    with ExitStack() as ctx:
        def scratch(name, shape=(T, D)):
            return nc.dram_tensor(name, shape, F32, kind="Internal").ap()
        g0, x1, g1, xT = scratch("g0"), scratch("x1"), scratch("g1"), scratch("xT", (P, KC, T))
        keep = Keep()

        def parts(c, tag):
            return [c.enter_context(nc.sbuf_tensor(f"{tag}{'hl'[s]}", [P, KC, T], F32R)) for s in (HI, LO)]

        with ExitStack() as c:
            keep.xn = parts(c, "xn0")
            keep.y = c.enter_context(nc.sbuf_tensor("y0", [P, NT, D], F32))
            layernorm_stage(nc, "ln0", A["x"], A["ident"], keep, xT)
            expert_stage(nc, "ffn", A["ffn_w"], 16, True, gate_of, top1_router(nc, A["ffn_gw"], 16, keep), keep,
                         silu_out(nc, g0, keep))
        time_mix_stage(nc, A["mix_w"], A["mix_vec"], xT, A["x"], g0, x1)
        with ExitStack() as c:
            keep.xn = parts(c, "xn1")
            with ExitStack() as c2:
                keep.y = c2.enter_context(nc.sbuf_tensor("y1", [P, NT, D], F32))
                layernorm_stage(nc, "ln1", x1, A["ident"], keep)
                expert_stage(nc, "moe", A["moe_w"], 18, False, gate_of, top4_router(nc, A, keep), keep,
                             output_biases(nc, g1, keep))
            attention_stage(nc, A, x1, g1, out, keep)


def kernel(**inp):
    import numpy as np
    import concourse.bacc as bacc
    from concourse.bass_utils import run_bass_kernel_spmd as run

    nc = bacc.Bacc("TRN2", target_bir_lowering=False, num_devices=1)
    arrays, A = {}, {}

    def give(name, a):
        a = np.ascontiguousarray(a)
        arrays["in_" + name] = a
        A[name] = nc.dram_tensor("in_" + name, a.shape, mybir.dt.from_np(a.dtype), kind="ExternalInput").ap()

    def chunks(wt, cols):
        k, m = wt.shape
        return wt.reshape(k // P, P, m // cols, cols).transpose(2, 1, 0, 3)

    inp = {n: np.asarray(v) for n, v in inp.items()}
    give("x", inp["L0_attn_x"].reshape(T, D))
    give("ident", np.eye(P, dtype=np.float32))
    give("ffn_gw", inp["L0_ffn_gate_w"].T.reshape(KC, P, 2).transpose(1, 0, 2))
    parts = []
    for e in range(2):
        g = chunks(inp["L0_ffn_w_gate"][e].T, 256).reshape(8, P, 1024)
        u = chunks(inp["L0_ffn_w_up"][e].T, 256).reshape(8, P, 1024)
        d = inp["L0_ffn_w_down"][e].T.reshape(8, 2, P, D).transpose(0, 2, 1, 3).reshape(8, P, 1024)
        parts.append(np.concatenate([g, u, d], axis=2))
    give("ffn_w", np.concatenate(parts))
    give("mix_w", np.stack([inp["L0_attn_" + n].T.reshape(KC, P, D).transpose(1, 0, 2)
                            for n in ("Wk", "Wv", "Wr", "Wo")]))
    give("mix_vec", np.stack([inp["L0_attn_" + n].reshape(KC, P).T for n in
                              ("tm_k", "tm_v", "tm_r", "time_decay", "time_first", "ln_g", "ln_b")], axis=1))
    FH = 384
    w1 = np.concatenate([inp["L1_ffn_shared_w1"], inp["L1_ffn_routed_w1"]])
    w2 = np.concatenate([inp["L1_ffn_shared_w2"], inp["L1_ffn_routed_w2"]])
    b1 = np.concatenate([inp["L1_ffn_shared_b1"], inp["L1_ffn_routed_b1"]])
    b2 = np.concatenate([inp["L1_ffn_shared_b2"], inp["L1_ffn_routed_b2"]])
    G, F = b1.shape
    w1 = np.pad(w1, ((0, 0), (0, 0), (0, FH - F))).reshape(G, KC, P, FH).transpose(0, 2, 1, 3).reshape(G, P, KC * FH)
    w2 = np.pad(w2, ((0, 0), (0, FH - F), (0, 0))).reshape(G, 3, P, D).transpose(0, 2, 1, 3).reshape(G, P, 3 * D)
    give("moe_w", np.concatenate([w1, w2], axis=2))
    give("moe_b1", np.pad(b1, ((0, 0), (0, FH - F))).reshape(G, 3, P).transpose(2, 1, 0))
    give("moe_b2", b2)
    give("moe_cen", inp["L1_ffn_centroids"].T.reshape(KC, P, 16).transpose(1, 0, 2))
    give("moe_bias", np.broadcast_to(inp["L1_ffn_bias"], (P, 16)))
    give("moe_lower", np.broadcast_to(np.tril(np.ones((16, 16), np.float32), -1), (P, 16, 16)))
    qs, qg = (inp["L1_attn_Wq_" + n].reshape(D, H, 32) for n in ("sem", "geo"))
    ks, kg = (inp["L1_attn_Wk_" + n].reshape(D, HKV, 32) for n in ("sem", "geo"))
    wq = np.concatenate([qs, qg], axis=2).reshape(KC, P, HKV, 256)
    wk = np.concatenate([ks, kg, ks, kg], axis=2).reshape(KC, P, HKV, P)
    wv = inp["L1_attn_Wv"].reshape(KC, P, HKV, DV)
    wo = inp["L1_attn_Wo"].reshape(HKV, 2, P, D)
    att = np.concatenate([m.transpose(2, 1, 0, 3).reshape(HKV, P, -1) for m in (wq, wk, wv)]
                         + [wo.transpose(0, 2, 1, 3).reshape(HKV, P, -1)], axis=2)
    give("att_w", att.reshape(HKV, P, 2, AW // 2).transpose(0, 2, 1, 3))
    give("att_scale", np.repeat(inp["L1_attn_logit_scale"].reshape(8, 2), 64, axis=1).T)
    f4 = np.float32
    inv = (f4(1.0) / f4(10000.0) ** (np.arange(0, 32, 2, dtype=f4) / f4(32))).astype(f4)
    ang = (np.arange(T, dtype=f4)[None, :] * inv[:, None]).astype(f4)
    cos, sin = np.cos(ang).astype(f4), np.sin(ang).astype(f4)
    one, zero = np.ones((32, T), f4), np.zeros((32, T), f4)
    C = np.concatenate([one, cos, cos] * 2)
    S = np.concatenate([zero, -sin, sin] * 2)
    give("att_rope", np.stack([C, S], axis=1).reshape(P, 2, TB, BLK).transpose(2, 0, 1, 3))
    perm = np.zeros((P, P), f4)
    for m in range(P):
        if m % 64 >= 32:
            perm[m // 64 * 64 + 32 + (m % 64 - 32 + 16) % 32, m] = 1.0
    give("att_perm", perm)
    tok = np.arange(T).reshape(NT, P).T[:, :, None]
    slot = np.arange(32)[None, None, :]
    seen = (slot < NPOOL) & (MBLK * slot + MBLK - 1 <= tok)
    give("att_madd", np.where(seen, 0.0, np.where(slot < NPOOL, -1e9, -2e9)).astype(f4))
    give("att_mmul", seen[:, 0:4, :].astype(f4))
    give("att_extra", ((slot[:, 0] == NPOOL) & (np.arange(P)[:, None] < MBLK - 1)).astype(f4) * f4(WIN))
    give("att_wmask", np.where(np.arange(T - WIN, T)[None, None, :] <= tok[:, 14:16], 0.0, -1e9).astype(f4))
    o = nc.dram_tensor("out", (T, D), F32, kind="ExternalOutput").ap()
    program(nc, A, o)
    r = run(nc, [arrays], core_ids=[0])
    return r.results[0]["out"].reshape(1, T, D)
```

```python
from contextlib import ExitStack

import concourse.bass as bass
from concourse import mybir

F32 = mybir.dt.float32
F32R = mybir.dt.float32r
ALU = mybir.AluOpType
ACT = mybir.ActivationFunctionType
AX = mybir.AxisListType

P = 128
D = 512
KC = D // P
T = 2048
NT = T // P
TB = 4
BLK = T // TB
TPB = BLK // P
WCOLS = 3072

HI, LO = 0, 1
PASSES = [(HI, HI), (HI, LO), (LO, HI)]


def f32(ap):
    return ap.bitcast(F32)


class Pools:

    def __init__(self, nc, ctx, tag):
        self.nc, self.ctx, self.tag, self.sems = nc, ctx, tag, []
        ctx.callback(self.give_back)

    def sb(self, name, shape, dt=F32):
        return self.ctx.enter_context(self.nc.sbuf_tensor(f"{self.tag}_{name}", shape, dt))

    def ps(self, name, shape, dt=F32):
        return self.ctx.enter_context(self.nc.psum_tensor(f"{self.tag}_ps_{name}", shape, dt))

    def sem(self, name):
        self.sems.append(self.nc.alloc_semaphore(f"{self.tag}_{name}"))
        return self.sems[-1]

    def give_back(self):
        self.nc.clear_and_free_semaphores(self.sems)
        self.nc.all_engine_barrier()


class Chain:

    def __init__(self, eng, sem, base=0):
        self.eng, self.sem, self.n = eng, sem, base

    def __call__(self, ins):
        self.n = self.n + 1
        ins.then_inc(self.sem, 1)
        self.eng.wait_ge(self.sem, self.n)


def layernorm_stage(nc, tag, x_dram, ident_dram, keep, xT_dram=None):
    with ExitStack() as ctx:
        a = Pools(nc, ctx, tag)
        ident = a.sb("ident", [P, P])
        stats = a.sb("stats", [P, NT, 6])
        mv = a.sb("mv", [P, NT, 2])
        rstd = a.sb("rstd", [P, NT])
        eps = a.sb("eps", [P, 1])
        whole = [a.sb(f"whole{i}", [P, KC, BLK]) for i in range(2)] if xT_dram is not None else None
        banks = [a.ps(f"xT{i}", [P, KC, P]) for i in range(8)]
        s_wh = a.sem("whole_ready")
        s_st2 = [a.sem(f"whole_stored{i}") for i in range(2)]
        s_x = [a.sem(f"x_loaded{t}") for t in range(4)]
        s_id = a.sem("ident_loaded")
        s_eps = a.sem("eps_set")
        s_st = a.sem("stats_step")
        s_var = a.sem("var_ready")
        s_std = a.sem("std_ready")
        s_rstd = a.sem("rstd_ready")
        s_xn = a.sem("xn_ready")
        s_tr = a.sem("transposed")
        s_hi = a.sem("hi_ready")
        s_lo = a.sem("lo_ready")
        block = ctx.enter_context(nc.Block())
        y, xn = keep.y, keep.xn

        @block.sync
        def _(sp):
            sp.dma_start(ident[:], ident_dram).then_inc(s_id, 16)
            for b in range(4):
                sp.dma_start(y[:, 4 * b:4 * b + 4, :], x_dram[512 * b:512 * b + 512, :]
                             .rearrange("(t p) d -> p t d", p=P)).then_inc(s_x[b], 16)
            if whole:
                for b in range(4):
                    sp.wait_ge(s_wh, 4 * b + 4)
                    sp.dma_start(xT_dram[:, :, b * BLK:(b + 1) * BLK], whole[b % 2][:]).then_inc(s_st2[b % 2], 16)
                for i in range(2):
                    sp.wait_ge(s_st2[i], 32)

        def low_parts(dve, b):
            for t in range(TPB * b, TPB * b + TPB):
                dve.wait_ge(s_hi, t + 1)
                cols = slice(t * P, (t + 1) * P)
                nc.vector.tensor_tensor(xn[LO][:, :, cols], banks[t % 8][:], f32(xn[HI][:, :, cols]),
                                        ALU.subtract).then_inc(s_lo, 1)

        @block.vector
        def _(dve):
            nc.vector.memset(eps[:], 1e-5).then_inc(s_eps, 1)
            for b in range(TB):
                dve.wait_ge(s_x[b], 16)
                for t in range(TPB * b, TPB * b + TPB):
                    nc.vector.bn_stats(stats[:, t, :], y[:, t, :]).then_inc(s_st, 1)
                for t in range(TPB * b, TPB * b + TPB):
                    dve.wait_ge(s_st, t + 1)
                    nc.vector.bn_aggr(mv[:, t, :], stats[:, t, :]).then_inc(s_var, 1)
                dve.wait_ge(s_std, b + 1)
                tiles = slice(TPB * b, TPB * b + TPB)
                nc.vector.reciprocal(rstd[:, tiles], rstd[:, tiles]).then_inc(s_rstd, 1)
                dve.wait_ge(s_rstd, b + 1)
                for t in range(TPB * b, TPB * b + TPB):
                    nc.vector.tensor_scalar(y[:, t, :], y[:, t, :], mv[:, t, 0:1], rstd[:, t:t + 1],
                                            ALU.subtract, ALU.mult).then_inc(s_xn, 1)
                if b:
                    low_parts(dve, b - 1)
            low_parts(dve, TB - 1)

        @block.scalar
        def _(act):
            def std(b):
                tiles = slice(TPB * b, TPB * b + TPB)
                act.wait_ge(s_var, TPB * b + TPB)
                nc.scalar.activation(rstd[:, tiles], mv[:, tiles, 1], ACT.Sqrt, bias=eps[:]).then_inc(s_std, 1)

            act.wait_ge(s_eps, 1)
            std(0)
            for b in range(TB):
                if b + 1 < TB:
                    std(b + 1)
                for t in range(TPB * b, TPB * b + TPB):
                    act.wait_ge(s_tr, t + 1)
                    if whole:
                        if b >= 2 and t % TPB == 0:
                            act.wait_ge(s_st2[b % 2], 16)
                        nc.scalar.copy(whole[b % 2][:, :, (t % TPB) * P:(t % TPB + 1) * P],
                                       banks[t % 8][:]).then_inc(s_wh, 1)
                    nc.scalar.copy(xn[HI][:, :, t * P:(t + 1) * P], banks[t % 8][:]).then_inc(s_hi, 1)

        @block.tensor
        def _(pe):
            pe.wait_ge(s_id, 16)
            for t in range(NT):
                pe.wait_ge(s_xn, t + 1)
                if t >= 8:
                    pe.wait_ge(s_lo, t - 7)
                for c in range(KC):
                    last = nc.tensor.transpose(banks[t % 8][:, c, :], y[:, t, c * P:(c + 1) * P], ident[:])
                last.then_inc(s_tr, 1)


def expert_stage(nc, tag, w_dram, groups, gated, gate_of, router, keep, finish):
    FC = 2 if gated else 3
    MATS = 2 if gated else 1
    NB = FC * MATS
    HID = FC * P
    DOWN = MATS * KC * HID
    steps = groups * TB
    with ExitStack() as ctx:
        a = Pools(nc, ctx, tag)
        raw = a.sb("raw", [P, WCOLS])
        w = [[a.sb(f"w{j}{'hl'[s]}", [P, WCOLS], F32R) for s in (HI, LO)] for j in range(2)]
        h = [[a.sb(f"h{j}{'hl'[s]}", [P, FC, BLK], F32R) for s in (HI, LO)] for j in range(2)]
        h32 = [a.sb(f"h32_{f}", [P, BLK]) for f in range(FC)]
        sil = [a.sb(f"silu{f}", [P, BLK]) for f in range(FC)] if gated else None
        hb = [a.ps(f"hid{b}", [P, BLK]) for b in range(NB)]
        yb = [a.ps(f"y{b}", [P, D]) for b in range(TPB)]
        s_raw = a.sem("raw_loaded")
        s_whi = a.sem("w_hi_ready")
        s_w = a.sem("w_ready")
        s_hid = a.sem("hidden_summed")
        s_sil = a.sem("silu_ready")
        s_h32 = a.sem("h32_ready")
        s_hhi = a.sem("h_hi_ready")
        s_h = a.sem("h_ready")
        s_y = a.sem("y_summed")
        s_yadd = a.sem("y_added")
        s_bias = a.sem("bias_ready")
        bias = None if gated else a.sb("bias_now", [P, 2, FC])
        env = router(a, yb, [*h32, *(sil or [])])
        fin = finish(a, s_yadd, (steps - TB) * TPB)
        block = ctx.enter_context(nc.Block())
        xn, y = keep.xn, keep.y

        def pairs(eng, body):
            body(0, True)
            with eng.Fori(1, groups // 2) as i:
                body(i, False)

        @block.sync
        def _(sp):
            env.sync(sp)

            def load(i, first):
                for j in range(2):
                    g = 2 * i + j
                    if not (first and j == 0):
                        sp.wait_ge(s_w, g)
                    sp.dma_start(raw[:], w_dram[g, :, :] if first else
                                 w_dram[bass.ds(g, 1), :, :].rearrange("g p n -> p (g n)")).then_inc(s_raw, 16)
            pairs(sp, load)
            fin.sync(sp)

        @block.gpsimd
        def _(pool):
            def weights_lo(g, j):
                pool.wait_ge(s_whi, g + 1)
                nc.gpsimd.tensor_tensor(w[j][LO][:], raw[:], f32(w[j][HI][:]), ALU.subtract).then_inc(s_w, 1)

            def hidden(i, first, last=False):
                for j in range(2):
                    for tb in range(TB):
                        k = (2 * i + j) * TB + tb
                        for f in range(FC):
                            pool.wait_ge(s_hhi, k * FC + f + 1)
                            nc.gpsimd.tensor_tensor(h[tb % 2][LO][:, f, :], h32[f][:], f32(h[tb % 2][HI][:, f, :]),
                                                    ALU.subtract).then_inc(s_h, 1)
                        if tb == 1 and j == 0:
                            weights_lo(2 * i + 1, 1)
                        if tb == 1 and j == 1 and not last:
                            weights_lo(2 * i + 2, 0)

            weights_lo(0, 0)
            hidden(0, True)
            with pool.Fori(1, groups // 2 - 1) as i:
                hidden(i, False)
            hidden(groups // 2 - 1, False, last=True)

        @block.scalar
        def _(act):
            def weights_hi(g, j, fresh):
                act.wait_ge(s_raw, 16 * g + 16)
                if not fresh:
                    act.wait_ge(s_y, TB * TPB * (g - 1))
                nc.scalar.copy(w[j][HI][:], raw[:]).then_inc(s_whi, 1)

            def hidden(i, first, last=False):
                for j in range(2):
                    g = 2 * i + j
                    if not gated:
                        src = env.b1[:, :, g] if first else env.b1[:, :, bass.ds(g, 1)].rearrange("p f g -> p (f g)")
                        nc.scalar.copy(bias[:, j, :], src).then_inc(s_bias, 1)
                    for tb in range(TB):
                        k = g * TB + tb
                        fresh = first and j == 0 and tb == 0
                        if gated:
                            for f in range(FC):
                                act.wait_ge(s_hid, k * NB + 2 * f + 1)
                                if not fresh:
                                    act.wait_ge(s_h32, (k - 1) * FC + f + 1)
                                nc.scalar.activation(sil[f][:], hb[2 * f][:], ACT.Silu).then_inc(s_sil, 1)
                        else:
                            for f in range(FC):
                                act.wait_ge(s_hid, k * NB + f + 1)
                                if not fresh:
                                    act.wait_ge(s_h, (k - 1) * FC + f + 1)
                                if tb == 0 and f == 0:
                                    act.wait_ge(s_bias, 2 * i + j + 1)
                                nc.scalar.activation(h32[f][:], hb[f][:], ACT.Relu, bias=bias[:, j, f:f + 1])\
                                  .then_inc(s_h32, 1)
                        for f in range(FC):
                            act.wait_ge(s_h32, k * FC + f + 1)
                            if f == 0 and not (first and j == 0 and tb < 2):
                                act.wait_ge(s_y, (k - 1) * TPB)
                            nc.scalar.copy(h[tb % 2][HI][:, f, :], h32[f][:]).then_inc(s_hhi, 1)
                        if tb == 1 and j == 0:
                            weights_hi(2 * i + 1, 1, first)
                        if tb == 1 and j == 1 and not last:
                            weights_hi(2 * i + 2, 0, False)
                        if tb >= 2 and j == 1 and last:
                            fin.scalar_block(act, tb - 2)

            weights_hi(0, 0, True)
            env.scalar(act)
            hidden(0, True)
            with act.Fori(1, groups // 2 - 1) as i:
                hidden(i, False)
            hidden(groups // 2 - 1, False, last=True)
            for b in (2, 3):
                fin.scalar_block(act, b)

        @block.vector
        def _(dve):
            env.vector(dve)

            def add_y(g, k, tb, dyn):
                for tt in range(TPB):
                    tile = tb * TPB + tt
                    dve.wait_ge(s_y, k * TPB + tt + 1)
                    gate = gate_of(env, g, tile, dyn)
                    nc.vector.scalar_tensor_tensor(y[:, tile, :], yb[tt][:], gate, y[:, tile, :],
                                                   ALU.mult, ALU.add).then_inc(s_yadd, 1)

            def work(i, first):
                for j in range(2):
                    for tb in range(TB):
                        g = 2 * i + j
                        k = g * TB + tb
                        if gated:
                            for f in range(FC):
                                dve.wait_ge(s_sil, k * FC + f + 1)
                                dve.wait_ge(s_hid, k * NB + 2 * f + 2)
                                if not (first and j == 0 and tb == 0):
                                    dve.wait_ge(s_h, (k - 1) * FC + f + 1)
                                nc.vector.tensor_tensor(h32[f][:], hb[2 * f + 1][:], sil[f][:],
                                                        ALU.mult).then_inc(s_h32, 1)
                        if first and j == 0 and tb == 0:
                            continue
                        add_y(g if tb else g - 1, k - 1, (tb - 1) % TB, not first)
            pairs(dve, work)
            add_y(groups - 1, steps - 1, TB - 1, False)

        @block.tensor
        def _(pe):
            env.tensor(pe)

            def hidden(j, tb, k, fresh):
                for f in range(FC):
                    for m in range(MATS):
                        b = f * MATS + m
                        if not fresh:
                            pe.wait_ge(s_h32, (k - 1) * FC + f + 1)
                        for c in range(KC):
                            col = (m * KC + c) * HID + f * P
                            for n, (p, q) in enumerate(PASSES):
                                last = nc.tensor.matmul(hb[b][:], w[j][p][:, col:col + P],
                                                        xn[q][:, c, tb * BLK:(tb + 1) * BLK],
                                                        start=(c == 0 and n == 0), stop=(c == KC - 1 and n == 2))
                        last.then_inc(s_hid, 1)

            def down(j, tb, k, fresh):
                pe.wait_ge(s_h, (k + 1) * FC)
                if fresh:
                    env.tensor_before_y(pe)
                for tt in range(TPB):
                    if not fresh:
                        pe.wait_ge(s_yadd, (k - 1) * TPB + tt + 1)
                    for f in range(FC):
                        for n, (p, q) in enumerate(PASSES):
                            last = nc.tensor.matmul(yb[tt][:], h[tb % 2][p][:, f, tt * P:(tt + 1) * P],
                                                    w[j][q][:, DOWN + f * D:DOWN + (f + 1) * D],
                                                    start=(f == 0 and n == 0), stop=(f == FC - 1 and n == 2))
                    last.then_inc(s_y, 1)

            def work(i, first):
                for j in range(2):
                    g = 2 * i + j
                    pe.wait_ge(s_w, g + 1)
                    for tb in range(TB):
                        k = g * TB + tb
                        fresh = first and j == 0
                        hidden(j, tb, k, fresh and tb == 0)
                        if fresh and tb == 0:
                            continue
                        down(j if tb else 1 - j, (tb - 1) % TB, k - 1, fresh and tb == 1)
            pairs(pe, work)
            down(1, TB - 1, steps - 1, False)


class Stage:

    def sync(self, eng): pass
    def scalar(self, eng): pass
    def vector(self, eng): pass
    def tensor(self, eng): pass
    def tensor_before_y(self, eng): pass


def logits_tensor(nc, pe, keep, wt, s_wt, yb, lgT, s_lgT, ident, E, ps, s_lg):
    pe.wait_ge(s_wt, 1)
    for b in range(TB):
        for c in range(KC):
            for n, (p, q) in enumerate(PASSES):
                last = nc.tensor.matmul(yb[b][0:E, :], wt[p][:, c, :], keep.xn[q][:, c, b * BLK:(b + 1) * BLK],
                                        start=(c == 0 and n == 0), stop=(c == KC - 1 and n == 2))
        last.then_inc(s_lg, 1)
    pe.wait_ge(s_lgT, TB)
    for t in range(NT):
        last = nc.tensor.transpose(ps[:, t, :], lgT[t // TPB][:, t % TPB * P:(t % TPB + 1) * P], ident[0:E, 0:E])
    last.then_inc(s_lg, 1)


def top1_router(nc, gw_dram, ident_dram, groups, keep):
    E = 2

    def router(a, yb, free):
        env = Stage()
        raw = a.sb("gw_raw", [P, KC, E])
        gw = [a.sb(f"gw{'hl'[s]}", [P, KC, E], F32R) for s in (HI, LO)]
        lg = a.sb("logits", [P, NT, E])
        red = a.sb("red", [P, NT])
        pr = a.sb("probs", [P, E, NT])
        sel = a.sb("sel", [P, E, NT])
        env.gates = a.sb("gates", [P, groups, NT])
        ps = yb[0][:, 0:NT * E].rearrange("p (t e) -> p t e", e=E)
        s_in = a.sem("gw_loaded")
        s_c = a.sem("gate_chain")
        s_gw = a.sem("gw_ready")
        s_lgT = a.sem("logit_rows_read")
        ident = a.sb("ident", [P, P])
        lgT = [m[0:E, :] for m in free]
        s_lg = a.sem("logits_summed")
        s_read = a.sem("logits_read")
        s_e = a.sem("gate_exp")
        s_d = a.sem("gate_shifted")

        def sync(sp):
            sp.dma_start(raw[:], gw_dram).then_inc(s_in, 16)
            sp.dma_start(ident[:], ident_dram).then_inc(s_in, 16)

        def vector(dve):
            link = Chain(dve, s_c)
            dve.wait_ge(s_in, 32)
            link(nc.vector.tensor_copy(gw[HI][:], raw[:]))
            nc.vector.tensor_tensor(gw[LO][:], raw[:], f32(gw[HI][:]), ALU.subtract).then_inc(s_gw, 1)
            link(nc.vector.memset(keep.y[:], 0.0))
            dve.wait_ge(s_lg, TB + 1)
            nc.vector.tensor_copy(lg[:], ps).then_inc(s_read, 1)
            dve.wait_ge(s_read, 1)
            link(nc.vector.tensor_reduce(red[:], lg[:], AX.X, ALU.max))
            nc.vector.tensor_tensor(lg[:], lg[:], red[:].unsqueeze(2).to_broadcast([P, NT, E]),
                                    ALU.subtract).then_inc(s_d, 1)
            dve.wait_ge(s_e, 1)
            link(nc.vector.tensor_reduce(red[:], lg[:], AX.X, ALU.add))
            link(nc.vector.reciprocal(red[:], red[:]))
            link(nc.vector.tensor_tensor(pr[:].rearrange("p e t -> p t e"), lg[:],
                                         red[:].unsqueeze(2).to_broadcast([P, NT, E]), ALU.mult))
            link(nc.vector.tensor_tensor(sel[:, 0, :], pr[:, 0, :], pr[:, 1, :], ALU.is_ge))
            link(nc.vector.tensor_scalar(sel[:, 1, :], sel[:, 0, :], -1.0, 1.0, ALU.mult, ALU.add))
            link(nc.vector.tensor_tensor(pr[:], pr[:], sel[:], ALU.mult))
            half = groups // E
            for e in range(E):
                link(nc.vector.tensor_copy(env.gates[:, e * half:(e + 1) * half, :],
                                           pr[:, e:e + 1, :].to_broadcast([P, half, NT])))

        def scalar(act):
            for b in range(TB):
                act.wait_ge(s_lg, b + 1)
                nc.scalar.copy(lgT[b], yb[b][0:E, :]).then_inc(s_lgT, 1)
            act.wait_ge(s_d, 1)
            nc.scalar.activation(lg[:], lg[:], ACT.Exp).then_inc(s_e, 1)

        def tensor(pe):
            logits_tensor(nc, pe, keep, gw, s_gw, yb, lgT, s_lgT, ident, E, ps, s_lg)

        env.sync, env.vector, env.scalar, env.tensor = sync, vector, scalar, tensor
        env.tensor_before_y = lambda pe: pe.wait_ge(s_read, 1)
        return env

    return router


def silu_out(nc, out_dram, keep):
    def finish(a, s_yadd, y_before):
        fin = Stage()
        s_g = a.sem("silu_y_ready")
        s_out = a.sem("silu_y_stored")

        def scalar_block(act, b):
            for t in range(TPB * b, TPB * b + TPB):
                act.wait_ge(s_yadd, y_before + t + 1)
                nc.scalar.activation(keep.y[:, t, :], keep.y[:, t, :], ACT.Silu).then_inc(s_g, 1)

        def sync(sp):
            for b in range(TB):
                sp.wait_ge(s_g, TPB * (b + 1))
                sp.dma_start(out_dram[BLK * b:BLK * (b + 1), :].rearrange("(t p) d -> p t d", p=P),
                             keep.y[:, TPB * b:TPB * (b + 1), :]).then_inc(s_out, 16)
            sp.wait_ge(s_out, 16 * TB)

        fin.scalar_block, fin.sync = scalar_block, sync
        return fin
    return finish


def time_mix_stage(nc, w_dram, vec_dram, xT_dram, x_dram, g_dram, x1_dram):
    TM_K, TM_V, TM_R, DECAY, FIRST, LN_G, LN_B = range(7)
    K_, V_, R_, O_ = range(4)
    PP, AA, BB = range(3)
    with ExitStack() as ctx:
        a = Pools(nc, ctx, "mix")
        x = a.sb("x", [P, KC, BLK + 1])
        d = a.sb("d", [P, KC, BLK])
        w = [a.sb(f"w{m}", [P, KC, D]) for m in range(4)]
        mix = [a.sb(f"mix{m}", [P, KC, BLK]) for m in range(3)]
        state = a.sb("state", [P, 3, KC, BLK + 1])
        r = a.sb("r", [P, KC, BLK])
        wkv = a.sb("wkv", [P, KC, BLK])
        ln = a.sb("ln", [P, KC, BLK])
        sq = a.sb("sq", [P, KC, BLK])
        E = [a.sb(f"e{i}", [P, 4, BLK]) for i in range(2)]
        ks = [a.sb(f"k{i}", [P, BLK]) for i in range(2)]
        vs = [a.sb(f"v{i}", [P, BLK]) for i in range(2)]
        q = [a.sb(f"q{i}", [P, BLK]) for i in range(2)]
        f2v = [a.sb(f"f2v{i}", [P, BLK]) for i in range(2)]
        rstd = a.sb("rstd", [P, BLK])
        g_in = [a.sb(f"g_in{i}", [P, D]) for i in range(2)]
        x_in = [a.sb(f"x_in{i}", [P, D]) for i in range(2)]
        vec = a.sb("vec", [P, 7, KC])
        negew = a.sb("negew", [P, KC])
        mean_w = a.sb("mean_w", [P, P])
        eps = a.sb("eps", [P, 1])
        kp = [a.ps(f"k{i}", [P, BLK]) for i in range(2)]
        vp = [a.ps(f"v{i}", [P, BLK]) for i in range(2)]
        ro = [a.ps(f"ro{i}", [P, BLK]) for i in range(2)]
        mp = a.ps("mean", [P, BLK])
        qp = a.ps("var", [P, BLK])
        N = dict(k_sum=4, v_sum=4, r_sum=4, kv_read=8, r_gate=4, diff=1, mix_kv=8, mix_r=4, carry=1,
                 pp_scan=4, q=4, e2_arg=4, shifts=12, exps=4, f2v=4, scans=8, num=12, den=12, wkv=4,
                 mean_sum=1, centred=4, square=4, var_sum=1, std=1, rstd=1, normed=4, affine=4, gated=4,
                 s_sum=4, scaled=4, x1=4)
        S = {n: a.sem(n) for n in N}
        s_const = a.sem("vectors_loaded")
        s_w = a.sem("weights_loaded")
        s_x = a.sem("x_loaded")
        s_zero = a.sem("zeroed")
        s_negew = a.sem("negew_step")
        tiles_in = [a.sem(f"tiles_loaded{i}") for i in range(2)]
        stored = [a.sem(f"x1_stored{i}") for i in range(2)]
        block = ctx.enter_context(nc.Block())

        def waiter(eng, tb):
            def wait(name, n):
                v = N[name] * tb + n
                if not (isinstance(v, int) and v <= 0):
                    eng.wait_ge(S[name], v)
            return wait

        def order(eng, load, diff, mix_kv, mix_r, kv, front, exps, back, mean, centre, variance, norm, output, gate):
            def steps(tb, before, after):
                now = waiter(eng, tb)
                prev = waiter(eng, tb - 1) if before else None
                kv(now, tb, 0)
                if before:
                    mean(prev)
                mix_r(now, tb)
                front(now, tb, 0)
                if before:
                    centre(prev)
                kv(now, tb, 1)
                exps(now, 0)
                if before:
                    variance(prev)
                front(now, tb, 1)
                back(now, 0)
                kv(now, tb, 2)
                exps(now, 1)
                if before:
                    norm(prev)
                front(now, tb, 2)
                back(now, 1)
                kv(now, tb, 3)
                exps(now, 2)
                front(now, tb, 3)
                if after:
                    load(tb + 1)
                    diff(waiter(eng, tb + 1), tb + 1)
                if before:
                    output(prev, tb - 1)
                exps(now, 3)
                back(now, 2)
                if after:
                    mix_kv(waiter(eng, tb + 1), tb + 1)
                gate(now, before)
                back(now, 3)
            load(0)
            diff(waiter(eng, 0), 0)
            mix_kv(waiter(eng, 0), 0)
            steps(0, False, True)
            with eng.Fori(1, TB - 1) as tb:
                steps(tb, True, True)
            steps(TB - 1, True, False)
            prev = waiter(eng, TB - 1)
            for step in (mean, centre, variance, norm):
                step(prev)
            output(prev, TB - 1)

        def nothing(*_):
            pass

        @block.sync
        def _(sp):
            sp.dma_start(vec[:], vec_dram).then_inc(s_const, 16)

            def load(tb):
                if isinstance(tb, int) and tb == 0:
                    sp.dma_start(x[:, :, 1:BLK + 1], xT_dram[:, :, 0:BLK]).then_inc(s_x, 16)
                    for m in range(4):
                        sp.dma_start(w[m][:], w_dram[m, :, :, :]).then_inc(s_w, 16)
                    return
                src = xT_dram[:, :, bass.ds(tb * BLK - 1, BLK + 1)] if not isinstance(tb, int) else \
                    xT_dram[:, :, tb * BLK - 1:(tb + 1) * BLK]
                waiter(sp, tb)("mix_r", 0)
                sp.dma_start(x[:], src).then_inc(s_x, 16)

            def output(wait, tb):
                def rows(t, tt):
                    row = (TPB * tb + tt) * P
                    return t[row:row + P, :] if isinstance(tb, int) else t[bass.ds(row, P), :]

                def fetch(tt):
                    if not (isinstance(tb, int) and tb == 0 and tt < 2):
                        sp.wait_ge(stored[tt % 2], 16 * (2 * tb + tt // 2))
                    sp.dma_start(g_in[tt % 2][:], rows(g_dram, tt)).then_inc(tiles_in[tt % 2], 16)
                    sp.dma_start(x_in[tt % 2][:], rows(x_dram, tt)).then_inc(tiles_in[tt % 2], 16)
                fetch(0)
                fetch(1)
                for tt in range(TPB):
                    wait("x1", tt + 1)
                    sp.dma_start(rows(x1_dram, tt), g_in[tt % 2][:]).then_inc(stored[tt % 2], 16)
                    if tt < 2:
                        fetch(tt + 2)
            order(sp, load, *[nothing] * 11, output, nothing)
            for i in range(2):
                sp.wait_ge(stored[i], 32 * TB)

        @block.gpsimd
        def _(pool):
            pool.wait_ge(s_zero, 5)

            def diff(wait, tb):
                pool.wait_ge(s_x, 16 * tb + 16)
                wait("mix_r", 0)
                nc.gpsimd.tensor_tensor(d[:], x[:, :, 1:BLK + 1], x[:, :, 0:BLK], ALU.subtract).then_inc(S["diff"], 1)

            def front(wait, tb, c):
                e = E[c % 2]
                pp = state[:, PP, c, :]
                wait("wkv", c - 1)
                wait("pp_scan", c + 1)
                nc.gpsimd.tensor_tensor(e[:, 0, :], pp[:, 0:BLK], pp[:, 1:BLK + 1], ALU.subtract)\
                  .then_inc(S["shifts"], 1)
                nc.gpsimd.tensor_tensor(e[:, 1, :], ks[c % 2][:], pp[:, 1:BLK + 1], ALU.subtract)\
                  .then_inc(S["shifts"], 1)
                wait("q", c + 1)
                nc.gpsimd.tensor_tensor(e[:, 2, :], pp[:, 0:BLK], q[c % 2][:], ALU.subtract).then_inc(S["shifts"], 1)

            def back(wait, c):
                e = E[c % 2]
                wait("exps", c + 1)
                wait("scans", 2 * c - 2)
                nc.gpsimd.tensor_tensor(f2v[c % 2][:], e[:, 1, :], vs[c % 2][:], ALU.mult).then_inc(S["f2v"], 1)
                wait("scans", 2 * c + 2)
                nc.gpsimd.tensor_tensor(e[:, 0, :], e[:, 2, :], state[:, AA, c, 0:BLK], ALU.mult).then_inc(S["num"], 1)
                nc.gpsimd.tensor_tensor(e[:, 1, :], e[:, 3, :], vs[c % 2][:], ALU.mult).then_inc(S["num"], 1)
                wait("num", 3 * c + 2)
                nc.gpsimd.tensor_tensor(e[:, 0, :], e[:, 0, :], e[:, 1, :], ALU.add).then_inc(S["num"], 1)

            def norm(wait):
                for c in range(KC):
                    wait("affine", c + 1)
                    nc.gpsimd.tensor_tensor(ln[:, c, :], ln[:, c, :], r[:, c, :], ALU.mult).then_inc(S["gated"], 1)
            order(pool, nothing, diff, nothing, nothing, nothing, front, nothing, back, nothing, nothing, nothing,
                  norm, nothing, nothing)

        @block.vector
        def _(dve):
            nc.vector.memset(mean_w[:], 1.0 / D).then_inc(s_zero, 1)
            nc.vector.memset(eps[:], 1e-5).then_inc(s_zero, 1)
            nc.vector.memset(state[:, PP, :, 0:1], -1e38).then_inc(s_zero, 1)
            nc.vector.memset(state[:, AA:BB + 1, :, 0:1], 0.0).then_inc(s_zero, 1)
            nc.vector.memset(x[:, :, 0:1], 0.0).then_inc(s_zero, 1)
            dve.wait_ge(s_zero, 5)
            dve.wait_ge(s_negew, 1)
            nc.vector.tensor_scalar_mul(negew[:], negew[:], -1.0).then_inc(s_negew, 1)
            dve.wait_ge(s_negew, 2)

            def blend(m, c, sem):
                nc.vector.scalar_tensor_tensor(mix[m][:, c, :], d[:, c, :], vec[:, TM_K + m, c:c + 1], x[:, c, 0:BLK],
                                               ALU.mult, ALU.add).then_inc(S[sem], 1)

            def mix_kv(wait, tb):
                wait("diff", 1)
                wait("v_sum", 0)
                for c in range(KC):
                    blend(K_, c, "mix_kv")
                    blend(V_, c, "mix_kv")

            def mix_r(wait, tb):
                wait("r_sum", 0)
                for c in range(KC):
                    blend(R_, c, "mix_r")
                if not (isinstance(tb, int) and tb == 0):
                    wait("num", 0)
                    wait("wkv", 0)
                    nc.vector.tensor_copy(state[:, :, :, 0:1], state[:, :, :, BLK:BLK + 1]).then_inc(S["carry"], 1)
                    wait("carry", 0)

            def front(wait, tb, c):
                k, qq = ks[c % 2], q[c % 2]
                pp = state[:, PP, c, :]
                wait("kv_read", 2 * c + 2)
                nc.vector.tensor_tensor_scan(pp[:, 1:BLK + 1], negew[:, c:c + 1].to_broadcast([P, BLK]), k[:],
                                             pp[:, 0:1], ALU.add, ALU.max).then_inc(S["pp_scan"], 1)
                wait("pp_scan", c + 1)
                wait("wkv", c - 1)
                wait("num", 3 * c - 3)
                nc.vector.scalar_tensor_tensor(qq[:], k[:], vec[:, FIRST, c:c + 1], pp[:, 0:BLK],
                                               ALU.add, ALU.max).then_inc(S["q"], 1)
                wait("q", c + 1)
                nc.vector.scalar_tensor_tensor(E[c % 2][:, 3, :], k[:], vec[:, FIRST, c:c + 1], qq[:],
                                               ALU.add, ALU.subtract).then_inc(S["e2_arg"], 1)

            def back(wait, c):
                e, qq = E[c % 2], q[c % 2]
                aa, bb = state[:, AA, c, :], state[:, BB, c, :]
                wait("exps", c + 1)
                nc.vector.tensor_tensor_scan(bb[:, 1:BLK + 1], e[:, 0, :], e[:, 1, :], bb[:, 0:1],
                                             ALU.mult, ALU.add).then_inc(S["scans"], 1)
                wait("f2v", c + 1)
                nc.vector.tensor_tensor_scan(aa[:, 1:BLK + 1], e[:, 0, :], f2v[c % 2][:], aa[:, 0:1],
                                             ALU.mult, ALU.add).then_inc(S["scans"], 1)
                wait("scans", 2 * c + 2)
                nc.vector.tensor_tensor(qq[:], e[:, 2, :], bb[:, 0:BLK], ALU.mult).then_inc(S["den"], 1)
                wait("den", 3 * c + 1)
                nc.vector.tensor_tensor(qq[:], qq[:], e[:, 3, :], ALU.add).then_inc(S["den"], 1)
                wait("den", 3 * c + 2)
                nc.vector.reciprocal(qq[:], qq[:]).then_inc(S["den"], 1)
                wait("den", 3 * c + 3)
                wait("num", 3 * c + 3)
                nc.vector.tensor_tensor(wkv[:, c, :], e[:, 0, :], qq[:], ALU.mult).then_inc(S["wkv"], 1)

            def centre(wait):
                wait("mean_sum", 1)
                for c in range(KC):
                    nc.vector.tensor_tensor(ln[:, c, :], wkv[:, c, :], mp[:], ALU.subtract).then_inc(S["centred"], 1)

            def norm(wait):
                wait("std", 1)
                nc.vector.reciprocal(rstd[:], rstd[:]).then_inc(S["rstd"], 1)
                wait("rstd", 1)
                for c in range(KC):
                    wait("square", c + 1)
                    nc.vector.tensor_tensor(ln[:, c, :], ln[:, c, :], rstd[:], ALU.mult).then_inc(S["normed"], 1)

            def output(wait, tb):
                for tt in range(TPB):
                    wait("s_sum", tt + 1)
                    dve.wait_ge(tiles_in[tt % 2], 32 * (2 * tb + tt // 2 + 1))
                    nc.vector.tensor_tensor(g_in[tt % 2][:], ro[tt % 2][:], g_in[tt % 2][:], ALU.mult)\
                      .then_inc(S["scaled"], 1)
                    wait("scaled", tt + 1)
                    nc.vector.tensor_tensor(g_in[tt % 2][:], g_in[tt % 2][:], x_in[tt % 2][:], ALU.add)\
                      .then_inc(S["x1"], 1)
            order(dve, nothing, nothing, mix_kv, mix_r, nothing, front, nothing, back, nothing, centre, nothing,
                  norm, output, nothing)

        @block.scalar
        def _(act):
            act.wait_ge(s_const, 16)
            nc.scalar.activation(negew[:], vec[:, DECAY, :], ACT.Exp).then_inc(s_negew, 1)
            act.wait_ge(s_zero, 5)

            def kv(wait, tb, c):
                wait("num", 3 * c - 3)
                wait("e2_arg", c - 1)
                wait("k_sum", c + 1)
                nc.scalar.copy(ks[c % 2][:], kp[c % 2][:]).then_inc(S["kv_read"], 1)
                wait("v_sum", c + 1)
                nc.scalar.copy(vs[c % 2][:], vp[c % 2][:]).then_inc(S["kv_read"], 1)

            def exps(wait, c):
                wait("shifts", 3 * c + 3)
                wait("e2_arg", c + 1)
                nc.scalar.activation(E[c % 2][:], E[c % 2][:], ACT.Exp).then_inc(S["exps"], 1)

            def centre(wait):
                for c in range(KC):
                    wait("centred", c + 1)
                    nc.scalar.activation(sq[:, c, :], ln[:, c, :], ACT.Square).then_inc(S["square"], 1)

            def norm(wait):
                wait("var_sum", 1)
                nc.scalar.activation(rstd[:], qp[:], ACT.Sqrt, bias=eps[:]).then_inc(S["std"], 1)
                for c in range(KC):
                    wait("normed", c + 1)
                    nc.scalar.activation(ln[:, c, :], ln[:, c, :], ACT.Identity, bias=vec[:, LN_B, c:c + 1],
                                         scale=vec[:, LN_G, c:c + 1]).then_inc(S["affine"], 1)

            def gate(wait, before):
                wait("gated", 0)
                for c in range(KC):
                    wait("r_sum", c + 1)
                    nc.scalar.activation(r[:, c, :], ro[c % 2][:], ACT.Sigmoid).then_inc(S["r_gate"], 1)
            order(act, nothing, nothing, nothing, nothing, kv, nothing, exps, nothing, nothing, centre, nothing,
                  norm, nothing, gate)

        @block.tensor
        def _(pe):
            pe.wait_ge(s_zero, 5)

            def project(bank, m, c, sem):
                for k in range(KC):
                    last = nc.tensor.matmul(bank[:], w[m][:, k, c * P:(c + 1) * P], mix[m][:, k, :],
                                            start=(k == 0), stop=(k == KC - 1))
                last.then_inc(S[sem], 1)

            def average(bank, src, sem):
                for k in range(KC):
                    last = nc.tensor.matmul(bank[:], mean_w[:], src[:, k, :], start=(k == 0), stop=(k == KC - 1))
                last.then_inc(S[sem], 1)

            def kv(wait, tb, c):
                if isinstance(tb, int) and tb == 0 and c == 0:
                    pe.wait_ge(s_w, 64)
                if c == 0:
                    wait("mix_kv", 8)
                wait("kv_read", 2 * c - 2)
                project(kp[c % 2], K_, c, "k_sum")
                project(vp[c % 2], V_, c, "v_sum")

            def mean(wait):
                wait("wkv", 4)
                average(mp, wkv, "mean_sum")

            def variance(wait):
                wait("square", 4)
                average(qp, sq, "var_sum")

            def output(wait, tb):
                wait("gated", 4)
                for tt in range(TPB):
                    if tt < 2:
                        wait("r_gate", 3 + tt)
                    else:
                        wait("scaled", tt - 1)
                    for k in range(KC):
                        last = nc.tensor.matmul(ro[tt % 2][:], ln[:, k, tt * P:(tt + 1) * P], w[O_][:, k, :],
                                                start=(k == 0), stop=(k == KC - 1))
                    last.then_inc(S["s_sum"], 1)

            def gate(wait, before):
                wait("mix_r", 4)
                for c in range(KC):
                    if c >= 2:
                        wait("r_gate", c - 1)
                    elif before:
                        wait("scaled", c - 1)
                    project(ro[c % 2], R_, c, "r_sum")
            order(pe, nothing, nothing, nothing, nothing, kv, nothing, nothing, nothing, mean, nothing, variance,
                  nothing, output, gate)


def top4_router(nc, A, keep):
    E, SH, TOP = 16, 2, 4
    G = E + SH

    def router(a, yb, free):
        env = Stage()
        env.b1 = a.sb("b1", [P, 3, G])
        env.gates = a.sb("gates", [P, G, NT])
        ident = a.sb("ident", [P, P])
        raw = a.sb("cen_raw", [P, KC, E])
        cen = [a.sb(f"cen{'hl'[s]}", [P, KC, E], F32R) for s in (HI, LO)]
        bias = a.sb("bias", [P, E])
        lower = a.sb("lower", [P, E, E])
        sc = a.sb("scores", [P, NT, E])
        rank = a.sb("rank", [P, NT, E])
        red = a.sb("red", [P, NT])
        gt = a.sb("greater", [P, 4, E * E])
        eq = a.sb("equal", [P, 4, E * E])
        ps = yb[0][:, 0:NT * E].rearrange("p (t e) -> p t e", e=E)
        s_in = a.sem("router_loaded")
        s_c = a.sem("router_chain")
        s_cen = a.sem("centroids_ready")
        s_lg = a.sem("logits_summed")
        s_lgT = a.sem("sigmoid_rows")
        s_read = a.sem("scores_read")
        lgT = [m[0:E, 2 * i:2 * i + 2, :].rearrange("p a n -> p (a n)") for m in (gt, eq) for i in range(2)]

        def sync(sp):
            for dst, src in ((env.b1, A["moe_b1"]), (ident, A["ident"]),
                             (raw, A["moe_cen"]), (bias, A["moe_bias"]), (lower, A["moe_lower"])):
                sp.dma_start(dst[:], src).then_inc(s_in, 16)

        def vector(dve):
            link = Chain(dve, s_c)
            dve.wait_ge(s_in, 16 * 5)
            link(nc.vector.tensor_copy(cen[HI][:], raw[:]))
            nc.vector.tensor_tensor(cen[LO][:], raw[:], f32(cen[HI][:]), ALU.subtract).then_inc(s_cen, 1)
            link(nc.vector.memset(env.gates[:, 0:SH, :], 1.0))
            dve.wait_ge(s_lg, TB + 1)
            nc.vector.tensor_tensor(sc[:], ps, bias[:].unsqueeze(1).to_broadcast([P, NT, E]), ALU.add)\
              .then_inc(s_read, 1)
            dve.wait_ge(s_read, 1)
            for b in range(4):
                part = sc[:, 4 * b:4 * b + 4, :]
                g4, e4 = (m[:].rearrange("p t (i j) -> p t i j", j=E) for m in (gt, eq))
                other = part.unsqueeze(2).to_broadcast([P, 4, E, E])
                own = part.unsqueeze(3).to_broadcast([P, 4, E, E])
                link(nc.vector.tensor_tensor(g4, other, own, ALU.is_gt))
                link(nc.vector.tensor_tensor(e4, other, own, ALU.is_equal))
                link(nc.vector.tensor_tensor(eq[:], eq[:], lower[:].rearrange("p i j -> p (i j)").unsqueeze(1)
                                             .to_broadcast([P, 4, E * E]), ALU.mult))
                link(nc.vector.tensor_tensor(gt[:], gt[:], eq[:], ALU.add))
                link(nc.vector.tensor_reduce(rank[:, 4 * b:4 * b + 4, :], g4, AX.X, ALU.add))
            link(nc.vector.tensor_scalar(rank[:], rank[:], float(TOP), None, ALU.is_lt))
            link(nc.vector.tensor_tensor(sc[:], sc[:], rank[:], ALU.mult))
            link(nc.vector.tensor_reduce(red[:], sc[:], AX.X, ALU.add))
            link(nc.vector.tensor_scalar(red[:], red[:], 1e-8, None, ALU.max))
            link(nc.vector.reciprocal(red[:], red[:]))
            link(nc.vector.tensor_tensor(env.gates[:, SH:G, :].rearrange("p e t -> p t e"), sc[:],
                                         red[:].unsqueeze(2).to_broadcast([P, NT, E]), ALU.mult))

        def scalar(act):
            act.wait_ge(s_in, 16 * 5)
            for b in range(TB):
                act.wait_ge(s_lg, b + 1)
                nc.scalar.activation(lgT[b], yb[b][0:E, :], ACT.Sigmoid).then_inc(s_lgT, 1)

        def tensor(pe):
            logits_tensor(nc, pe, keep, cen, s_cen, yb, lgT, s_lgT, ident, E, ps, s_lg)

        env.sync, env.vector, env.scalar, env.tensor = sync, vector, scalar, tensor
        env.tensor_before_y = lambda pe: pe.wait_ge(s_read, 1)
        return env

    return router


H, HKV, DH, DV = 16, 4, 64, 64
MBLK, NPOOL, WIN = 64, 28, 256
WQ, WK, WV, WOUT = 0, 1024, 1536, 1792
AW = 2816


def attention_stage(nc, A, x1_dram, g_dram, out_dram, keep):
    PARTS = [(WK, WOUT), (WQ, WK), (WOUT, AW)]
    with ExitStack() as ctx:
        a = Pools(nc, ctx, "att")
        xn = keep.xn
        raw_kv = a.sb("raw_kv", [P, WOUT - WK])
        raw_q = a.sb("raw_q", [P, WK - WQ])
        w = [a.sb(f"w{'hl'[s]}", [P, AW], F32R) for s in (HI, LO)]
        s_acc = a.sb("s_acc", [P, NT, D])
        rope = [a.sb(f"rope{i}", [P, 2, BLK]) for i in range(2)]
        q32 = [a.sb(f"q32_{i}", [P, BLK]) for i in range(2)]
        qp = [[a.sb(f"q{i}{'hl'[s]}", [P, BLK], F32R) for s in (HI, LO)] for i in range(2)]
        t1 = [a.sb(f"t1_{i}", [P, BLK]) for i in range(2)]
        rot = [a.sb(f"rot{i}", [P, BLK]) for i in range(2)]
        qr = [a.sb(f"qr{'hl'[s]}", [P, 2, BLK], F32R) for s in (HI, LO)]
        sm = [a.sb(f"sm{i}", [P, TPB, 4, 32]) for i in range(2)]
        sw = a.sb("sw", [P, 2, 4, WIN])
        pT = [a.sb(f"pT{'hl'[s]}", [P, BLK], F32R) for s in (HI, LO)]
        pw = [a.sb(f"pw{'hl'[s]}", [P, 2, WIN], F32R) for s in (HI, LO)]
        oT = [a.sb(f"oT{'hl'[s]}", [P, 2, BLK], F32R) for s in (HI, LO)]
        kbd = [a.sb(f"kbd{'hl'[s]}", [P, 2, 32], F32R) for s in (HI, LO)]
        kwin = [a.sb(f"kwin{'hl'[s]}", [P, 2, WIN], F32R) for s in (HI, LO)]
        vbd = [a.sb(f"vbd{'hl'[s]}", [P, 2, 2, DV], F32R) for s in (HI, LO)]
        vwin = [a.sb(f"vwin{'hl'[s]}", [P, 2, 3, DV], F32R) for s in (HI, LO)]
        xbar = [a.sb(f"xbar{'hl'[s]}", [P, KC, 4, 32], F32R) for s in (HI, LO)]
        pool_s = [sm[0][:, :, i, :] for i in range(2)]
        kpool = a.sb("kpool", [P, 32])
        ident = a.sb("ident", [P, P])
        perm = a.sb("perm", [P, P], F32R)
        madd = a.sb("madd", [P, NT, 32])
        mmul = a.sb("mmul", [P, 32])
        extra = a.sb("extra", [P, 32])
        wmask = a.sb("wmask", [P, 3 * P])
        scale = a.sb("scale", [P, 2 * HKV])
        scale_now = a.sb("scale_now", [P, 2])
        mx = a.sb("mx", [P, TPB * 4])
        mw = a.sb("mw", [P, 8])
        bA = [a.ps(f"qsum{i}", [P, BLK]) for i in range(2)]
        bB = a.ps("swapped", [P, BLK])
        bS = a.ps("scores", [P, TPB, 2, 2, 32])
        bT = a.ps("pT", [P, BLK])
        bP = a.ps("pv", [P, BLK])
        bO = [a.ps(f"o{i}", [P, D]) for i in range(2)]
        bW = [bS[:].rearrange("p t c h k -> p (t c h k)"), bT[:]]
        N = dict(q_sum=12, q32=12, q_hi=12, q_lo=12, t1=12, swapped=12, t2=12, rotated=12, qr_hi=8, qr_lo=8,
                 k_pool=4, kp_mean=1, k_hi=4, k_lo=4, v_sum=3, v_hi=6, v_lo=6, scores=4, masked=4, max=4, shifted=4,
                 exps=4, prob=4, sums=4, inv=4, pT_sum=4, pT_hi=4, pT_lo=4, pv=6, o_hi=8, o_lo=8, s_sum=16, s_add=16,
                 win_s=4, win_m=4, win_max=1, win_mx=1, win_sh=2, win_e=2, win_sum=1, win_tot=1, win_p=2,
                 win_T=4, win_hi=4, win_lo=4, w_hi=3, w_lo=3, m_mul=1, m_add=1, m_fix=1, scale=1, win_pv=4)
        S = {n: a.sem(n) for n in N}
        s_kv = a.sem("kv_weights_loaded")
        s_q = a.sem("q_out_weights_loaded")
        s_rope = [a.sem(f"rope_loaded{i}") for i in range(2)]
        s_const = a.sem("const_loaded")
        s_zero = a.sem("zeroed")
        s_xb = a.sem("xbar_step")
        s_xbr = a.sem("xbar_ready")
        s_perm = a.sem("perm_ready")
        s_sc = a.sem("scale_step")
        s_tile = [a.sem(f"tiles_loaded{i}") for i in range(2)]
        s_st = [a.sem(f"stored{i}") for i in range(2)]
        s_fin = a.sem("final_step")
        s_res = a.sem("result")
        block = ctx.enter_context(nc.Block())

        def as_pair(m):
            return m.rearrange("p (a h) k -> p a (h k)", a=2)
        pair_x = [rope[0][:], as_pair(sw[:, 0])]
        pair_g = [rope[1][:], as_pair(sw[:, 1])]

        def waiter(eng, g):
            def wait(name, n):
                v = N[name] * g + n
                if not (isinstance(v, int) and v <= 0):
                    eng.wait_ge(S[name], v)
            return wait

        def groups(eng, boundary, main):
            now = waiter(eng, 0)
            boundary(now, None, 0, None)
            main(now, 0)
            with eng.Fori(1, HKV) as g:
                now = waiter(eng, g)
                boundary(now, waiter(eng, g - 1), g, g - 1)
                main(now, g)
            boundary(None, waiter(eng, HKV - 1), None, HKV - 1)

        def order(eng, weights, start, finish, values, mask, exps, probs, turn, attend, turn_win, attend_win, output):
            def boundary(now, last, g, g_last):
                if now:
                    weights(now, g, 0)
                if last:
                    finish(last, g_last, 11)
                    turn(last, 2)
                if now:
                    start(now, g, 0)
                if last:
                    attend(last, 2, 0)
                    mask(last, 3, now is not None)
                    exps(last, 3)
                    attend(last, 2, 1)
                if now:
                    weights(now, g, 1)
                    finish(now, g, 0)
                if last:
                    output(last, 2, 0)
                    output(last, 2, 1)
                    probs(last, 3)
                    output(last, 2, 2)
                    output(last, 2, 3)
                if now:
                    start(now, g, 1)
                if last:
                    turn(last, 3)
                if now:
                    start(now, g, 2)
                    finish(now, g, 1)
                if last:
                    turn_win(last, 0)
                    turn_win(last, 1)
                    attend_win(last, 0)
                if now:
                    start(now, g, 3)
                if last:
                    attend_win(last, 1)
                    turn_win(last, 2)
                    turn_win(last, 3)
                if now:
                    finish(now, g, 2)
                if last:
                    attend_win(last, 2)
                    attend_win(last, 3)
                    for tt in range(TPB):
                        output(last, 3, tt)
                if now:
                    weights(now, g, 2)

            def main(now, g):
                for t in range(4):
                    finish(now, g, 3 + 2 * t)
                    if t >= 2:
                        turn(now, t - 2)
                    start(now, g, 4 + 2 * t)
                    if t == 0:
                        values(now)
                    if t >= 2:
                        attend(now, t - 2, 0)
                    start(now, g, 5 + 2 * t)
                    if t >= 2:
                        attend(now, t - 2, 1)
                    if t >= 1:
                        mask(now, t - 1)
                        exps(now, t - 1)
                    finish(now, g, 4 + 2 * t)
                    if t >= 2:
                        output(now, t - 2, 0)
                        output(now, t - 2, 1)
                    if t >= 1:
                        probs(now, t - 1)
                    if t >= 2:
                        output(now, t - 2, 2)
                        output(now, t - 2, 3)
            groups(eng, boundary, main)

        def nothing(*_):
            pass

        def block_of(u):
            return u if u < 4 else (u - 4) // 2

        USES = [0, 1, 2, 3, 0, 1, 2, 3]

        def slot_of(u):
            return u if u < 4 else 4 + (u - 4) // 2

        @block.sync
        def _(sp):
            for dst, src in ((ident, A["ident"]), (madd, A["att_madd"]), (mmul, A["att_mmul"]),
                             (extra, A["att_extra"]), (wmask, A["att_wmask"]), (scale, A["att_scale"]),
                             (t1[0], A["att_perm"])):
                sp.dma_start(dst[:, 0:P] if dst is t1[0] else dst[:], src).then_inc(s_const, 16)

            def load_weights(wait, g, part):
                part_dram = A[("att_kv", "att_q", "att_out")[part]]
                src = part_dram[g * P:(g + 1) * P, :] if isinstance(g, int) else part_dram[bass.ds(g * P, P), :]
                if part == 0:
                    wait("w_lo", -2)
                elif part == 1:
                    wait("w_lo", 0)
                else:
                    wait("w_lo", 2)
                if part == 0:
                    sp.dma_start(raw_kv[:], src).then_inc(s_kv, 16)
                else:
                    sp.dma_start(raw_q[:], src).then_inc(s_q, 16)

            def body(g):
                wait = waiter(sp, g)
                load_weights(wait, g, 0)
                load_weights(wait, g, 1)
                for i, b in enumerate(USES):
                    wait("rotated", {0: -2, 1: 0, 2: 1, 3: 2, 4: 3, 5: 4, 6: 6, 7: 8}[i])
                    sp.dma_start(rope[i % 2][:], A["att_rope"][b, :, :, :]).then_inc(s_rope[i % 2], 16)
                    if i == 2:
                        load_weights(wait, g, 2)

            body(0)
            with sp.Fori(1, HKV) as g:
                body(g)
            def rows(m, i):
                return m[2 * i * P:2 * (i + 1) * P, :].rearrange("(t p) d -> p t d", p=P)

            def fetch(i):
                sp.dma_start(pair_x[i % 2], rows(x1_dram, i)).then_inc(s_tile[i % 2], 16)
                sp.dma_start(pair_g[i % 2], rows(g_dram, i)).then_inc(s_tile[i % 2], 16)
            sp.wait_ge(S["rotated"], N["rotated"] * HKV)
            fetch(0)
            sp.wait_ge(S["win_T"], N["win_T"] * HKV)
            fetch(1)
            for i in range(NT // 2):
                sp.wait_ge(s_res, i + 1)
                if i + 2 < NT // 2:
                    fetch(i + 2)
                sp.dma_start(rows(out_dram, i), s_acc[:, 2 * i:2 * i + 2, :]).then_inc(s_st[i % 2], 16)
            for i in range(2):
                sp.wait_ge(s_st[i], 16 * NT // 4)

        @block.gpsimd
        def _(pool):
            for m in (*kbd, *kwin, *vbd, *vwin):
                nc.gpsimd.memset(f32(m[:]), 0.0).then_inc(s_zero, 1)

            def weights(wait, g, part):
                c0, c1 = PARTS[part]
                wait("w_hi", part + 1)
                nc.gpsimd.tensor_tensor(w[LO][:, c0:c1], (raw_kv if part == 0 else raw_q)[:], f32(w[HI][:, c0:c1]),
                                        ALU.subtract).then_inc(S["w_lo"], 1)

            def start(wait, g, u):
                j = u % 2
                wait("q_hi", u + 1)
                nc.gpsimd.tensor_tensor(qp[j][LO][:], q32[j][:], f32(qp[j][HI][:]), ALU.subtract).then_inc(S["q_lo"], 1)
                i = slot_of(u)
                pool.wait_ge(s_rope[i % 2], 16 * (4 * g + i // 2 + 1))
                wait("rotated", u - 1)
                nc.gpsimd.tensor_tensor(t1[j][:], q32[j][:], rope[i % 2][:, 0, :], ALU.mult).then_inc(S["t1"], 1)

            def finish(wait, g, u):
                if u >= 4:
                    n = u - 4
                    wait("qr_hi", n + 1)
                    nc.gpsimd.tensor_tensor(qr[LO][:, n % 2, :], rot[u % 2][:], f32(qr[HI][:, n % 2, :]),
                                            ALU.subtract).then_inc(S["qr_lo"], 1)

            def exps(wait, tb):
                if tb == 0:
                    wait("exps", 1)
                    nc.gpsimd.tensor_tensor(sm[0][:, 0, :, :], sm[0][:, 0, :, :],
                                            extra[:].unsqueeze(1).to_broadcast([P, 4, 32]), ALU.add)\
                      .then_inc(S["m_fix"], 1)
            order(pool, weights, start, finish, nothing, nothing, exps, nothing, nothing, nothing, nothing, nothing,
                  nothing)

        @block.scalar
        def _(act):
            act.wait_ge(s_const, 16 * 7)
            nc.scalar.activation(scale[:], scale[:], ACT.Exp).then_inc(s_sc, 1)
            act.wait_ge(s_sc, 1)
            nc.scalar.mul(scale[:], scale[:], float(32.0 ** -0.5)).then_inc(s_sc, 1)
            nc.scalar.copy(perm[:], t1[0][:, 0:P]).then_inc(s_perm, 1)
            act.wait_ge(s_sc, 2)
            act.wait_ge(s_zero, 8)

            def weights(wait, g, part):
                c0, c1 = PARTS[part]
                if part == 0:
                    wait("q32", 0)
                    nc.scalar.copy(scale_now[:], scale[:, 2 * g:2 * g + 2] if isinstance(g, int) else
                                   scale[:, bass.ds(2 * g, 2)]).then_inc(S["scale"], 1)
                    act.wait_ge(s_kv, 16 * g + 16)
                    wait("q_sum", 0)
                else:
                    act.wait_ge(s_q, 32 * g + 16 * part)
                    if part == 2:
                        wait("s_sum", 0)
                nc.scalar.copy(w[HI][:, c0:c1], (raw_kv if part == 0 else raw_q)[:]).then_inc(S["w_hi"], 1)

            def start(wait, g, u):
                j = u % 2
                wait("q_sum", u + 1)
                wait("t1", u - 1)
                if u < 4:
                    nc.scalar.copy(q32[j][:], bA[j][:]).then_inc(S["q32"], 1)
                else:
                    c = (u - 4) % 2
                    wait("scale", 1)
                    nc.scalar.activation(q32[j][:], bA[j][:], ACT.Copy, scale=scale_now[:, c:c + 1])\
                      .then_inc(S["q32"], 1)
                wait("q32", u + 1)
                wait("swapped", u - 1)
                nc.scalar.copy(qp[j][HI][:], q32[j][:]).then_inc(S["q_hi"], 1)

            def finish(wait, g, u):
                wait("rotated", u + 1)
                if u >= 4:
                    n = u - 4
                    wait("scores", n // 2)
                    if n < 2:
                        wait("win_s", 0)
                    nc.scalar.copy(qr[HI][:, n % 2, :], rot[u % 2][:]).then_inc(S["qr_hi"], 1)
                elif u == 3:
                    wait("win_s", 0)
                    for e in range(2):
                        rows = slice(64 * e, 64 * e + 64)
                        nc.scalar.copy(kwin[HI][rows, e, :], rot[1][rows, BLK - WIN:BLK]).then_inc(S["k_hi"], 1)
                    wait("kp_mean", 1)
                    for e in range(2):
                        rows = slice(64 * e, 64 * e + 64)
                        nc.scalar.copy(kbd[HI][rows, e, 0:NPOOL], kpool[rows, 0:NPOOL]).then_inc(S["k_hi"], 1)

            def values(wait):
                wait("v_sum", 1)
                for h in range(4):
                    rows = slice(32 * h, 32 * h + 32)
                    nc.scalar.copy(vbd[HI][rows, h // 2, h % 2, :], bT[rows, 0:DV]).then_inc(S["v_hi"], 1)
                for kt in range(2):
                    wait("v_sum", kt + 2)
                    nc.scalar.copy(vwin[HI][:, kt, 1, :], bO[kt][:, 0:DV]).then_inc(S["v_hi"], 1)

            def exps(wait, tb):
                wait("shifted", tb + 1)
                nc.scalar.activation(sm[tb % 2][:], sm[tb % 2][:], ACT.Exp).then_inc(S["exps"], 1)
                if tb == 3:
                    for i in range(2):
                        wait("win_sh", i + 1)
                        nc.scalar.activation(sw[:, i], sw[:, i], ACT.Exp).then_inc(S["win_e"], 1)

            def turn(wait, tb):
                wait("pT_sum", tb + 1)
                nc.scalar.copy(pT[HI][:], bT[:]).then_inc(S["pT_hi"], 1)

            def attend(wait, tb, p):
                if tb < 3:
                    wait("pv", 2 * tb + p + 1)
                else:
                    wait("win_pv", 2 * p + 2)
                if p == 0:
                    wait("s_sum", 4 * tb)
                nc.scalar.copy(oT[HI][:, p, :], bP[:]).then_inc(S["o_hi"], 1)

            def attend_win(wait, h):
                wait("win_T", h + 1)
                wait("win_pv", h)
                nc.scalar.copy(pw[HI][:].rearrange("p a n -> p (a n)"), bW[h % 2]).then_inc(S["win_hi"], 1)
                if h % 2:
                    attend(wait, 3, h // 2)
            order(act, weights, start, finish, values, nothing, exps, nothing, turn, attend, nothing, attend_win, nothing)

        @block.vector
        def _(dve):
            link = Chain(dve, s_xb)
            for s in (HI, LO):
                for c in range(KC):
                    nc.vector.tensor_reduce(pool_s[s][:, c, 0:NPOOL], f32(xn[s][:, c, 0:NPOOL * MBLK])
                                            .rearrange("p (b m) -> p b m", m=MBLK), AX.X, ALU.add)
                    link(nc.vector.tensor_reduce(pool_s[s][:, c, NPOOL:NPOOL + 1], f32(xn[s][:, c, T - WIN:T]),
                                                 AX.X, ALU.add))
            link(nc.vector.tensor_tensor(pool_s[0][:, :, 0:29], pool_s[0][:, :, 0:29], pool_s[1][:, :, 0:29], ALU.add))
            link(nc.vector.memset(pool_s[0][:, :, 29:32], 0.0))
            link(nc.vector.tensor_scalar_mul(pool_s[0][:, :, 0:NPOOL], pool_s[0][:, :, 0:NPOOL], 1.0 / MBLK))
            link(nc.vector.tensor_scalar_mul(pool_s[0][:, :, NPOOL:NPOOL + 1], pool_s[0][:, :, NPOOL:NPOOL + 1], 1.0 / WIN))
            for h in range(4):
                link(nc.vector.tensor_copy(xbar[HI][:, :, h, :], pool_s[0]))
            for h in range(4):
                nc.vector.tensor_tensor(xbar[LO][:, :, h, :], pool_s[0], f32(xbar[HI][:, :, h, :]), ALU.subtract)\
                  .then_inc(s_xbr, 1)
            link(nc.vector.memset(s_acc[:], 0.0))
            dve.wait_ge(s_xbr, 4)
            dve.wait_ge(s_zero, 8)
            dve.wait_ge(s_const, 16 * 7)

            def finish(wait, g, u):
                j = u % 2
                i = slot_of(u)
                wait("swapped", u + 1)
                dve.wait_ge(s_rope[i % 2], 16 * (4 * g + i // 2 + 1))
                if u < 2:
                    wait("qr_lo", u - 1)
                elif u < 6:
                    wait("k_pool", u - 1 if u < 5 else 4)
                    if u == 5:
                        wait("k_lo", 2)
                else:
                    wait("qr_lo", u - 5)
                nc.vector.tensor_tensor(rot[j][:], bB[:], rope[i % 2][:, 1, :], ALU.mult).then_inc(S["t2"], 1)
                wait("t2", u + 1)
                wait("t1", u + 1)
                nc.vector.tensor_tensor(rot[j][:], rot[j][:], t1[j][:], ALU.add).then_inc(S["rotated"], 1)
                if u < 4:
                    wait("rotated", u + 1)
                    nb = 8 if u < 3 else 4
                    nc.vector.tensor_reduce(kpool[:, 8 * u:8 * u + nb], rot[j][:, 0:nb * MBLK]
                                            .rearrange("p (b m) -> p b m", m=MBLK), AX.X, ALU.add)\
                      .then_inc(S["k_pool"], 1)
                if u == 3:
                    wait("k_pool", 4)
                    nc.vector.tensor_scalar_mul(kpool[:, 0:NPOOL], kpool[:, 0:NPOOL], 1.0 / MBLK)\
                      .then_inc(S["kp_mean"], 1)
                    wait("kp_mean", 1)
                    for e in range(2):
                        rows = slice(64 * e, 64 * e + 64)
                        wait("k_hi", e + 1)
                        nc.vector.tensor_tensor(kwin[LO][rows, e, :], rot[1][rows, BLK - WIN:BLK],
                                                f32(kwin[HI][rows, e, :]), ALU.subtract).then_inc(S["k_lo"], 1)
                    for e in range(2):
                        rows = slice(64 * e, 64 * e + 64)
                        wait("k_hi", e + 3)
                        nc.vector.tensor_tensor(kbd[LO][rows, e, 0:NPOOL], kpool[rows, 0:NPOOL],
                                                f32(kbd[HI][rows, e, 0:NPOOL]), ALU.subtract).then_inc(S["k_lo"], 1)

            def values(wait):
                for h in range(4):
                    rows = slice(32 * h, 32 * h + 32)
                    wait("v_hi", h + 1)
                    nc.vector.tensor_tensor(vbd[LO][rows, h // 2, h % 2, :], bT[rows, 0:DV],
                                            f32(vbd[HI][rows, h // 2, h % 2, :]), ALU.subtract).then_inc(S["v_lo"], 1)
                for kt in range(2):
                    wait("v_hi", kt + 5)
                    nc.vector.tensor_tensor(vwin[LO][:, kt, 1, :], bO[kt][:, 0:DV], f32(vwin[HI][:, kt, 1, :]),
                                            ALU.subtract).then_inc(S["v_lo"], 1)

            def mask(wait, tb, more=True):
                m = sm[tb % 2]
                sc = bS[:].rearrange("p t c h k -> p t (c h) k")
                wait("scores", tb + 1)
                wait("pT_sum", tb - 1)
                wait("prob", tb)
                first = 0
                if tb == 0:
                    wait("win_p", 0)
                    first = 1
                    nc.vector.tensor_tensor(m[:, 0], sc[:, 0], mmul[:].unsqueeze(1).to_broadcast([P, 4, 32]),
                                            ALU.mult).then_inc(S["m_mul"], 1)
                nc.vector.tensor_tensor(m[:, first:], sc[:, first:], madd[:, 4 * tb + first:4 * tb + 4, :].unsqueeze(2)
                                        .to_broadcast([P, 4 - first, 4, 32]), ALU.add).then_inc(S["masked"], 1)
                if tb == 0:
                    wait("m_mul", 1)
                    nc.vector.tensor_tensor(m[:, 0], m[:, 0], madd[:, 0, :].unsqueeze(1).to_broadcast([P, 4, 32]),
                                            ALU.add).then_inc(S["m_add"], 1)
                    wait("m_add", 1)
                if tb == 3:
                    wait("win_T", 0)
                    for i in range(2):
                        for c in range(2):
                            n = 2 * i + c
                            wait("win_s", n + 1)
                            nc.vector.tensor_tensor(sw[:, i, 2 * c:2 * c + 2, :], bA[c][:]
                                                    .rearrange("p (h k) -> p h k", h=2),
                                                    wmask[:, (1 - i) * P:(3 - i) * P].unsqueeze(1).to_broadcast([P, 2, WIN]), ALU.add)\
                              .then_inc(S["win_m"], 1)
                wait("masked", tb + 1)
                nc.vector.tensor_reduce(mx[:], m[:].rearrange("p t h k -> p (t h) k"), AX.X, ALU.max)\
                  .then_inc(S["max"], 1)
                wait("max", tb + 1)
                if tb == 3:
                    wait("win_m", 4)
                    nc.vector.tensor_reduce(mw[:], sw[:].rearrange("p t h k -> p (t h) k"), AX.X, ALU.max)\
                      .then_inc(S["win_max"], 1)
                    wait("win_max", 1)
                    nc.vector.tensor_tensor(mx[:, 8:16], mx[:, 8:16], mw[:], ALU.max).then_inc(S["win_mx"], 1)
                    wait("win_mx", 1)
                nc.vector.tensor_tensor(m[:], m[:], mx[:].rearrange("p (t h) -> p t h", h=4).unsqueeze(3)
                                        .to_broadcast([P, 4, 4, 32]), ALU.subtract).then_inc(S["shifted"], 1)
                if tb == 3:
                    for i in range(2):
                        nc.vector.tensor_tensor(sw[:, i], sw[:, i], mx[:, 8 + 4 * i:12 + 4 * i].unsqueeze(2)
                                                .to_broadcast([P, 4, WIN]), ALU.subtract).then_inc(S["win_sh"], 1)

            def probs(wait, tb):
                m = sm[tb % 2]
                wait("exps", tb + 1)
                if tb == 0:
                    wait("m_fix", 1)
                if tb == 3:
                    wait("win_sh", 2)
                nc.vector.tensor_reduce(mx[:], m[:].rearrange("p t h k -> p (t h) k"), AX.X, ALU.add)\
                  .then_inc(S["sums"], 1)
                wait("sums", tb + 1)
                if tb == 3:
                    wait("win_e", 2)
                    nc.vector.tensor_reduce(mw[:], sw[:].rearrange("p t h k -> p (t h) k"), AX.X, ALU.add)\
                      .then_inc(S["win_sum"], 1)
                    wait("win_sum", 1)
                    nc.vector.tensor_tensor(mx[:, 8:16], mx[:, 8:16], mw[:], ALU.add).then_inc(S["win_tot"], 1)
                    wait("win_tot", 1)
                nc.vector.reciprocal(mx[:], mx[:]).then_inc(S["inv"], 1)
                wait("inv", tb + 1)
                nc.vector.tensor_tensor(m[:], m[:], mx[:].rearrange("p (t h) -> p t h", h=4).unsqueeze(3)
                                        .to_broadcast([P, 4, 4, 32]), ALU.mult).then_inc(S["prob"], 1)
                if tb == 3:
                    for i in range(2):
                        nc.vector.tensor_tensor(sw[:, i], sw[:, i], mx[:, 8 + 4 * i:12 + 4 * i].unsqueeze(2)
                                                .to_broadcast([P, 4, WIN]), ALU.mult).then_inc(S["win_p"], 1)

            def turn(wait, tb):
                wait("pT_hi", tb + 1)
                nc.vector.tensor_tensor(pT[LO][:], bT[:], f32(pT[HI][:]), ALU.subtract).then_inc(S["pT_lo"], 1)

            def attend(wait, tb, p):
                wait("o_hi", 2 * tb + p + 1)
                nc.vector.tensor_tensor(oT[LO][:, p, :], bP[:], f32(oT[HI][:, p, :]), ALU.subtract)\
                  .then_inc(S["o_lo"], 1)

            def attend_win(wait, h):
                wait("win_hi", h + 1)
                nc.vector.tensor_tensor(pw[LO][:].rearrange("p a n -> p (a n)"), bW[h % 2],
                                        f32(pw[HI][:]).rearrange("p a n -> p (a n)"), ALU.subtract)\
                  .then_inc(S["win_lo"], 1)
                if h % 2:
                    attend(wait, 3, h // 2)

            def output(wait, tb, tt):
                t = 4 * tb + tt
                wait("s_sum", t + 1)
                nc.vector.tensor_tensor(s_acc[:, t, :], bO[tt % 2][:], s_acc[:, t, :], ALU.add)\
                  .then_inc(S["s_add"], 1)

            order(dve, nothing, nothing, finish, values, mask, nothing, probs, turn, attend, nothing, attend_win, output)
            fin = Chain(dve, s_fin)
            for i in range(NT // 2):
                dve.wait_ge(s_tile[i % 2], 32 * (i // 2 + 1))
                if i == 0:
                    dve.wait_ge(S["s_add"], N["s_add"] * HKV)
                pair = s_acc[:, 2 * i:2 * i + 2, :]
                fin(nc.vector.tensor_tensor(pair, pair, pair_g[i % 2], ALU.mult))
                nc.vector.tensor_tensor(pair, pair, pair_x[i % 2], ALU.add).then_inc(s_res, 1)

        @block.tensor
        def _(pe):
            pe.wait_ge(s_perm, 1)
            pe.wait_ge(s_xbr, 4)
            pe.wait_ge(s_zero, 8)

            def start(wait, g, u):
                j = u % 2
                tb = block_of(u)
                if u == 0:
                    wait("w_lo", 1)
                if u == 4:
                    wait("w_lo", 2)
                wait("q32", u - 1)
                if u in (1, 2):
                    wait("win_m", u - 2)
                cols = tb * BLK
                for c in range(KC):
                    col = (WK + c * P) if u < 4 else (WQ + c * 256 + (u - 4) % 2 * P)
                    for n, (p, q) in enumerate(PASSES):
                        last = nc.tensor.matmul(bA[j][:], w[p][:, col:col + P], xn[q][:, c, cols:cols + BLK],
                                                start=(c == 0 and n == 0), stop=(c == KC - 1 and n == 2))
                last.then_inc(S["q_sum"], 1)

            def finish(wait, g, u):
                j = u % 2
                wait("q_lo", u + 1)
                wait("t2", u)
                for s in (HI, LO):
                    last = nc.tensor.matmul(bB[:], perm[:], qp[j][s][:], start=(s == HI), stop=(s == LO))
                last.then_inc(S["swapped"], 1)

            def values(wait):
                wait("win_lo", 0)
                for c in range(KC):
                    for n, (p, q) in enumerate(PASSES):
                        last = nc.tensor.matmul(bT[:, 0:DV], xbar[p][:, c].rearrange("p h k -> p (h k)"),
                                                w[q][:, WV + c * DV:WV + (c + 1) * DV],
                                                start=(c == 0 and n == 0), stop=(c == KC - 1 and n == 2))
                last.then_inc(S["v_sum"], 1)
                for kt in range(2):
                    wait("s_add", kt - 1)
                    k0 = T - WIN + kt * P
                    for c in range(KC):
                        for n, (p, q) in enumerate(PASSES):
                            last = nc.tensor.matmul(bO[kt][:, 0:DV], xn[p][:, c, k0:k0 + P],
                                                    w[q][:, WV + c * DV:WV + (c + 1) * DV],
                                                    start=(c == 0 and n == 0), stop=(c == KC - 1 and n == 2))
                    last.then_inc(S["v_sum"], 1)

            def mask(wait, tb, more=True):
                wait("k_lo", 4)
                wait("qr_lo", 2 * tb + 2)
                wait("masked", tb)
                if tb == 0:
                    wait("win_lo", 0)
                if tb == 1:
                    wait("m_mul", 1)
                for tt in range(TPB):
                    for c in range(2):
                        for n, (p, q) in enumerate(PASSES):
                            last = nc.tensor.matmul(bS[:, tt, c].rearrange("p h k -> p (h k)"),
                                                    qr[p][:, c, tt * P:(tt + 1) * P],
                                                    kbd[q][:].rearrange("p h k -> p (h k)"),
                                                    start=(n == 0), stop=(n == 2))
                last.then_inc(S["scores"], 1)
                if tb < 3:
                    return
                for i in range(2):
                    for c in range(2):
                        if i:
                            wait("win_m", c + 1)
                        else:
                            wait("q32", 13 if c == 0 and more else 12)
                        for n, (p, q) in enumerate(PASSES):
                            last = nc.tensor.matmul(bA[c][:], qr[p][:, c, (2 + i) * P:(3 + i) * P],
                                                    kwin[q][:].rearrange("p h k -> p (h k)"),
                                                    start=(n == 0), stop=(n == 2))
                        last.then_inc(S["win_s"], 1)

            def turn(wait, tb):
                wait("prob", tb + 1)
                if tb == 0:
                    wait("v_lo", 6)
                else:
                    wait("pT_lo", tb)
                for tt in range(TPB):
                    last = nc.tensor.transpose(bT[:, tt * P:(tt + 1) * P],
                                               sm[tb % 2][:, tt].rearrange("p h k -> p (h k)"), ident[:])
                last.then_inc(S["pT_sum"], 1)

            def pooled(p_, last_pass):
                for n, (p, q) in enumerate(PASSES):
                    last = nc.tensor.matmul(bP[:], vbd[p][:, p_].rearrange("p h d -> p (h d)"), pT[q][:],
                                            start=(n == 0), stop=(n == 2 and last_pass))
                return last

            def attend(wait, tb, p_):
                wait("pT_lo", tb + 1)
                wait("o_lo", 2 * tb + p_)
                pooled(p_, True).then_inc(S["pv"], 1)

            def turn_win(wait, h):
                wait("win_p", 2)
                if h == 0:
                    wait("masked", 4)
                elif h == 1:
                    wait("pT_lo", 4)
                else:
                    wait("win_lo", h - 1)
                for kt in range(2):
                    for i in range(2):
                        o = kt * WIN + i * P
                        last = nc.tensor.transpose(bW[h % 2][:, o:o + P], sw[:, i, h, kt * P:(kt + 1) * P], ident[:])
                last.then_inc(S["win_T"], 1)

            def attend_win(wait, h):
                e = h % 2
                if e == 0:
                    wait("pT_lo", 4)
                    wait("o_lo", 6 + h // 2)
                    pooled(h // 2, False)
                wait("win_lo", h + 1)
                for kt in range(2):
                    for n, (p, q) in enumerate(PASSES):
                        vv = vwin[p][:, kt, 1 - e:3 - e, :].rearrange("p a d -> p (a d)")
                        last = nc.tensor.matmul(bP[:, WIN:BLK], vv, pw[q][:, kt, :], start=False,
                                                stop=(e == 1 and kt == 1 and n == 2))
                last.then_inc(S["win_pv"], 1)

            def output(wait, tb, tt):
                if tt == 0:
                    wait("o_lo", 2 * tb + 2)
                    wait("w_lo", 3)
                wait("s_add", 4 * tb + tt - 1)
                for c in range(2):
                    for n, (p, q) in enumerate(PASSES):
                        col = WOUT + c * D
                        last = nc.tensor.matmul(bO[tt % 2][:], oT[p][:, c, tt * P:(tt + 1) * P],
                                                w[q][:, col:col + D], start=(c == 0 and n == 0),
                                                stop=(c == 1 and n == 2))
                last.then_inc(S["s_sum"], 1)
            order(pe, nothing, start, finish, values, mask, nothing, nothing, turn, attend, turn_win, attend_win, output)


class Keep:
    pass


def gate_of(env, g, tile, dynamic):
    return env.gates[:, bass.ds(g, 1), tile] if dynamic else env.gates[:, g, tile:tile + 1]


def program(nc, A, out):
    with ExitStack() as ctx:
        def scratch(name, shape=(T, D)):
            return nc.dram_tensor(name, shape, F32, kind="Internal").ap()
        g0, x1, g1, xT = scratch("g0"), scratch("x1"), scratch("g1"), scratch("xT", (P, KC, T))
        keep = Keep()

        def parts(c, tag):
            return [c.enter_context(nc.sbuf_tensor(f"{tag}{'hl'[s]}", [P, KC, T], F32R)) for s in (HI, LO)]

        with ExitStack() as c:
            keep.xn = parts(c, "xn0")
            keep.y = c.enter_context(nc.sbuf_tensor("y0", [P, NT, D], F32))
            layernorm_stage(nc, "ln0", A["x"], A["ident"], keep, xT)
            expert_stage(nc, "ffn", A["ffn_w"], 16, True, gate_of, top1_router(nc, A["ffn_gw"], A["ident"], 16, keep), keep,
                         silu_out(nc, g0, keep))
        time_mix_stage(nc, A["mix_w"], A["mix_vec"], xT, A["x"], g0, x1)
        with ExitStack() as c:
            keep.xn = parts(c, "xn1")
            with ExitStack() as c2:
                keep.y = c2.enter_context(nc.sbuf_tensor("y1", [P, NT, D], F32))
                layernorm_stage(nc, "ln1", x1, A["ident"], keep)
                expert_stage(nc, "moe", A["moe_w"], 18, False, gate_of, top4_router(nc, A, keep), keep,
                             silu_out(nc, g1, keep))
            attention_stage(nc, A, x1, g1, out, keep)


def kernel(**inp):
    import numpy as np
    import concourse.bacc as bacc
    from concourse.bass_utils import run_bass_kernel_spmd as run

    nc = bacc.Bacc("TRN2", target_bir_lowering=False, num_devices=1)
    arrays, A = {}, {}

    def give(name, a):
        a = np.ascontiguousarray(a)
        arrays["in_" + name] = a
        A[name] = nc.dram_tensor("in_" + name, a.shape, mybir.dt.from_np(a.dtype), kind="ExternalInput").ap()

    def chunks(wt, cols):
        k, m = wt.shape
        return wt.reshape(k // P, P, m // cols, cols).transpose(2, 1, 0, 3)

    inp = {n: np.asarray(v) for n, v in inp.items()}
    give("x", inp["L0_attn_x"].reshape(T, D))
    give("ident", np.eye(P, dtype=np.float32))
    give("ffn_gw", inp["L0_ffn_gate_w"].T.reshape(KC, P, 2).transpose(1, 0, 2))
    parts = []
    for e in range(2):
        g = chunks(inp["L0_ffn_w_gate"][e].T, 256).reshape(8, P, 1024)
        u = chunks(inp["L0_ffn_w_up"][e].T, 256).reshape(8, P, 1024)
        d = inp["L0_ffn_w_down"][e].T.reshape(8, 2, P, D).transpose(0, 2, 1, 3).reshape(8, P, 1024)
        parts.append(np.concatenate([g, u, d], axis=2))
    give("ffn_w", np.concatenate(parts))
    give("mix_w", np.stack([inp["L0_attn_" + n].T.reshape(KC, P, D).transpose(1, 0, 2)
                            for n in ("Wk", "Wv", "Wr", "Wo")]))
    give("mix_vec", np.stack([inp["L0_attn_" + n].reshape(KC, P).T for n in
                              ("tm_k", "tm_v", "tm_r", "time_decay", "time_first", "ln_g", "ln_b")], axis=1))
    FH = 384
    w1 = np.concatenate([inp["L1_ffn_shared_w1"], inp["L1_ffn_routed_w1"]])
    w2 = np.concatenate([inp["L1_ffn_shared_w2"], inp["L1_ffn_routed_w2"]])
    b1 = np.concatenate([inp["L1_ffn_shared_b1"], inp["L1_ffn_routed_b1"]])
    b2 = np.concatenate([inp["L1_ffn_shared_b2"], inp["L1_ffn_routed_b2"]])
    G, F = b1.shape
    w1 = np.pad(w1, ((0, 0), (0, 0), (0, FH - F))).reshape(G, KC, P, FH).transpose(0, 2, 1, 3).reshape(G, P, KC * FH)
    w2 = np.concatenate([w2, b2[:, None, :], np.zeros((G, FH - F - 1, D), w2.dtype)], axis=1)
    b1 = np.concatenate([b1, np.ones((G, 1), b1.dtype), np.zeros((G, FH - F - 1), b1.dtype)], axis=1)
    w2 = w2.reshape(G, 3, P, D).transpose(0, 2, 1, 3).reshape(G, P, 3 * D)
    give("moe_w", np.concatenate([w1, w2], axis=2))
    give("moe_b1", b1.reshape(G, 3, P).transpose(2, 1, 0))
    give("moe_cen", inp["L1_ffn_centroids"].T.reshape(KC, P, 16).transpose(1, 0, 2))
    give("moe_bias", np.broadcast_to(inp["L1_ffn_bias"], (P, 16)))
    give("moe_lower", np.broadcast_to(np.tril(np.ones((16, 16), np.float32), -1), (P, 16, 16)))
    qs, qg = (inp["L1_attn_Wq_" + n].reshape(D, H, 32) for n in ("sem", "geo"))
    ks, kg = (inp["L1_attn_Wk_" + n].reshape(D, HKV, 32) for n in ("sem", "geo"))
    wq = np.concatenate([qs, qg], axis=2).reshape(KC, P, HKV, 256)
    wk = np.concatenate([ks, kg, ks, kg], axis=2).reshape(KC, P, HKV, P)
    wv = inp["L1_attn_Wv"].reshape(KC, P, HKV, DV)
    wo = inp["L1_attn_Wo"].reshape(HKV, 2, P, D)
    att = np.concatenate([m.transpose(2, 1, 0, 3).reshape(HKV, P, -1) for m in (wq, wk, wv)]
                         + [wo.transpose(0, 2, 1, 3).reshape(HKV, P, -1)], axis=2)
    for name, c0, c1 in (("kv", WK, WOUT), ("q", WQ, WK), ("out", WOUT, AW)):
        give("att_" + name, att[:, :, c0:c1].reshape(HKV * P, c1 - c0))
    give("att_scale", np.repeat(inp["L1_attn_logit_scale"].reshape(8, 2), 64, axis=1).T)
    f4 = np.float32
    inv = (f4(1.0) / f4(10000.0) ** (np.arange(0, 32, 2, dtype=f4) / f4(32))).astype(f4)
    ang = (np.arange(T, dtype=f4)[None, :] * inv[:, None]).astype(f4)
    cos, sin = np.cos(ang).astype(f4), np.sin(ang).astype(f4)
    one, zero = np.ones((32, T), f4), np.zeros((32, T), f4)
    C = np.concatenate([one, cos, cos] * 2)
    S = np.concatenate([zero, -sin, sin] * 2)
    give("att_rope", np.stack([C, S], axis=1).reshape(P, 2, TB, BLK).transpose(2, 0, 1, 3))
    perm = np.zeros((P, P), f4)
    for m in range(P):
        if m % 64 >= 32:
            perm[m // 64 * 64 + 32 + (m % 64 - 32 + 16) % 32, m] = 1.0
    give("att_perm", perm)
    tok = np.arange(T).reshape(NT, P).T[:, :, None]
    slot = np.arange(32)[None, None, :]
    seen = (slot < NPOOL) & (MBLK * slot + MBLK - 1 <= tok)
    give("att_madd", np.where(seen, 0.0, np.where(slot < NPOOL, -1e9, -2e9)).astype(f4))
    give("att_mmul", seen[:, 0, :].astype(f4))
    give("att_extra", ((slot[:, 0] == NPOOL) & (np.arange(P)[:, None] < MBLK - 1)).astype(f4) * f4(WIN))
    give("att_wmask", np.where(np.arange(-P, 2 * P)[None, :] <= np.arange(P)[:, None], 0.0, -1e9).astype(f4))
    o = nc.dram_tensor("out", (T, D), F32, kind="ExternalOutput").ap()
    program(nc, A, o)
    r = run(nc, [arrays], core_ids=[0])
    return r.results[0]["out"].reshape(1, T, D)
```

```python
from contextlib import ExitStack

import concourse.bass as bass
from concourse import mybir

F32 = mybir.dt.float32
F32R = mybir.dt.float32r
ALU = mybir.AluOpType
ACT = mybir.ActivationFunctionType
AX = mybir.AxisListType

P = 128
D = 512
KC = D // P
T = 2048
NT = T // P
TB = 4
BLK = T // TB
TPB = BLK // P
WCOLS = 3072

HI, LO = 0, 1
PASSES = [(HI, HI), (HI, LO), (LO, HI)]


def f32(ap):
    return ap.bitcast(F32)


class Pools:

    def __init__(self, nc, ctx, tag):
        self.nc, self.ctx, self.tag, self.sems = nc, ctx, tag, []
        ctx.callback(self.give_back)

    def sb(self, name, shape, dt=F32):
        return self.ctx.enter_context(self.nc.sbuf_tensor(f"{self.tag}_{name}", shape, dt))

    def ps(self, name, shape, dt=F32):
        return self.ctx.enter_context(self.nc.psum_tensor(f"{self.tag}_ps_{name}", shape, dt))

    def sem(self, name):
        self.sems.append(self.nc.alloc_semaphore(f"{self.tag}_{name}"))
        return self.sems[-1]

    def give_back(self):
        self.nc.clear_and_free_semaphores(self.sems)
        self.nc.all_engine_barrier()


class Chain:

    def __init__(self, eng, sem, base=0):
        self.eng, self.sem, self.n = eng, sem, base

    def __call__(self, ins):
        self.n = self.n + 1
        ins.then_inc(self.sem, 1)
        self.eng.wait_ge(self.sem, self.n)


def layernorm_stage(nc, tag, x_dram, ident_dram, keep, xT_dram=None):
    with ExitStack() as ctx:
        a = Pools(nc, ctx, tag)
        ident = a.sb("ident", [P, P])
        stats = a.sb("stats", [P, NT, 6])
        mv = a.sb("mv", [P, NT, 2])
        rstd = a.sb("rstd", [P, NT])
        eps = a.sb("eps", [P, 1])
        whole = [a.sb(f"whole{i}", [P, KC, BLK]) for i in range(2)] if xT_dram is not None else None
        banks = [a.ps(f"xT{i}", [P, KC, P]) for i in range(8)]
        s_wh = a.sem("whole_ready")
        s_st2 = [a.sem(f"whole_stored{i}") for i in range(2)]
        s_x = [a.sem(f"x_loaded{t}") for t in range(4)]
        s_id = a.sem("ident_loaded")
        s_eps = a.sem("eps_set")
        s_st = a.sem("stats_step")
        s_var = a.sem("var_ready")
        s_std = a.sem("std_ready")
        s_rstd = a.sem("rstd_ready")
        s_xn = a.sem("xn_ready")
        s_tr = a.sem("transposed")
        s_hi = a.sem("hi_ready")
        s_lo = a.sem("lo_ready")
        block = ctx.enter_context(nc.Block())
        y, xn = keep.y, keep.xn

        @block.sync
        def _(sp):
            sp.dma_start(ident[:], ident_dram).then_inc(s_id, 16)
            for b in range(4):
                sp.dma_start(y[:, 4 * b:4 * b + 4, :], x_dram[512 * b:512 * b + 512, :]
                             .rearrange("(t p) d -> p t d", p=P)).then_inc(s_x[b], 16)
            if whole:
                for b in range(4):
                    sp.wait_ge(s_wh, 4 * b + 4)
                    sp.dma_start(xT_dram[:, :, b * BLK:(b + 1) * BLK], whole[b % 2][:]).then_inc(s_st2[b % 2], 16)
                for i in range(2):
                    sp.wait_ge(s_st2[i], 32)

        def low_parts(dve, b):
            for t in range(TPB * b, TPB * b + TPB):
                dve.wait_ge(s_hi, t + 1)
                cols = slice(t * P, (t + 1) * P)
                nc.vector.tensor_tensor(xn[LO][:, :, cols], banks[t % 8][:], f32(xn[HI][:, :, cols]),
                                        ALU.subtract).then_inc(s_lo, 1)

        @block.vector
        def _(dve):
            nc.vector.memset(eps[:], 1e-5).then_inc(s_eps, 1)
            for b in range(TB):
                dve.wait_ge(s_x[b], 16)
                for t in range(TPB * b, TPB * b + TPB):
                    nc.vector.bn_stats(stats[:, t, :], y[:, t, :]).then_inc(s_st, 1)
                for t in range(TPB * b, TPB * b + TPB):
                    dve.wait_ge(s_st, t + 1)
                    nc.vector.bn_aggr(mv[:, t, :], stats[:, t, :]).then_inc(s_var, 1)
                dve.wait_ge(s_std, b + 1)
                tiles = slice(TPB * b, TPB * b + TPB)
                nc.vector.reciprocal(rstd[:, tiles], rstd[:, tiles]).then_inc(s_rstd, 1)
                dve.wait_ge(s_rstd, b + 1)
                for t in range(TPB * b, TPB * b + TPB):
                    nc.vector.tensor_scalar(y[:, t, :], y[:, t, :], mv[:, t, 0:1], rstd[:, t:t + 1],
                                            ALU.subtract, ALU.mult).then_inc(s_xn, 1)
                if b:
                    low_parts(dve, b - 1)
            low_parts(dve, TB - 1)

        @block.scalar
        def _(act):
            def std(b):
                tiles = slice(TPB * b, TPB * b + TPB)
                act.wait_ge(s_var, TPB * b + TPB)
                nc.scalar.activation(rstd[:, tiles], mv[:, tiles, 1], ACT.Sqrt, bias=eps[:]).then_inc(s_std, 1)

            act.wait_ge(s_eps, 1)
            std(0)
            for b in range(TB):
                if b + 1 < TB:
                    std(b + 1)
                for t in range(TPB * b, TPB * b + TPB):
                    act.wait_ge(s_tr, t + 1)
                    if whole:
                        if b >= 2 and t % TPB == 0:
                            act.wait_ge(s_st2[b % 2], 16)
                        nc.scalar.copy(whole[b % 2][:, :, (t % TPB) * P:(t % TPB + 1) * P],
                                       banks[t % 8][:]).then_inc(s_wh, 1)
                    nc.scalar.copy(xn[HI][:, :, t * P:(t + 1) * P], banks[t % 8][:]).then_inc(s_hi, 1)

        @block.tensor
        def _(pe):
            pe.wait_ge(s_id, 16)
            for t in range(NT):
                pe.wait_ge(s_xn, t + 1)
                if t >= 8:
                    pe.wait_ge(s_lo, t - 7)
                for c in range(KC):
                    last = nc.tensor.transpose(banks[t % 8][:, c, :], y[:, t, c * P:(c + 1) * P], ident[:])
                last.then_inc(s_tr, 1)


def shared_experts_stage(nc, A, router, keep):
    FC, G = 3, 2
    HID = FC * P
    DOWN = KC * HID
    with ExitStack() as ctx:
        a = Pools(nc, ctx, "shared")
        raw = a.sb("raw", [P, WCOLS])
        w = [[a.sb(f"w{j}{'hl'[s]}", [P, WCOLS], F32R) for s in (HI, LO)] for j in range(G)]
        h = [[a.sb(f"h{j}{'hl'[s]}", [P, FC, BLK], F32R) for s in (HI, LO)] for j in range(2)]
        h32 = [a.sb(f"h32_{f}", [P, BLK]) for f in range(FC)]
        b1 = a.sb("b1", [P, FC, G])
        hb = [a.ps(f"hid{b}", [P, BLK]) for b in range(FC)]
        yb = [a.ps(f"y{b}", [P, D]) for b in range(TPB)]
        s_raw = a.sem("raw_loaded")
        s_b1 = a.sem("b1_loaded")
        s_whi = a.sem("w_hi_ready")
        s_w = a.sem("w_ready")
        s_hid = a.sem("hidden_summed")
        s_h32 = a.sem("h32_ready")
        s_hhi = a.sem("h_hi_ready")
        s_h = a.sem("h_ready")
        s_y = a.sem("y_summed")
        s_yadd = a.sem("y_added")
        env = router(a, yb)
        block = ctx.enter_context(nc.Block())
        xn, y = keep.xn, keep.y

        @block.sync
        def _(sp):
            env.sync(sp)
            sp.dma_start(b1[:], A["moe_b1"]).then_inc(s_b1, 16)
            for g in range(G):
                if g:
                    sp.wait_ge(s_w, g)
                sp.dma_start(raw[:], A["moe_shared"][g, :, :]).then_inc(s_raw, 16)

        @block.gpsimd
        def _(pool):
            def weights_lo(g):
                pool.wait_ge(s_whi, g + 1)
                nc.gpsimd.tensor_tensor(w[g][LO][:], raw[:], f32(w[g][HI][:]), ALU.subtract).then_inc(s_w, 1)
            weights_lo(0)
            for k in range(G * TB):
                for f in range(FC):
                    pool.wait_ge(s_hhi, k * FC + f + 1)
                    nc.gpsimd.tensor_tensor(h[k % 2][LO][:, f, :], h32[f][:], f32(h[k % 2][HI][:, f, :]),
                                            ALU.subtract).then_inc(s_h, 1)
                if k == 0:
                    weights_lo(1)
                env.pool_step(pool, k)

        @block.scalar
        def _(act):
            def weights_hi(g):
                act.wait_ge(s_raw, 16 * g + 16)
                nc.scalar.copy(w[g][HI][:], raw[:]).then_inc(s_whi, 1)
            weights_hi(0)
            env.scalar(act)
            act.wait_ge(s_b1, 16)
            for k in range(G * TB):
                g = k // TB
                for f in range(FC):
                    act.wait_ge(s_hid, k * FC + f + 1)
                    if k:
                        act.wait_ge(s_h, (k - 1) * FC + f + 1)
                    nc.scalar.activation(h32[f][:], hb[f][:], ACT.Relu, bias=b1[:, f, g:g + 1]).then_inc(s_h32, 1)
                for f in range(FC):
                    act.wait_ge(s_h32, k * FC + f + 1)
                    if f == 0 and k >= 2:
                        act.wait_ge(s_y, (k - 1) * TPB)
                    nc.scalar.copy(h[k % 2][HI][:, f, :], h32[f][:]).then_inc(s_hhi, 1)
                if k == 0:
                    weights_hi(1)

        @block.vector
        def _(dve):
            env.vector(dve)
            for k in range(G * TB):
                for tt in range(TPB):
                    tile = k % TB * TPB + tt
                    dve.wait_ge(s_y, k * TPB + tt + 1)
                    nc.vector.tensor_tensor(y[:, tile, :], yb[tt][:], y[:, tile, :], ALU.add).then_inc(s_yadd, 1)

        @block.tensor
        def _(pe):
            env.tensor(pe)

            def hidden(k):
                g, tb = k // TB, k % TB
                pe.wait_ge(s_w, g + 1)
                for f in range(FC):
                    if k:
                        pe.wait_ge(s_h32, (k - 1) * FC + f + 1)
                    for c in range(KC):
                        col = c * HID + f * P
                        for n, (p, q) in enumerate(PASSES):
                            last = nc.tensor.matmul(hb[f][:], w[g][p][:, col:col + P],
                                                    xn[q][:, c, tb * BLK:(tb + 1) * BLK],
                                                    start=(c == 0 and n == 0), stop=(c == KC - 1 and n == 2))
                    last.then_inc(s_hid, 1)

            def down(k):
                g = k // TB
                pe.wait_ge(s_h, (k + 1) * FC)
                if k == 0:
                    env.tensor_before_y(pe)
                for tt in range(TPB):
                    if k:
                        pe.wait_ge(s_yadd, (k - 1) * TPB + tt + 1)
                    for f in range(FC):
                        for n, (p, q) in enumerate(PASSES):
                            last = nc.tensor.matmul(yb[tt][:], h[k % 2][p][:, f, tt * P:(tt + 1) * P],
                                                    w[g][q][:, DOWN + f * D:DOWN + (f + 1) * D],
                                                    start=(f == 0 and n == 0), stop=(f == FC - 1 and n == 2))
                    last.then_inc(s_y, 1)

            for k in range(G * TB):
                hidden(k)
                env.tensor_step(pe, k)
                if k:
                    down(k - 1)
            down(G * TB - 1)


class Stage:
    pass


def logits_tensor(nc, pe, keep, wt, s_wt, yb, lgT, s_lgT, ident, E, ps, s_lg):
    pe.wait_ge(s_wt, 1)
    for b in range(TB):
        for c in range(KC):
            for n, (p, q) in enumerate(PASSES):
                last = nc.tensor.matmul(yb[b][0:E, :], wt[p][:, c, :], keep.xn[q][:, c, b * BLK:(b + 1) * BLK],
                                        start=(c == 0 and n == 0), stop=(c == KC - 1 and n == 2))
        last.then_inc(s_lg, 1)
    pe.wait_ge(s_lgT, TB)
    for t in range(NT):
        last = nc.tensor.transpose(ps[:, t, :], lgT[t // TPB][:, t % TPB * P:(t % TPB + 1) * P], ident[0:E, 0:E])
    last.then_inc(s_lg, 1)


RT = NT + 1
RG = 16
RW = KC * 2 * P + D


def dispatch_stage(nc, A, keep, xs_dram):
    E = 2
    with ExitStack() as ctx:
        a = Pools(nc, ctx, "route")
        gw_raw = a.sb("gw_raw", [P, KC, E])
        gw = [a.sb(f"gw{'hl'[s]}", [P, KC, E], F32R) for s in (HI, LO)]
        ident = a.sb("ident", [P, P])
        consts = a.sb("consts", [P, P + NT + NT + RT])
        tri, index, start = consts[:, 0:P], consts[:, P:P + NT], consts[:, P + NT:P + 2 * NT]
        tile_no = consts[:, P + 2 * NT:]
        ones = a.sb("ones", [P, P])
        zero = a.sb("zero", [P, D])
        rows = [a.sb(f"logit_rows{b}", [E, BLK]) for b in range(TB)]
        lg = a.sb("logits", [P, NT, E])
        red = a.sb("red", [P, NT])
        pr = a.sb("probs", [P, NT, E])
        sel = a.sb("sel", [P, NT])
        count = a.sb("count", [P, NT])
        total = a.sb("total", [P, NT])
        tiles0 = a.sb("tiles0", [P, 1])
        other = a.sb("other", [P, NT])
        flags = a.sb("flags", [P, RT])
        banks = [a.ps(f"rows{b}", [P, BLK]) for b in range(TB)]
        lp = a.ps("logits", [P, NT, E])
        cp = a.ps("count", [P, NT])
        tp = a.ps("total", [P, NT])
        s_in = a.sem("loaded")
        s_zero = a.sem("zero_ready")
        s_fill = a.sem("rows_zeroed")
        s_gw = a.sem("gw_ready")
        s_lg = a.sem("logits_summed")
        s_rows = a.sem("logit_rows_read")
        s_c = a.sem("chain")
        s_sh = a.sem("shifted")
        s_exp = a.sem("exponentials")
        s_sel = a.sem("sel_ready")
        s_cnt = a.sem("counted")
        s_pos = a.sem("positions_ready")
        s_out = a.sem("rows_scattered")
        block = ctx.enter_context(nc.Block())
        y = keep.y

        @block.sync
        def _(sp):
            for dst, src in ((gw_raw, A["ffn_gw"]), (ident, A["ident"]), (consts, A["route_consts"])):
                sp.dma_start(dst[:], src).then_inc(s_in, 16)
            sp.wait_ge(s_zero, 1)
            for i in range(RT):
                sp.dma_start(xs_dram[i * P:(i + 1) * P, :], zero[:]).then_inc(s_fill, 16)
            sp.wait_ge(s_fill, 16 * RT)

        @block.gpsimd
        def _(pool):
            nc.gpsimd.memset(zero[:], 0.0).then_inc(s_zero, 1)
            pool.wait_ge(s_fill, 16 * RT)
            pool.wait_ge(s_pos, 1)
            for t in range(NT):
                nc.gpsimd.indirect_dma_start(
                    out=xs_dram, out_offset=bass.IndirectOffsetOnAxis(ap=keep.pos[:, t:t + 1], axis=0),
                    in_=y[:, t, :], in_offset=None).then_inc(s_out, 16)
            pool.wait_ge(s_out, 16 * NT)

        @block.vector
        def _(dve):
            link = Chain(dve, s_c)
            dve.wait_ge(s_in, 48)
            link(nc.vector.memset(ones[:], 1.0))
            link(nc.vector.tensor_copy(gw[HI][:], gw_raw[:]))
            nc.vector.tensor_tensor(gw[LO][:], gw_raw[:], f32(gw[HI][:]), ALU.subtract).then_inc(s_gw, 1)
            dve.wait_ge(s_lg, TB + 1)
            link(nc.vector.tensor_reduce(red[:], lp[:], AX.X, ALU.max))
            nc.vector.tensor_tensor(lg[:], lp[:], red[:].unsqueeze(2).to_broadcast([P, NT, E]),
                                    ALU.subtract).then_inc(s_sh, 1)
            dve.wait_ge(s_exp, 1)
            link(nc.vector.tensor_reduce(red[:], lg[:], AX.X, ALU.add))
            link(nc.vector.reciprocal(red[:], red[:]))
            link(nc.vector.tensor_tensor(pr[:], lg[:], red[:].unsqueeze(2).to_broadcast([P, NT, E]), ALU.mult))
            nc.vector.tensor_tensor(sel[:], pr[:, :, 0], pr[:, :, 1], ALU.is_ge).then_inc(s_sel, 1)
            link(nc.vector.tensor_reduce(keep.top[:], pr[:], AX.X, ALU.max))
            dve.wait_ge(s_cnt, 1)
            link(nc.vector.tensor_copy(count[:], tp[:]))
            link(nc.vector.tensor_tensor_scan(total[:], ones[:, 0:NT], count[:], 0.0, ALU.mult, ALU.add))
            link(nc.vector.tensor_tensor(other[:], total[:, NT - 1:NT].to_broadcast([P, NT]), start, ALU.is_gt))
            link(nc.vector.tensor_reduce(tiles0[:], other[:], AX.X, ALU.add))
            link(nc.vector.tensor_tensor(count[:], total[:], count[:], ALU.subtract))
            link(nc.vector.tensor_tensor(count[:], cp[:], count[:], ALU.add))
            link(nc.vector.tensor_tensor(other[:], index, count[:], ALU.subtract))
            link(nc.vector.tensor_scalar(total[:], tiles0[:].to_broadcast([P, NT]), float(P), None, ALU.mult))
            link(nc.vector.tensor_tensor(other[:], other[:], total[:], ALU.add))
            link(nc.vector.tensor_scalar(count[:], count[:], -1.0, None, ALU.add))
            link(nc.vector.tensor_tensor(count[:], count[:], other[:], ALU.subtract))
            link(nc.vector.tensor_tensor(count[:], count[:], sel[:], ALU.mult))
            link(nc.vector.tensor_tensor(count[:], count[:], other[:], ALU.add))
            link(nc.vector.tensor_tensor(flags[:], tile_no, tiles0[:].to_broadcast([P, RT]), ALU.is_ge))
            link(nc.vector.tensor_scalar(flags[:], flags[:], float(RW), None, ALU.mult))
            link(nc.vector.tensor_copy(keep.offset[:], flags[:]))
            nc.vector.tensor_copy(keep.pos[:], count[:]).then_inc(s_pos, 1)

        @block.scalar
        def _(act):
            for b in range(TB):
                act.wait_ge(s_lg, b + 1)
                nc.scalar.copy(rows[b][:], banks[b][0:E, :]).then_inc(s_rows, 1)
            act.wait_ge(s_sh, 1)
            nc.scalar.activation(lg[:], lg[:], ACT.Exp).then_inc(s_exp, 1)

        @block.tensor
        def _(pe):
            logits_tensor(nc, pe, keep, gw, s_gw, banks, [m[:] for m in rows], s_rows, ident, E, lp, s_lg)
            pe.wait_ge(s_sel, 1)
            nc.tensor.matmul(cp[:], tri, sel[:], start=True, stop=True)
            nc.tensor.matmul(tp[:], ones[:], sel[:], start=True, stop=True).then_inc(s_cnt, 1)


def routed_ffn_stage(nc, w_dram, xs_dram, ys_dram, ident_dram, keep):
    GU = 2 * P
    DOWN = KC * GU
    PIECES = 4
    PC = 2 * RW // PIECES
    with ExitStack() as ctx:
        a = Pools(nc, ctx, "rffn")
        x_in = [a.sb(f"x_in{i}", [P, D]) for i in range(4)]
        xs = [a.sb(f"xs{'hl'[s]}", [P, KC, RT * P], F32R) for s in (HI, LO)]
        y = a.sb("y", [P, RT, D])
        ident = a.sb("ident", [P, P])
        raw = a.sb("raw", [P, 2 * RW])
        w = [[a.sb(f"w{j}{'hl'[s]}", [P, 2 * RW], F32R) for s in (HI, LO)] for j in range(2)]
        sil = [a.sb(f"silu{i}", [P, P]) for i in range(2)]
        h32 = [a.sb(f"h32_{i}", [P, P]) for i in range(2)]
        hT = [[a.sb(f"hT{i}{'hl'[s]}", [P, P], F32R) for s in (HI, LO)] for i in range(2)]
        hb = [a.ps(f"hidden{i}", [P, GU]) for i in range(2)]
        tb = [a.ps(f"turned{i}", [P, P]) for i in range(2)]
        yb = [a.ps(f"y{i}", [P, D]) for i in range(2)]
        xb = [a.ps(f"x{i}", [P, KC, P]) for i in range(2)]
        s_id = a.sem("ident_loaded")
        s_in = [a.sem(f"x_loaded{i}") for i in range(4)]
        s_xt = a.sem("x_transposed")
        s_xhi = a.sem("x_hi_ready")
        s_x = a.sem("x_ready")
        s_raw = a.sem("raw_loaded")
        s_whi = a.sem("w_hi_ready")
        s_w = a.sem("w_ready")
        s_hid = a.sem("hidden_summed")
        s_sil = a.sem("silu_ready")
        s_h32 = a.sem("h32_ready")
        s_T = a.sem("h_transposed")
        s_hhi = a.sem("h_hi_ready")
        s_h = a.sem("h_ready")
        s_y = a.sem("y_summed")
        s_yadd = a.sem("y_added")
        s_zero = a.sem("y_zeroed")
        s_out = a.sem("y_stored")
        block = ctx.enter_context(nc.Block())

        def pairs(eng, body):
            body(0, True, False)
            with eng.Fori(1, RG // 2 - 1) as i:
                body(i, False, False)
            body(RG // 2 - 1, False, True)

        def walk(i, first, now, before, two_before, between=None):
            for j in range(2):
                for t in range(RT):
                    n = RT * j + t
                    k = 2 * RT * i + n
                    now(k, n, j, t)
                    if not (first and n < 1):
                        before(k - 1, n - 1)
                    if not (first and n < 2):
                        two_before(k - 2, n - 2, j if t >= 2 else 1 - j, (t - 2) % RT)
                    if between:
                        between(2 * i + j, j, t)

        @block.sync
        def _(sp):
            sp.dma_start(ident[:], ident_dram).then_inc(s_id, 16)
            for t in range(RT):
                if t >= 4:
                    sp.wait_ge(s_xt, t - 3)
                sp.dma_start(x_in[t % 4][:], xs_dram[t * P:(t + 1) * P, :]).then_inc(s_in[t % 4], 16)
                if t == 3:
                    sp.dma_start(raw[:], w_dram[0, :, :]).then_inc(s_raw, 16)

            def load(i, first, last):
                for j in range(2):
                    g = 2 * i + j
                    if last and j == 1:
                        continue
                    src = w_dram[g + 1, :, :] if isinstance(i, int) else \
                        w_dram[bass.ds(g + 1, 1), :, :].rearrange("g p n -> p (g n)")
                    sp.wait_ge(s_w, PIECES * (g + 1))
                    sp.dma_start(raw[:], src).then_inc(s_raw, 16)
            pairs(sp, load)
            for t in range(RT):
                sp.wait_ge(s_yadd, RT * (RG - 1) + t + 1)
                sp.dma_start(ys_dram[t * P:(t + 1) * P, :], y[:, t, :]).then_inc(s_out, 16)
            sp.wait_ge(s_out, 16 * RT)

        def pieces(g, j, t, last_group, split):
            if not last_group and t % 2 == 0 and 4 <= t < 4 + 2 * PIECES:
                split(g + 1, 1 - j, (t - 4) // 2)

        @block.gpsimd
        def _(pool):
            def split(g, j, piece):
                cols = slice(piece * PC, (piece + 1) * PC)
                pool.wait_ge(s_whi, PIECES * g + piece + 1)
                nc.gpsimd.tensor_tensor(w[j][LO][:, cols], raw[:, cols], f32(w[j][HI][:, cols]), ALU.subtract)\
                  .then_inc(s_w, 1)
            nc.gpsimd.memset(y[:], 0.0).then_inc(s_zero, 1)
            for piece in range(PIECES):
                split(0, 0, piece)

            def body(i, first, last):
                for j in range(2):
                    for t in range(RT):
                        pieces(2 * i + j, j, t, last and j == 1, split)
            pairs(pool, body)

        @block.scalar
        def _(act):
            def split(g, j, piece):
                cols = slice(piece * PC, (piece + 1) * PC)
                if piece == 0:
                    act.wait_ge(s_raw, 16 * (g + 1))
                    if not isinstance(g, int) or g >= 2:
                        act.wait_ge(s_y, RT * (g - 1))
                nc.scalar.copy(w[j][HI][:, cols], raw[:, cols]).then_inc(s_whi, 1)
            for t in range(RT):
                act.wait_ge(s_xt, t + 1)
                nc.scalar.copy(xs[HI][:, :, t * P:(t + 1) * P], xb[t % 2][:]).then_inc(s_xhi, 1)
                if 4 <= t < 4 + PIECES:
                    split(0, 0, t - 4)

            def silu(k, n, j, t):
                act.wait_ge(s_hid, k + 1)
                if not isinstance(k, int) or k >= 2:
                    act.wait_ge(s_h32, k - 1)
                nc.scalar.activation(sil[n % 2][:], hb[n % 2][:, 0:P], ACT.Silu).then_inc(s_sil, 1)

            def high(k, n):
                act.wait_ge(s_T, k + 1)
                if not isinstance(k, int) or k >= 2:
                    act.wait_ge(s_y, k - 1)
                nc.scalar.copy(hT[n % 2][HI][:], tb[n % 2][:]).then_inc(s_hhi, 1)

            def body(i, first, last):
                walk(i, first, silu, high, lambda *_: None,
                     lambda g, j, t: pieces(g, j, t, last and j == 1, split))
            pairs(act, body)
            high(RG * RT - 1, RG * RT - 1)

        @block.vector
        def _(dve):
            for t in range(RT):
                dve.wait_ge(s_xhi, t + 1)
                cols = slice(t * P, (t + 1) * P)
                nc.vector.tensor_tensor(xs[LO][:, :, cols], xb[t % 2][:], f32(xs[HI][:, :, cols]),
                                        ALU.subtract).then_inc(s_x, 1)
            dve.wait_ge(s_zero, 1)

            def product(k, n, j, t):
                dve.wait_ge(s_sil, k + 1)
                if not isinstance(k, int) or k >= 2:
                    dve.wait_ge(s_T, k - 1)
                nc.vector.tensor_tensor(h32[n % 2][:], hb[n % 2][:, P:GU], sil[n % 2][:], ALU.mult).then_inc(s_h32, 1)

            def low(k, n):
                dve.wait_ge(s_hhi, k + 1)
                nc.vector.tensor_tensor(hT[n % 2][LO][:], tb[n % 2][:], f32(hT[n % 2][HI][:]), ALU.subtract)\
                  .then_inc(s_h, 1)

            def add(k, n, j, t):
                dve.wait_ge(s_y, k + 1)
                nc.vector.tensor_tensor(y[:, t, :], yb[n % 2][:], y[:, t, :], ALU.add).then_inc(s_yadd, 1)
            pairs(dve, lambda i, first, last: walk(i, first, product, low, add))
            end = RG * RT
            low(end - 1, end - 1)
            add(end - 2, end - 2, 1, RT - 2)
            add(end - 1, end - 1, 1, RT - 1)

        @block.tensor
        def _(pe):
            at = {}

            def look(n):
                if n not in at:
                    t = n % RT
                    at[n] = pe.value_load(keep.offset[0:1, t:t + 1], min_val=0, max_val=RW)
                return at[n]

            pe.wait_ge(s_id, 16)
            for t in range(RT):
                pe.wait_ge(s_in[t % 4], 16 * (t // 4 + 1))
                if t >= 2:
                    pe.wait_ge(s_x, t - 1)
                for c in range(KC):
                    last = nc.tensor.transpose(xb[t % 2][:, c, :], x_in[t % 4][:, c * P:(c + 1) * P], ident[:])
                last.then_inc(s_xt, 1)
            pe.wait_ge(s_x, RT)

            def hidden(k, n, j, t):
                mine = look(n)
                if n < 2 and not (isinstance(k, int) and k < 2):
                    look(n - 2)
                if t == 0:
                    pe.wait_ge(s_w, PIECES * (k // RT + 1) if isinstance(k, int) else group_ready[j])
                if not isinstance(k, int) or k >= 2:
                    pe.wait_ge(s_h32, k - 1)
                for c in range(KC):
                    for m, (p, q) in enumerate(PASSES):
                        last = nc.tensor.matmul(hb[n % 2][:], xs[p][:, c, t * P:(t + 1) * P],
                                                w[j][q][:, bass.ds(mine + c * GU, GU)],
                                                start=(c == 0 and m == 0), stop=(c == KC - 1 and m == 2))
                    if c == 0 and n + 1 < 2 * RT:
                        look(n + 1)
                last.then_inc(s_hid, 1)

            def turn(k, n):
                pe.wait_ge(s_h32, k + 1)
                if not isinstance(k, int) or k >= 2:
                    pe.wait_ge(s_h, k - 1)
                nc.tensor.transpose(tb[n % 2][:], h32[n % 2][:], ident[:]).then_inc(s_T, 1)

            def down(k, n, j, t):
                mine = look(n)
                pe.wait_ge(s_h, k + 1)
                if not isinstance(k, int) or k >= 2:
                    pe.wait_ge(s_yadd, k - 1)
                for m, (p, q) in enumerate(PASSES):
                    last = nc.tensor.matmul(yb[n % 2][:], hT[n % 2][p][:], w[j][q][:, bass.ds(mine + DOWN, D)],
                                            start=(m == 0), stop=(m == 2))
                last.then_inc(s_y, 1)

            group_ready = [None, None]

            def body(i, first, last):
                at.clear()
                for j in range(2):
                    group_ready[j] = PIECES * (2 * i + j + 1)
                walk(i, first, hidden, turn, down)
            pairs(pe, body)
            at.clear()
            end = RG * RT
            turn(end - 1, end - 1)
            down(end - 2, end - 2, 1, RT - 2)
            down(end - 1, end - 1, 1, RT - 1)


def combine_stage(nc, ys_dram, keep, out_dram):
    with ExitStack() as ctx:
        a = Pools(nc, ctx, "comb")
        y = a.sb("y", [P, NT, D])
        s_in = [a.sem(f"rows_gathered{t}") for t in range(NT)]
        s_g = a.sem("silu_ready")
        s_out = a.sem("stored")
        block = ctx.enter_context(nc.Block())

        @block.gpsimd
        def _(pool):
            for t in range(NT):
                nc.gpsimd.indirect_dma_start(
                    out=y[:, t, :], out_offset=None, in_=ys_dram,
                    in_offset=bass.IndirectOffsetOnAxis(ap=keep.pos[:, t:t + 1], axis=0)).then_inc(s_in[t], 16)

        @block.scalar
        def _(act):
            for t in range(NT):
                act.wait_ge(s_in[t], 16)
                nc.scalar.activation(y[:, t, :], y[:, t, :], ACT.Silu, scale=keep.top[:, t:t + 1]).then_inc(s_g, 1)

        @block.sync
        def _(sp):
            for b in range(TB):
                sp.wait_ge(s_g, TPB * (b + 1))
                sp.dma_start(out_dram[BLK * b:BLK * (b + 1), :].rearrange("(t p) d -> p t d", p=P),
                             y[:, TPB * b:TPB * (b + 1), :]).then_inc(s_out, 16)
            sp.wait_ge(s_out, 16 * TB)


def time_mix_stage(nc, w_dram, vec_dram, xT_dram, x_dram, g_dram, x1_dram):
    TM_K, DECAY, FIRST, LN_G, LN_B = 0, 3, 4, 5, 6
    K_, V_, R_, O_ = range(4)
    PP, AA, BB = range(3)
    with ExitStack() as ctx:
        a = Pools(nc, ctx, "mix")
        x = a.sb("x", [P, KC, BLK + 1])
        d = a.sb("d", [P, KC, BLK])
        w = [a.sb(f"w{m}", [P, KC, D]) for m in range(4)]
        mix = [a.sb(f"mix{m}", [P, KC, BLK]) for m in range(3)]
        state = a.sb("state", [P, 3, KC, BLK + 1])
        r = a.sb("r", [P, KC, BLK])
        wkv = a.sb("wkv", [P, KC, BLK])
        ln = a.sb("ln", [P, KC, BLK])
        sq = a.sb("sq", [P, KC, BLK])
        E = [a.sb(f"e{i}", [P, 4, BLK]) for i in range(2)]
        ks = [a.sb(f"k{i}", [P, BLK]) for i in range(2)]
        vs = [a.sb(f"v{i}", [P, BLK]) for i in range(2)]
        q = [a.sb(f"q{i}", [P, BLK]) for i in range(2)]
        f2v = [a.sb(f"f2v{i}", [P, BLK]) for i in range(2)]
        rstd = a.sb("rstd", [P, BLK])
        g_in = [a.sb(f"g_in{i}", [P, D]) for i in range(2)]
        x_in = [a.sb(f"x_in{i}", [P, D]) for i in range(2)]
        vec = a.sb("vec", [P, 7, KC])
        negew = a.sb("negew", [P, KC])
        mean_w = a.sb("mean_w", [P, P])
        eps = a.sb("eps", [P, 1])
        kp = [a.ps(f"k{i}", [P, BLK]) for i in range(2)]
        vp = [a.ps(f"v{i}", [P, BLK]) for i in range(2)]
        ro = [a.ps(f"ro{i}", [P, BLK]) for i in range(2)]
        mp = a.ps("mean", [P, BLK])
        qp = a.ps("var", [P, BLK])
        N = dict(k_sum=4, v_sum=4, r_sum=4, kv_read=8, r_gate=4, diff=1, mix_kv=8, mix_r=4, carry=1,
                 pp_scan=4, q=4, e2_arg=4, shifts=12, exps=4, f2v=4, scans=8, num=12, den=12, wkv=4,
                 mean_sum=1, centred=4, square=4, var_sum=1, std=1, rstd=1, normed=4, affine=4, gated=4,
                 s_sum=4, scaled=4, x1=4)
        S = {n: a.sem(n) for n in N}
        s_const = a.sem("vectors_loaded")
        s_w = a.sem("weights_loaded")
        s_x = a.sem("x_loaded")
        s_zero = a.sem("zeroed")
        s_negew = a.sem("negew_step")
        tiles_in = [a.sem(f"tiles_loaded{i}") for i in range(2)]
        stored = [a.sem(f"x1_stored{i}") for i in range(2)]
        block = ctx.enter_context(nc.Block())

        def waiter(eng, tb):
            def wait(name, n):
                v = N[name] * tb + n
                if not (isinstance(v, int) and v <= 0):
                    eng.wait_ge(S[name], v)
            return wait

        def order(eng, load, diff, mix_kv, mix_r, kv, front, exps, back, mean, centre, variance, norm, output, gate):
            def steps(tb, before, after):
                now = waiter(eng, tb)
                prev = waiter(eng, tb - 1) if before else None
                kv(now, tb, 0)
                if before:
                    mean(prev)
                mix_r(now, tb)
                front(now, tb, 0)
                if before:
                    centre(prev)
                kv(now, tb, 1)
                exps(now, 0)
                if before:
                    variance(prev)
                front(now, tb, 1)
                if before:
                    norm(prev)
                back(now, 0)
                kv(now, tb, 2)
                exps(now, 1)
                front(now, tb, 2)
                back(now, 1)
                kv(now, tb, 3)
                exps(now, 2)
                front(now, tb, 3)
                if after:
                    load(tb + 1)
                    diff(waiter(eng, tb + 1), tb + 1)
                if before:
                    output(prev, tb - 1)
                exps(now, 3)
                back(now, 2)
                if after:
                    mix_kv(waiter(eng, tb + 1), tb + 1)
                gate(now, before)
                back(now, 3)
            load(0)
            diff(waiter(eng, 0), 0)
            mix_kv(waiter(eng, 0), 0)
            steps(0, False, True)
            with eng.Fori(1, TB - 1) as tb:
                steps(tb, True, True)
            steps(TB - 1, True, False)
            prev = waiter(eng, TB - 1)
            for step in (mean, centre, variance, norm):
                step(prev)
            output(prev, TB - 1)

        def nothing(*_):
            pass

        @block.sync
        def _(sp):
            sp.dma_start(vec[:], vec_dram).then_inc(s_const, 16)

            def load(tb):
                if isinstance(tb, int) and tb == 0:
                    sp.dma_start(x[:, :, 1:BLK + 1], xT_dram[:, :, 0:BLK]).then_inc(s_x, 16)
                    for m in range(4):
                        sp.dma_start(w[m][:], w_dram[m, :, :, :]).then_inc(s_w, 16)
                    return
                src = xT_dram[:, :, bass.ds(tb * BLK - 1, BLK + 1)] if not isinstance(tb, int) else \
                    xT_dram[:, :, tb * BLK - 1:(tb + 1) * BLK]
                waiter(sp, tb)("mix_r", 0)
                sp.dma_start(x[:], src).then_inc(s_x, 16)

            def output(wait, tb):
                def rows(t, tt):
                    row = (TPB * tb + tt) * P
                    return t[row:row + P, :] if isinstance(tb, int) else t[bass.ds(row, P), :]

                def fetch(tt):
                    if not (isinstance(tb, int) and tb == 0 and tt < 2):
                        sp.wait_ge(stored[tt % 2], 16 * (2 * tb + tt // 2))
                    sp.dma_start(g_in[tt % 2][:], rows(g_dram, tt)).then_inc(tiles_in[tt % 2], 16)
                    sp.dma_start(x_in[tt % 2][:], rows(x_dram, tt)).then_inc(tiles_in[tt % 2], 16)
                fetch(0)
                fetch(1)
                for tt in range(TPB):
                    wait("x1", tt + 1)
                    sp.dma_start(rows(x1_dram, tt), g_in[tt % 2][:]).then_inc(stored[tt % 2], 16)
                    if tt < 2:
                        fetch(tt + 2)
            order(sp, load, *[nothing] * 11, output, nothing)
            for i in range(2):
                sp.wait_ge(stored[i], 32 * TB)

        @block.gpsimd
        def _(pool):
            pool.wait_ge(s_zero, 5)

            def diff(wait, tb):
                pool.wait_ge(s_x, 16 * tb + 16)
                wait("mix_r", 0)
                nc.gpsimd.tensor_tensor(d[:], x[:, :, 1:BLK + 1], x[:, :, 0:BLK], ALU.subtract).then_inc(S["diff"], 1)

            def front(wait, tb, c):
                e = E[c % 2]
                pp = state[:, PP, c, :]
                wait("wkv", c - 1)
                wait("pp_scan", c + 1)
                nc.gpsimd.tensor_tensor(e[:, 0, :], pp[:, 0:BLK], pp[:, 1:BLK + 1], ALU.subtract)\
                  .then_inc(S["shifts"], 1)
                nc.gpsimd.tensor_tensor(e[:, 1, :], ks[c % 2][:], pp[:, 1:BLK + 1], ALU.subtract)\
                  .then_inc(S["shifts"], 1)
                wait("q", c + 1)
                nc.gpsimd.tensor_tensor(e[:, 2, :], pp[:, 0:BLK], q[c % 2][:], ALU.subtract).then_inc(S["shifts"], 1)

            def back(wait, c):
                e = E[c % 2]
                wait("exps", c + 1)
                wait("scans", 2 * c - 2)
                nc.gpsimd.tensor_tensor(f2v[c % 2][:], e[:, 1, :], vs[c % 2][:], ALU.mult).then_inc(S["f2v"], 1)
                wait("scans", 2 * c + 2)
                nc.gpsimd.tensor_tensor(e[:, 0, :], e[:, 2, :], state[:, AA, c, 0:BLK], ALU.mult).then_inc(S["num"], 1)
                nc.gpsimd.tensor_tensor(e[:, 1, :], e[:, 3, :], vs[c % 2][:], ALU.mult).then_inc(S["num"], 1)
                wait("num", 3 * c + 2)
                nc.gpsimd.tensor_tensor(e[:, 0, :], e[:, 0, :], e[:, 1, :], ALU.add).then_inc(S["num"], 1)

            def norm(wait):
                for c in range(KC):
                    wait("affine", c + 1)
                    nc.gpsimd.tensor_tensor(ln[:, c, :], ln[:, c, :], r[:, c, :], ALU.mult).then_inc(S["gated"], 1)
            order(pool, nothing, diff, nothing, nothing, nothing, front, nothing, back, nothing, nothing, nothing,
                  norm, nothing, nothing)

        @block.vector
        def _(dve):
            nc.vector.memset(mean_w[:], 1.0 / D).then_inc(s_zero, 1)
            nc.vector.memset(eps[:], 1e-5).then_inc(s_zero, 1)
            nc.vector.memset(state[:, PP, :, 0:1], -1e38).then_inc(s_zero, 1)
            nc.vector.memset(state[:, AA:BB + 1, :, 0:1], 0.0).then_inc(s_zero, 1)
            nc.vector.memset(x[:, :, 0:1], 0.0).then_inc(s_zero, 1)
            dve.wait_ge(s_zero, 5)
            dve.wait_ge(s_negew, 1)
            nc.vector.tensor_scalar_mul(negew[:], negew[:], -1.0).then_inc(s_negew, 1)
            dve.wait_ge(s_negew, 2)

            def blend(m, c, sem):
                nc.vector.scalar_tensor_tensor(mix[m][:, c, :], d[:, c, :], vec[:, TM_K + m, c:c + 1], x[:, c, 0:BLK],
                                               ALU.mult, ALU.add).then_inc(S[sem], 1)

            def mix_kv(wait, tb):
                wait("diff", 1)
                wait("v_sum", 0)
                for c in range(KC):
                    blend(K_, c, "mix_kv")
                    blend(V_, c, "mix_kv")

            def mix_r(wait, tb):
                wait("r_sum", 0)
                for c in range(KC):
                    blend(R_, c, "mix_r")
                if not (isinstance(tb, int) and tb == 0):
                    wait("num", 0)
                    wait("wkv", 0)
                    nc.vector.tensor_copy(state[:, :, :, 0:1], state[:, :, :, BLK:BLK + 1]).then_inc(S["carry"], 1)
                    wait("carry", 0)

            def front(wait, tb, c):
                k, qq = ks[c % 2], q[c % 2]
                pp = state[:, PP, c, :]
                wait("kv_read", 2 * c + 2)
                nc.vector.tensor_tensor_scan(pp[:, 1:BLK + 1], negew[:, c:c + 1].to_broadcast([P, BLK]), k[:],
                                             pp[:, 0:1], ALU.add, ALU.max).then_inc(S["pp_scan"], 1)
                wait("pp_scan", c + 1)
                wait("wkv", c - 1)
                wait("num", 3 * c - 3)
                nc.vector.scalar_tensor_tensor(qq[:], k[:], vec[:, FIRST, c:c + 1], pp[:, 0:BLK],
                                               ALU.add, ALU.max).then_inc(S["q"], 1)
                wait("q", c + 1)
                nc.vector.scalar_tensor_tensor(E[c % 2][:, 3, :], k[:], vec[:, FIRST, c:c + 1], qq[:],
                                               ALU.add, ALU.subtract).then_inc(S["e2_arg"], 1)

            def back(wait, c):
                e, qq = E[c % 2], q[c % 2]
                aa, bb = state[:, AA, c, :], state[:, BB, c, :]
                wait("exps", c + 1)
                nc.vector.tensor_tensor_scan(bb[:, 1:BLK + 1], e[:, 0, :], e[:, 1, :], bb[:, 0:1],
                                             ALU.mult, ALU.add).then_inc(S["scans"], 1)
                wait("f2v", c + 1)
                nc.vector.tensor_tensor_scan(aa[:, 1:BLK + 1], e[:, 0, :], f2v[c % 2][:], aa[:, 0:1],
                                             ALU.mult, ALU.add).then_inc(S["scans"], 1)
                wait("scans", 2 * c + 2)
                nc.vector.tensor_tensor(qq[:], e[:, 2, :], bb[:, 0:BLK], ALU.mult).then_inc(S["den"], 1)
                wait("den", 3 * c + 1)
                nc.vector.tensor_tensor(qq[:], qq[:], e[:, 3, :], ALU.add).then_inc(S["den"], 1)
                wait("den", 3 * c + 2)
                nc.vector.reciprocal(qq[:], qq[:]).then_inc(S["den"], 1)
                wait("den", 3 * c + 3)
                wait("num", 3 * c + 3)
                nc.vector.tensor_tensor(wkv[:, c, :], e[:, 0, :], qq[:], ALU.mult).then_inc(S["wkv"], 1)

            def centre(wait):
                wait("mean_sum", 1)
                for c in range(KC):
                    nc.vector.tensor_tensor(ln[:, c, :], wkv[:, c, :], mp[:], ALU.subtract).then_inc(S["centred"], 1)

            def norm(wait):
                wait("std", 1)
                nc.vector.reciprocal(rstd[:], rstd[:]).then_inc(S["rstd"], 1)
                wait("rstd", 1)
                for c in range(KC):
                    wait("square", c + 1)
                    nc.vector.tensor_tensor(ln[:, c, :], ln[:, c, :], rstd[:], ALU.mult).then_inc(S["normed"], 1)

            def output(wait, tb):
                for tt in range(TPB):
                    wait("s_sum", tt + 1)
                    dve.wait_ge(tiles_in[tt % 2], 32 * (2 * tb + tt // 2 + 1))
                    nc.vector.tensor_tensor(g_in[tt % 2][:], ro[tt % 2][:], g_in[tt % 2][:], ALU.mult)\
                      .then_inc(S["scaled"], 1)
                    wait("scaled", tt + 1)
                    nc.vector.tensor_tensor(g_in[tt % 2][:], g_in[tt % 2][:], x_in[tt % 2][:], ALU.add)\
                      .then_inc(S["x1"], 1)
            order(dve, nothing, nothing, mix_kv, mix_r, nothing, front, nothing, back, nothing, centre, nothing,
                  norm, output, nothing)

        @block.scalar
        def _(act):
            act.wait_ge(s_const, 16)
            nc.scalar.activation(negew[:], vec[:, DECAY, :], ACT.Exp).then_inc(s_negew, 1)
            act.wait_ge(s_zero, 5)

            def kv(wait, tb, c):
                wait("num", 3 * c - 3)
                wait("e2_arg", c - 1)
                wait("k_sum", c + 1)
                nc.scalar.copy(ks[c % 2][:], kp[c % 2][:]).then_inc(S["kv_read"], 1)
                wait("v_sum", c + 1)
                nc.scalar.copy(vs[c % 2][:], vp[c % 2][:]).then_inc(S["kv_read"], 1)

            def exps(wait, c):
                wait("shifts", 3 * c + 3)
                wait("e2_arg", c + 1)
                nc.scalar.activation(E[c % 2][:], E[c % 2][:], ACT.Exp).then_inc(S["exps"], 1)

            def centre(wait):
                for c in range(KC):
                    wait("centred", c + 1)
                    nc.scalar.activation(sq[:, c, :], ln[:, c, :], ACT.Square).then_inc(S["square"], 1)

            def norm(wait):
                wait("var_sum", 1)
                nc.scalar.activation(rstd[:], qp[:], ACT.Sqrt, bias=eps[:]).then_inc(S["std"], 1)
                for c in range(KC):
                    wait("normed", c + 1)
                    nc.scalar.activation(ln[:, c, :], ln[:, c, :], ACT.Identity, bias=vec[:, LN_B, c:c + 1],
                                         scale=vec[:, LN_G, c:c + 1]).then_inc(S["affine"], 1)

            def gate(wait, before):
                wait("gated", 0)
                for c in range(KC):
                    wait("r_sum", c + 1)
                    nc.scalar.activation(r[:, c, :], ro[c % 2][:], ACT.Sigmoid).then_inc(S["r_gate"], 1)
            order(act, nothing, nothing, nothing, nothing, kv, nothing, exps, nothing, nothing, centre, nothing,
                  norm, nothing, gate)

        @block.tensor
        def _(pe):
            pe.wait_ge(s_zero, 5)

            def project(bank, m, c, sem):
                for k in range(KC):
                    last = nc.tensor.matmul(bank[:], w[m][:, k, c * P:(c + 1) * P], mix[m][:, k, :],
                                            start=(k == 0), stop=(k == KC - 1))
                last.then_inc(S[sem], 1)

            def average(bank, src, sem):
                for k in range(KC):
                    last = nc.tensor.matmul(bank[:], mean_w[:], src[:, k, :], start=(k == 0), stop=(k == KC - 1))
                last.then_inc(S[sem], 1)

            def kv(wait, tb, c):
                if isinstance(tb, int) and tb == 0 and c == 0:
                    pe.wait_ge(s_w, 64)
                if c == 0:
                    wait("mix_kv", 8)
                wait("kv_read", 2 * c - 2)
                project(kp[c % 2], K_, c, "k_sum")
                project(vp[c % 2], V_, c, "v_sum")

            def mean(wait):
                wait("wkv", 4)
                average(mp, wkv, "mean_sum")

            def variance(wait):
                wait("square", 4)
                average(qp, sq, "var_sum")

            def output(wait, tb):
                wait("gated", 4)
                for tt in range(TPB):
                    if tt < 2:
                        wait("r_gate", 3 + tt)
                    else:
                        wait("scaled", tt - 1)
                    for k in range(KC):
                        last = nc.tensor.matmul(ro[tt % 2][:], ln[:, k, tt * P:(tt + 1) * P], w[O_][:, k, :],
                                                start=(k == 0), stop=(k == KC - 1))
                    last.then_inc(S["s_sum"], 1)

            def gate(wait, before):
                wait("mix_r", 4)
                for c in range(KC):
                    if c >= 2:
                        wait("r_gate", c - 1)
                    elif before:
                        wait("scaled", c - 1)
                    project(ro[c % 2], R_, c, "r_sum")
            order(pe, nothing, nothing, nothing, nothing, kv, nothing, nothing, nothing, mean, nothing, variance,
                  nothing, output, gate)


def top4_router(nc, A, keep, xn_dram, idx_dram):
    E, TOP = 16, 4

    def router(a, yb):
        env = Stage()
        ident = a.sb("ident", [P, P])
        raw = a.sb("cen_raw", [P, KC, E])
        cen = [a.sb(f"cen{'hl'[s]}", [P, KC, E], F32R) for s in (HI, LO)]
        bias = a.sb("bias", [P, E])
        lower = a.sb("lower", [P, E, E])
        consts = a.sb("consts", [P, P + 2 * NT + 8 + MT])
        tri, ids, keep_on = consts[:, 0:P], consts[:, P:P + NT], consts[:, P + NT:P + 2 * NT]
        starts, tile_no = consts[:, P + 2 * NT:P + 2 * NT + 8], consts[:, P + 2 * NT + 8:]
        ones = a.sb("ones", [P, P])
        zero = a.sb("zero", [P, 2 * MT])
        sc = a.sb("scores", [P, NT, E])
        rank = a.sb("rank", [P, NT, E])
        sel = a.sb("sel", [P, NT, E])
        red = a.sb("red", [P, NT])
        gt = a.sb("greater", [P, 4, E * E])
        eq = a.sb("equal", [P, 4, E * E])
        tiles = a.sb("tiles", [P, E])
        upto = a.sb("tiles_upto", [P, E])
        base = a.sb("base", [P, E])
        counts = a.ps("counts", [P, 2, NT, E])
        ps = yb[0][:, 0:NT * E].rearrange("p (t e) -> p t e", e=E)
        s_in = a.sem("router_loaded")
        s_c = a.sem("router_chain")
        s_cen = a.sem("centroids_ready")
        s_lg = a.sem("logits_summed")
        s_lgT = a.sem("sigmoid_rows")
        s_read = a.sem("scores_read")
        s_sel = a.sem("sel_ready")
        s_cnt = a.sem("counted")
        s_pos = a.sem("places_ready")
        s_zero = a.sem("zero_ready")
        s_fill = a.sem("rows_zeroed")
        s_xn = a.sem("xn_stored")
        s_scat = a.sem("tokens_scattered")
        flat = [m[:].rearrange("p a n -> p (a n)") for m in (gt, eq)]
        lgT = [m[0:E, i * BLK:(i + 1) * BLK] for m in flat for i in range(2)]
        total, cum = (m[:, 0:E * NT].rearrange("p (e t) -> p e t", t=NT) for m in flat)
        place = flat[1][:, E * NT:2 * E * NT].rearrange("p (t e) -> p t e", e=E)
        mine, prod = (flat[i][:, 2 * E * NT:3 * E * NT].rearrange("p (t e) -> p t e", e=E) for i in range(2))
        go_on = flat[0][:, 2 * E * NT:3 * E * NT].rearrange("p (e t) -> p e t", t=NT)
        more = flat[0][:, 3 * E * NT:3 * E * NT + 8 * E].rearrange("p (e k) -> p e k", k=8)
        past = flat[0][:, 0:MT * E].rearrange("p (i e) -> p i e", e=E)

        def sync(sp):
            for dst, src in ((ident, A["ident"]), (raw, A["moe_cen"]), (bias, A["moe_bias"]),
                             (lower, A["moe_lower"]), (consts, A["moe_consts"])):
                sp.dma_start(dst[:], src).then_inc(s_in, 16)
            sp.dma_start(xn_dram.rearrange("(t p) d -> p t d", p=P), keep.y[:]).then_inc(s_xn, 16)
            sp.wait_ge(s_zero, 1)
            sp.dma_start(idx_dram.rearrange("(p a) o -> p (a o)", p=P), zero[:]).then_inc(s_fill, 16)

        def vector(dve):
            link = Chain(dve, s_c)
            nc.vector.memset(zero[:], 0.0).then_inc(s_zero, 1)
            link(nc.vector.memset(ones[:], 1.0))
            dve.wait_ge(s_in, 16 * 5)
            link(nc.vector.tensor_copy(cen[HI][:], raw[:]))
            nc.vector.tensor_tensor(cen[LO][:], raw[:], f32(cen[HI][:]), ALU.subtract).then_inc(s_cen, 1)
            dve.wait_ge(s_lg, TB + 1)
            nc.vector.tensor_tensor(sc[:], ps, bias[:].unsqueeze(1).to_broadcast([P, NT, E]), ALU.add)\
              .then_inc(s_read, 1)
            dve.wait_ge(s_read, 1)
            for b in range(4):
                part = sc[:, 4 * b:4 * b + 4, :]
                g4, e4 = (m[:].rearrange("p t (i j) -> p t i j", j=E) for m in (gt, eq))
                other = part.unsqueeze(2).to_broadcast([P, 4, E, E])
                own = part.unsqueeze(3).to_broadcast([P, 4, E, E])
                link(nc.vector.tensor_tensor(g4, other, own, ALU.is_gt))
                link(nc.vector.tensor_tensor(e4, other, own, ALU.is_equal))
                link(nc.vector.tensor_tensor(eq[:], eq[:], lower[:].rearrange("p i j -> p (i j)").unsqueeze(1)
                                             .to_broadcast([P, 4, E * E]), ALU.mult))
                link(nc.vector.tensor_tensor(gt[:], gt[:], eq[:], ALU.add))
                link(nc.vector.tensor_reduce(rank[:, 4 * b:4 * b + 4, :], g4, AX.X, ALU.add))
            nc.vector.tensor_scalar(sel[:], rank[:], float(TOP), None, ALU.is_lt).then_inc(s_sel, 1)
            dve.wait_ge(s_sel, 1)
            link(nc.vector.tensor_tensor(sc[:], sc[:], sel[:], ALU.mult))
            link(nc.vector.tensor_reduce(red[:], sc[:], AX.X, ALU.add))
            link(nc.vector.tensor_scalar(red[:], red[:], 1e-8, None, ALU.max))
            link(nc.vector.reciprocal(red[:], red[:]))
            link(nc.vector.tensor_tensor(sc[:], sc[:], red[:].unsqueeze(2).to_broadcast([P, NT, E]), ALU.mult))
            dve.wait_ge(s_cnt, 1)
            link(nc.vector.tensor_copy(total.rearrange("p e t -> p t e"), counts[:, 1]))
            link(nc.vector.tensor_copy(go_on, keep_on.unsqueeze(1).to_broadcast([P, E, NT])))
            link(nc.vector.tensor_tensor_scan(cum.rearrange("p e t -> p (e t)"), go_on.rearrange("p e t -> p (e t)"),
                                              total.rearrange("p e t -> p (e t)"), 0.0, ALU.mult, ALU.add))
            link(nc.vector.tensor_tensor(more, cum[:, :, NT - 1:NT].to_broadcast([P, E, 8]),
                                         starts.unsqueeze(1).to_broadcast([P, E, 8]), ALU.is_gt))
            link(nc.vector.tensor_reduce(tiles[:], more, AX.X, ALU.add))
            link(nc.vector.tensor_tensor_scan(upto[:], ones[:, 0:E], tiles[:], 0.0, ALU.mult, ALU.add))
            link(nc.vector.tensor_tensor(base[:], upto[:], tiles[:], ALU.subtract))
            link(nc.vector.tensor_scalar(base[:], base[:], float(MR), -1.0, ALU.mult, ALU.add))
            link(nc.vector.tensor_tensor(cum, cum, total, ALU.subtract))
            link(nc.vector.tensor_tensor(cum, cum, base[:].unsqueeze(2).to_broadcast([P, E, NT]), ALU.add))
            link(nc.vector.tensor_tensor(place, counts[:, 0], cum.rearrange("p e t -> p t e"), ALU.add))
            for s in range(TOP):
                link(nc.vector.tensor_scalar(mine, rank[:], float(s), None, ALU.is_equal))
                link(nc.vector.tensor_tensor(prod, mine, place, ALU.mult))
                link(nc.vector.tensor_reduce(red[:], prod, AX.X, ALU.add))
                link(nc.vector.tensor_copy(keep.pos4[:, s, :], red[:]))
                link(nc.vector.tensor_tensor(prod, mine, sc[:], ALU.mult))
                link(nc.vector.tensor_reduce(keep.gate4[:, s, :], prod, AX.X, ALU.add))
            link(nc.vector.tensor_tensor(past, tile_no.unsqueeze(2).to_broadcast([P, MT, E]),
                                         upto[:].unsqueeze(1).to_broadcast([P, MT, E]), ALU.is_ge))
            link(nc.vector.tensor_reduce(flat[1][:, 0:MT], past, AX.X, ALU.add))
            link(nc.vector.tensor_scalar(flat[1][:, 0:MT], flat[1][:, 0:MT], float(E - 1), None, ALU.min))
            nc.vector.tensor_copy(keep.expert[:], flat[1][:, 0:MT]).then_inc(s_pos, 1)
            dve.wait_ge(s_xn, 16)

        def scalar(act):
            for b in range(TB):
                act.wait_ge(s_lg, b + 1)
                nc.scalar.activation(lgT[b], yb[b][0:E, :], ACT.Sigmoid).then_inc(s_lgT, 1)

        def tensor(pe):
            logits_tensor(nc, pe, keep, cen, s_cen, yb, lgT, s_lgT, ident, E, ps, s_lg)

        def tensor_step(pe, k):
            if k == 2:
                pe.wait_ge(s_sel, 1)
                nc.tensor.matmul(counts[:, 0].rearrange("p t e -> p (t e)"), tri,
                                 sel[:].rearrange("p t e -> p (t e)"), start=True, stop=True)
                nc.tensor.matmul(counts[:, 1].rearrange("p t e -> p (t e)"), ones[:],
                                 sel[:].rearrange("p t e -> p (t e)"), start=True, stop=True).then_inc(s_cnt, 1)

        def pool_step(pool, k):
            if k == 4:
                pool.wait_ge(s_fill, 16)
                pool.wait_ge(s_pos, 1)
            if k >= 4:
                for t in range(4 * (k - 4), 4 * (k - 4) + 4):
                    for s in range(TOP):
                        nc.gpsimd.indirect_dma_start(
                            out=idx_dram, out_offset=bass.IndirectOffsetOnAxis(ap=keep.pos4[:, s, t:t + 1], axis=0),
                            in_=ids[:, t:t + 1], in_offset=None).then_inc(s_scat, 16)
            if k == 7:
                pool.wait_ge(s_scat, 16 * NT * TOP)

        env.sync, env.vector, env.scalar, env.tensor = sync, vector, scalar, tensor
        env.tensor_step, env.pool_step = tensor_step, pool_step
        env.tensor_before_y = lambda pe: pe.wait_ge(s_read, 1)
        return env

    return router


MR = 256
MT = T * 4 // MR + 15
MF = 3


def routed_experts_stage(nc, A, xn_dram, idx_dram, ys_dram, keep):
    W1, W2 = KC * MF * P, MF * D
    with ExitStack() as ctx:
        a = Pools(nc, ctx, "moe")
        raw1 = [a.sb(f"raw1_{j}", [P, W1 + MF]) for j in range(2)]
        raw2 = a.sb("raw2", [P, W2])
        w1 = [[a.sb(f"w1_{j}{'hl'[s]}", [P, W1], F32R) for s in (HI, LO)] for j in range(2)]
        w2 = [[a.sb(f"w2_{j}{'hl'[s]}", [P, W2], F32R) for s in (HI, LO)] for j in range(2)]
        b1 = [a.sb(f"b1_{j}", [P, MF]) for j in range(2)]
        x_in = [[a.sb(f"x_in{j}{tt}", [P, D]) for tt in range(2)] for j in range(2)]
        xs = [[a.sb(f"xs{j}{'hl'[s]}", [P, KC, MR], F32R) for s in (HI, LO)] for j in range(2)]
        h32 = [a.sb(f"h32_{f}", [P, MR]) for f in range(MF)]
        h = [[a.sb(f"h{j}{'hl'[s]}", [P, MF, MR], F32R) for s in (HI, LO)] for j in range(2)]
        y = a.sb("y", [P, 2, D])
        ident = a.sb("ident", [P, P])
        rows = a.sb("rows", [2 * MT, P])
        idx = a.sb("idx", [P, 2 * MT], mybir.dt.uint32)
        now = [a.sb(f"idx_now{j}", [P, 2], mybir.dt.uint32) for j in range(2)]
        carrier = a.sb("carrier", [P, 1])
        s_carrier = a.sem("carrier_set")
        hb = [a.ps(f"hidden{f}", [P, MR]) for f in range(MF)]
        xb = [a.ps(f"x{i}", [P, KC, P]) for i in range(2)]
        yb = [a.ps(f"y{i}", [P, D]) for i in range(2)]
        ib = a.ps("idx", [P, 2 * MT])
        s_id = a.sem("ident_loaded")
        s_rows = a.sem("rows_loaded")
        s_ib = a.sem("rows_turned")
        s_idx = a.sem("idx_ready")
        s_now = a.sem("idx_now")
        s_raw1 = [a.sem(f"w1_loaded{j}") for j in range(2)]
        s_raw2 = a.sem("w2_loaded")
        s_b1 = a.sem("b1_ready")
        s_w1hi = a.sem("w1_hi_ready")
        s_w1 = a.sem("w1_ready")
        s_w2hi = a.sem("w2_hi_ready")
        s_w2 = a.sem("w2_ready")
        s_gath = [a.sem(f"x_gathered{j}") for j in range(2)]
        s_xt = a.sem("x_turned")
        s_xhi = a.sem("x_hi_ready")
        s_x = a.sem("x_ready")
        s_hid = a.sem("hidden_summed")
        s_h32 = a.sem("h32_ready")
        s_hhi = a.sem("h_hi_ready")
        s_h = a.sem("h_ready")
        s_y = a.sem("y_summed")
        s_yc = a.sem("y_copied")
        s_out = a.sem("y_stored")
        block = ctx.enter_context(nc.Block())

        def tiles(eng, run):
            run(0, 0)
            run(1, 1)
            with eng.Fori(1, (MT - 3) // 2) as i:
                run(2 * i, 0)
                run(2 * i + 1, 1)
            for s in range(MT - 3, MT):
                run(s, s % 2)

        def after(s, n):
            return not isinstance(s, int) or s + n < MT

        def wait(eng, sem, v):
            if not (isinstance(v, int) and v <= 0):
                eng.wait_ge(sem, v)

        @block.sync
        def _(sp):
            def weights_of(src_dram, s):
                e = sp.value_load(keep.expert[0:1, s:s + 1] if isinstance(s, int) else
                                  keep.expert[0:1, bass.ds(s, 1)], min_val=0, max_val=15)
                return src_dram[bass.ds(e, 1), :, :].rearrange("g p n -> p (g n)")
            sp.dma_start(rows[:], idx_dram.rearrange("(a p) o -> a (p o)", p=P)).then_inc(s_rows, 16)
            sp.dma_start(ident[:], A["ident"]).then_inc(s_id, 16)
            src = weights_of(A["moe_w1"], 0)
            sp.dma_start(raw1[0][:], src).then_inc(s_raw1[0], 16)
            src = weights_of(A["moe_w1"], 1)
            sp.dma_start(raw1[1][:], src).then_inc(s_raw1[1], 16)
            src = weights_of(A["moe_w2"], 0)
            sp.dma_start(raw2[:], src).then_inc(s_raw2, 16)

            def run(s, j):
                if after(s, 2):
                    src = weights_of(A["moe_w1"], s + 2)
                    wait(sp, s_w1, s + 1)
                    sp.dma_start(raw1[j][:], src).then_inc(s_raw1[j], 16)
                if after(s, 1):
                    src = weights_of(A["moe_w2"], s + 1)
                    wait(sp, s_w2, s + 1)
                    sp.dma_start(raw2[:], src).then_inc(s_raw2, 16)
                if not (isinstance(s, int) and s == 0):
                    store(s - 1)

            def store(s):
                dst = ys_dram[s * MR:(s + 1) * MR, :] if isinstance(s, int) else ys_dram[bass.ds(s * MR, MR), :]
                wait(sp, s_yc, 2 * s + 2)
                sp.dma_start(dst.rearrange("(t p) d -> p t d", p=P), y[:]).then_inc(s_out, 16)
            tiles(sp, run)
            store(MT - 1)
            sp.wait_ge(s_out, 16 * MT)

        @block.gpsimd
        def _(pool):
            def gather(s, j):
                wait(pool, s_xt, 2 * s - 2)
                src = idx[:, 2 * s:2 * s + 2] if isinstance(s, int) else idx[:, bass.ds(2 * s, 2)]
                nc.gpsimd.tensor_copy(now[j][:], src).then_inc(s_now, 1)
                wait(pool, s_now, s + 1)
                nc.gpsimd.tensor_tensor(carrier[:], carrier[:], carrier[:], ALU.add)
                for tt in range(2):
                    nc.gpsimd.indirect_dma_start(
                        out=x_in[j][tt][:], out_offset=None, in_=xn_dram,
                        in_offset=bass.IndirectOffsetOnAxis(ap=now[j][:, tt:tt + 1], axis=0)).then_inc(s_gath[j], 16)

            def split(s, j):
                wait(pool, s_w1hi, s + 1)
                nc.gpsimd.tensor_tensor(w1[j][LO][:], raw1[j][:, 0:W1], f32(w1[j][HI][:]), ALU.subtract).then_inc(s_w1, 1)
            nc.gpsimd.memset(carrier[:], 0.0).then_inc(s_carrier, 1)
            pool.wait_ge(s_carrier, 1)
            pool.wait_ge(s_idx, 1)
            gather(0, 0)
            gather(1, 1)
            split(0, 0)

            def run(s, j):
                if after(s, 1):
                    split(s + 1, 1 - j)
                if after(s, 2):
                    gather(s + 2, j)
            tiles(pool, run)

        @block.scalar
        def _(act):
            def split1(s, j):
                if isinstance(s, int):
                    wait(act, s_raw1[j], 16 * ((s - j) // 2 + 1))
                else:
                    wait(act, s_raw1[j], 8 * s - 8 * j + 16)
                wait(act, s_hid, MF * (s - 1))
                wait(act, s_h32, MF * (s - 1))
                nc.scalar.copy(b1[j][:], raw1[j][:, W1:W1 + MF]).then_inc(s_b1, 1)
                nc.scalar.copy(w1[j][HI][:], raw1[j][:, 0:W1]).then_inc(s_w1hi, 1)

            def high_x(s, j):
                for tt in range(2):
                    wait(act, s_xt, 2 * s + tt + 1)
                    nc.scalar.copy(xs[j][HI][:, :, tt * P:(tt + 1) * P], xb[tt][:]).then_inc(s_xhi, 1)
            split1(0, 0)
            high_x(0, 0)

            def run(s, j):
                if after(s, 1):
                    split1(s + 1, 1 - j)
                wait(act, s_raw2, 16 * (s + 1))
                wait(act, s_y, 2 * (s - 1))
                nc.scalar.copy(w2[j][HI][:], raw2[:]).then_inc(s_w2hi, 1)
                for f in range(MF):
                    wait(act, s_hid, MF * s + f + 1)
                    wait(act, s_h, MF * (s - 1) + f + 1)
                    if f == 0:
                        wait(act, s_b1, s + 1)
                    nc.scalar.activation(h32[f][:], hb[f][:], ACT.Relu, bias=b1[j][:, f:f + 1]).then_inc(s_h32, 1)
                for f in range(MF):
                    wait(act, s_h32, MF * s + f + 1)
                    nc.scalar.copy(h[j][HI][:, f, :], h32[f][:]).then_inc(s_hhi, 1)
                if after(s, 1):
                    high_x(s + 1, 1 - j)
            tiles(act, run)

        @block.vector
        def _(dve):
            def low_x(s, j):
                for tt in range(2):
                    cols = slice(tt * P, (tt + 1) * P)
                    wait(dve, s_xhi, 2 * s + tt + 1)
                    nc.vector.tensor_tensor(xs[j][LO][:, :, cols], xb[tt][:], f32(xs[j][HI][:, :, cols]),
                                            ALU.subtract).then_inc(s_x, 1)

            def copy_y(s):
                for tt in range(2):
                    wait(dve, s_y, 2 * s + tt + 1)
                    if tt == 0:
                        wait(dve, s_out, 16 * s)
                    nc.vector.tensor_copy(y[:, tt, :], yb[tt][:]).then_inc(s_yc, 1)
            dve.wait_ge(s_ib, 1)
            nc.vector.tensor_copy(idx[:], ib[:]).then_inc(s_idx, 1)
            low_x(0, 0)

            def run(s, j):
                wait(dve, s_w2hi, s + 1)
                nc.vector.tensor_tensor(w2[j][LO][:], raw2[:], f32(w2[j][HI][:]), ALU.subtract).then_inc(s_w2, 1)
                for f in range(MF):
                    wait(dve, s_hhi, MF * s + f + 1)
                    nc.vector.tensor_tensor(h[j][LO][:, f, :], h32[f][:], f32(h[j][HI][:, f, :]), ALU.subtract)\
                      .then_inc(s_h, 1)
                if after(s, 1):
                    low_x(s + 1, 1 - j)
                if not (isinstance(s, int) and s == 0):
                    copy_y(s - 1)
            tiles(dve, run)
            copy_y(MT - 1)

        @block.tensor
        def _(pe):
            def turn_x(s, j):
                for tt in range(2):
                    if tt == 0:
                        if isinstance(s, int):
                            wait(pe, s_gath[j], 32 * ((s - j) // 2 + 1))
                        else:
                            wait(pe, s_gath[j], 16 * s - 16 * j + 32)
                    wait(pe, s_x, 2 * s + tt - 1)
                    for c in range(KC):
                        last = nc.tensor.transpose(xb[tt][:, c, :], x_in[j][tt][:, c * P:(c + 1) * P], ident[:])
                    last.then_inc(s_xt, 1)

            def down(s, j):
                wait(pe, s_h, MF * (s + 1))
                wait(pe, s_w2, s + 1)
                for tt in range(2):
                    wait(pe, s_yc, 2 * (s - 1) + tt + 1)
                    for f in range(MF):
                        for n, (p, q) in enumerate(PASSES):
                            last = nc.tensor.matmul(yb[tt][:], h[j][p][:, f, tt * P:(tt + 1) * P],
                                                    w2[j][q][:, f * D:(f + 1) * D],
                                                    start=(f == 0 and n == 0), stop=(f == MF - 1 and n == 2))
                    last.then_inc(s_y, 1)
            pe.wait_ge(s_rows, 16)
            pe.wait_ge(s_id, 16)
            nc.tensor.transpose(ib[:], rows[:], ident[0:2 * MT, 0:2 * MT]).then_inc(s_ib, 1)
            turn_x(0, 0)

            def run(s, j):
                wait(pe, s_w1, s + 1)
                wait(pe, s_x, 2 * s + 2)
                for f in range(MF):
                    wait(pe, s_h32, MF * (s - 1) + f + 1)
                    for c in range(KC):
                        col = c * MF * P + f * P
                        for n, (p, q) in enumerate(PASSES):
                            last = nc.tensor.matmul(hb[f][:], w1[j][p][:, col:col + P], xs[j][q][:, c, :],
                                                    start=(c == 0 and n == 0), stop=(c == KC - 1 and n == 2))
                    last.then_inc(s_hid, 1)
                if after(s, 1):
                    turn_x(s + 1, 1 - j)
                if not (isinstance(s, int) and s == 0):
                    down(s - 1, 1 - j)
            tiles(pe, run)
            down(MT - 1, (MT - 1) % 2)


def mix_experts_stage(nc, ys_dram, keep, out_dram):
    TOP, DEPTH = 4, 8
    with ExitStack() as ctx:
        a = Pools(nc, ctx, "mixe")
        rows = [a.sb(f"rows{i}", [P, D]) for i in range(DEPTH)]
        s_in = [a.sem(f"rows_gathered{i}") for i in range(DEPTH)]
        s_add = a.sem("added")
        s_g = a.sem("silu_ready")
        s_out = a.sem("stored")
        block = ctx.enter_context(nc.Block())
        y = keep.y

        @block.gpsimd
        def _(pool):
            for n in range(TOP * NT):
                t, s, i = n // TOP, n % TOP, n % DEPTH
                if n >= DEPTH:
                    pool.wait_ge(s_add, n - DEPTH + 1)
                nc.gpsimd.indirect_dma_start(
                    out=rows[i][:], out_offset=None, in_=ys_dram,
                    in_offset=bass.IndirectOffsetOnAxis(ap=keep.pos4[:, s, t:t + 1], axis=0)).then_inc(s_in[i], 16)

        @block.vector
        def _(dve):
            for n in range(TOP * NT):
                t, s, i = n // TOP, n % TOP, n % DEPTH
                dve.wait_ge(s_in[i], 16 * (n // DEPTH + 1))
                if s:
                    dve.wait_ge(s_add, n)
                nc.vector.scalar_tensor_tensor(y[:, t, :], rows[i][:], keep.gate4[:, s, t:t + 1], y[:, t, :],
                                               ALU.mult, ALU.add).then_inc(s_add, 1)

        @block.scalar
        def _(act):
            for t in range(NT):
                act.wait_ge(s_add, TOP * (t + 1))
                nc.scalar.activation(y[:, t, :], y[:, t, :], ACT.Silu).then_inc(s_g, 1)

        @block.sync
        def _(sp):
            for b in range(TB):
                sp.wait_ge(s_g, TPB * (b + 1))
                sp.dma_start(out_dram[BLK * b:BLK * (b + 1), :].rearrange("(t p) d -> p t d", p=P),
                             y[:, TPB * b:TPB * (b + 1), :]).then_inc(s_out, 16)
            sp.wait_ge(s_out, 16 * TB)


H, HKV, DV = 16, 4, 64
MBLK, NPOOL, WIN = 64, 28, 256
WQ, WK, WV, WOUT = 0, 1024, 1536, 1792
AW = 2816


def attention_stage(nc, A, x1_dram, g_dram, out_dram, keep):
    PARTS = [(WK, WOUT), (WQ, WK), (WOUT, AW)]
    with ExitStack() as ctx:
        a = Pools(nc, ctx, "att")
        xn = keep.xn
        raw_kv = a.sb("raw_kv", [P, WOUT - WK])
        raw_q = a.sb("raw_q", [P, WK - WQ])
        w = [a.sb(f"w{'hl'[s]}", [P, AW], F32R) for s in (HI, LO)]
        s_acc = a.sb("s_acc", [P, NT, D])
        rope = [a.sb(f"rope{i}", [P, 2, BLK]) for i in range(2)]
        q32 = [a.sb(f"q32_{i}", [P, BLK]) for i in range(2)]
        qp = [[a.sb(f"q{i}{'hl'[s]}", [P, BLK], F32R) for s in (HI, LO)] for i in range(2)]
        t1 = [a.sb(f"t1_{i}", [P, BLK]) for i in range(2)]
        rot = [a.sb(f"rot{i}", [P, BLK]) for i in range(2)]
        qr = [a.sb(f"qr{'hl'[s]}", [P, 2, BLK], F32R) for s in (HI, LO)]
        sm = [a.sb(f"sm{i}", [P, TPB, 4, 32]) for i in range(2)]
        sw = a.sb("sw", [P, 2, 4, WIN])
        pT = [a.sb(f"pT{'hl'[s]}", [P, BLK], F32R) for s in (HI, LO)]
        pw = [a.sb(f"pw{'hl'[s]}", [P, 2, WIN], F32R) for s in (HI, LO)]
        oT = [a.sb(f"oT{'hl'[s]}", [P, 2, BLK], F32R) for s in (HI, LO)]
        kbd = [a.sb(f"kbd{'hl'[s]}", [P, 2, 32], F32R) for s in (HI, LO)]
        kwin = [a.sb(f"kwin{'hl'[s]}", [P, 2, WIN], F32R) for s in (HI, LO)]
        vbd = [a.sb(f"vbd{'hl'[s]}", [P, 2, 2, DV], F32R) for s in (HI, LO)]
        vwin = [a.sb(f"vwin{'hl'[s]}", [P, 2, 3, DV], F32R) for s in (HI, LO)]
        xbar = [a.sb(f"xbar{'hl'[s]}", [P, KC, 4, 32], F32R) for s in (HI, LO)]
        pool_s = [sm[0][:, :, i, :] for i in range(2)]
        kpool = a.sb("kpool", [P, 32])
        ident = a.sb("ident", [P, P])
        perm = a.sb("perm", [P, P], F32R)
        madd = a.sb("madd", [P, NT, 32])
        mmul = a.sb("mmul", [P, 32])
        extra = a.sb("extra", [P, 32])
        wmask = a.sb("wmask", [P, 3 * P])
        scale = a.sb("scale", [P, 2 * HKV])
        scale_now = a.sb("scale_now", [P, 2])
        mx = a.sb("mx", [P, TPB * 4])
        mw = a.sb("mw", [P, 8])
        bA = [a.ps(f"qsum{i}", [P, BLK]) for i in range(2)]
        bB = a.ps("swapped", [P, BLK])
        bS = a.ps("scores", [P, TPB, 2, 2, 32])
        bT = a.ps("pT", [P, BLK])
        bP = a.ps("pv", [P, BLK])
        bO = [a.ps(f"o{i}", [P, D]) for i in range(2)]
        bW = [bS[:].rearrange("p t c h k -> p (t c h k)"), bT[:]]
        N = dict(q_sum=12, q32=12, q_hi=12, q_lo=12, t1=12, swapped=12, t2=12, rotated=12, qr_hi=8, qr_lo=8,
                 k_pool=4, kp_mean=1, k_hi=4, k_lo=4, v_sum=3, v_hi=6, v_lo=6, scores=4, masked=4, max=4, shifted=4,
                 exps=4, prob=4, sums=4, inv=4, pT_sum=4, pT_hi=4, pT_lo=4, pv=6, o_hi=8, o_lo=8, s_sum=16, s_add=16,
                 win_s=4, win_m=4, win_max=1, win_mx=1, win_sh=2, win_e=2, win_sum=1, win_tot=1, win_p=2,
                 win_T=4, win_hi=4, win_lo=4, w_hi=3, w_lo=3, m_mul=1, m_add=1, m_fix=1, scale=1, win_pv=4)
        S = {n: a.sem(n) for n in N}
        s_kv = a.sem("kv_weights_loaded")
        s_q = a.sem("q_out_weights_loaded")
        s_rope = [a.sem(f"rope_loaded{i}") for i in range(2)]
        s_const = a.sem("const_loaded")
        s_zero = a.sem("zeroed")
        s_xb = a.sem("xbar_step")
        s_xbr = a.sem("xbar_ready")
        s_perm = a.sem("perm_ready")
        s_sc = a.sem("scale_step")
        s_tile = [a.sem(f"tiles_loaded{i}") for i in range(2)]
        s_st = [a.sem(f"stored{i}") for i in range(2)]
        s_fin = a.sem("final_step")
        s_res = a.sem("result")
        block = ctx.enter_context(nc.Block())

        def as_pair(m):
            return m.rearrange("p (a h) k -> p a (h k)", a=2)
        pair_x = [rope[0][:], as_pair(sw[:, 0])]
        pair_g = [rope[1][:], as_pair(sw[:, 1])]

        def waiter(eng, g):
            def wait(name, n):
                v = N[name] * g + n
                if not (isinstance(v, int) and v <= 0):
                    eng.wait_ge(S[name], v)
            return wait

        def groups(eng, boundary, main):
            now = waiter(eng, 0)
            boundary(now, None, 0, None)
            main(now, 0)
            with eng.Fori(1, HKV) as g:
                now = waiter(eng, g)
                boundary(now, waiter(eng, g - 1), g, g - 1)
                main(now, g)
            boundary(None, waiter(eng, HKV - 1), None, HKV - 1)

        def order(eng, weights, start, finish, values, mask, exps, probs, turn, attend, turn_win, attend_win, output):
            def boundary(now, last, g, g_last):
                if now:
                    weights(now, g, 0)
                if last:
                    finish(last, g_last, 11)
                    turn(last, 2)
                if now:
                    start(now, g, 0)
                if last:
                    attend(last, 2, 0)
                    mask(last, 3, now is not None)
                    exps(last, 3)
                    attend(last, 2, 1)
                if now:
                    weights(now, g, 1)
                    finish(now, g, 0)
                if last:
                    output(last, 2, 0)
                    output(last, 2, 1)
                    probs(last, 3)
                    output(last, 2, 2)
                    output(last, 2, 3)
                if now:
                    start(now, g, 1)
                if last:
                    turn(last, 3)
                if now:
                    start(now, g, 2)
                    finish(now, g, 1)
                if last:
                    turn_win(last, 0)
                    turn_win(last, 1)
                    attend_win(last, 0)
                if now:
                    start(now, g, 3)
                if last:
                    attend_win(last, 1)
                    turn_win(last, 2)
                    turn_win(last, 3)
                if now:
                    finish(now, g, 2)
                if last:
                    attend_win(last, 2)
                    attend_win(last, 3)
                    for tt in range(TPB):
                        output(last, 3, tt)
                if now:
                    weights(now, g, 2)

            def main(now, g):
                for t in range(4):
                    finish(now, g, 3 + 2 * t)
                    if t >= 2:
                        turn(now, t - 2)
                    start(now, g, 4 + 2 * t)
                    if t == 0:
                        values(now)
                    if t >= 2:
                        attend(now, t - 2, 0)
                    start(now, g, 5 + 2 * t)
                    if t >= 2:
                        attend(now, t - 2, 1)
                    if t >= 1:
                        mask(now, t - 1)
                        exps(now, t - 1)
                    finish(now, g, 4 + 2 * t)
                    if t >= 2:
                        output(now, t - 2, 0)
                        output(now, t - 2, 1)
                    if t >= 1:
                        probs(now, t - 1)
                    if t >= 2:
                        output(now, t - 2, 2)
                        output(now, t - 2, 3)
            groups(eng, boundary, main)

        def nothing(*_):
            pass

        def block_of(u):
            return u if u < 4 else (u - 4) // 2

        USES = [0, 1, 2, 3, 0, 1, 2, 3]

        def slot_of(u):
            return u if u < 4 else 4 + (u - 4) // 2

        @block.sync
        def _(sp):
            for dst, src in ((ident, A["ident"]), (madd, A["att_madd"]), (mmul, A["att_mmul"]),
                             (extra, A["att_extra"]), (wmask, A["att_wmask"]), (scale, A["att_scale"]),
                             (t1[0], A["att_perm"])):
                sp.dma_start(dst[:, 0:P] if dst is t1[0] else dst[:], src).then_inc(s_const, 16)

            def load_weights(wait, g, part):
                part_dram = A[("att_kv", "att_q", "att_out")[part]]
                src = part_dram[g * P:(g + 1) * P, :] if isinstance(g, int) else part_dram[bass.ds(g * P, P), :]
                if part == 0:
                    wait("w_lo", -2)
                elif part == 1:
                    wait("w_lo", 0)
                else:
                    wait("w_lo", 2)
                if part == 0:
                    sp.dma_start(raw_kv[:], src).then_inc(s_kv, 16)
                else:
                    sp.dma_start(raw_q[:], src).then_inc(s_q, 16)

            def body(g):
                wait = waiter(sp, g)
                load_weights(wait, g, 0)
                load_weights(wait, g, 1)
                for i, b in enumerate(USES):
                    wait("rotated", {0: -2, 1: 0, 2: 1, 3: 2, 4: 3, 5: 4, 6: 6, 7: 8}[i])
                    sp.dma_start(rope[i % 2][:], A["att_rope"][b, :, :, :]).then_inc(s_rope[i % 2], 16)
                    if i == 2:
                        load_weights(wait, g, 2)

            body(0)
            with sp.Fori(1, HKV) as g:
                body(g)
            def rows(m, i):
                return m[2 * i * P:2 * (i + 1) * P, :].rearrange("(t p) d -> p t d", p=P)

            def fetch(i):
                sp.dma_start(pair_x[i % 2], rows(x1_dram, i)).then_inc(s_tile[i % 2], 16)
                sp.dma_start(pair_g[i % 2], rows(g_dram, i)).then_inc(s_tile[i % 2], 16)
            sp.wait_ge(S["rotated"], N["rotated"] * HKV)
            fetch(0)
            sp.wait_ge(S["win_T"], N["win_T"] * HKV)
            fetch(1)
            for i in range(NT // 2):
                sp.wait_ge(s_res, i + 1)
                if i + 2 < NT // 2:
                    fetch(i + 2)
                sp.dma_start(rows(out_dram, i), s_acc[:, 2 * i:2 * i + 2, :]).then_inc(s_st[i % 2], 16)
            for i in range(2):
                sp.wait_ge(s_st[i], 16 * NT // 4)

        @block.gpsimd
        def _(pool):
            for m in (*kbd, *kwin, *vbd, *vwin):
                nc.gpsimd.memset(f32(m[:]), 0.0).then_inc(s_zero, 1)

            def weights(wait, g, part):
                c0, c1 = PARTS[part]
                wait("w_hi", part + 1)
                nc.gpsimd.tensor_tensor(w[LO][:, c0:c1], (raw_kv if part == 0 else raw_q)[:], f32(w[HI][:, c0:c1]),
                                        ALU.subtract).then_inc(S["w_lo"], 1)

            def start(wait, g, u):
                j = u % 2
                wait("q_hi", u + 1)
                nc.gpsimd.tensor_tensor(qp[j][LO][:], q32[j][:], f32(qp[j][HI][:]), ALU.subtract).then_inc(S["q_lo"], 1)
                i = slot_of(u)
                pool.wait_ge(s_rope[i % 2], 16 * (4 * g + i // 2 + 1))
                wait("rotated", u - 1)
                nc.gpsimd.tensor_tensor(t1[j][:], q32[j][:], rope[i % 2][:, 0, :], ALU.mult).then_inc(S["t1"], 1)

            def finish(wait, g, u):
                if u >= 4:
                    n = u - 4
                    wait("qr_hi", n + 1)
                    nc.gpsimd.tensor_tensor(qr[LO][:, n % 2, :], rot[u % 2][:], f32(qr[HI][:, n % 2, :]),
                                            ALU.subtract).then_inc(S["qr_lo"], 1)

            def exps(wait, tb):
                if tb == 0:
                    wait("exps", 1)
                    nc.gpsimd.tensor_tensor(sm[0][:, 0, :, :], sm[0][:, 0, :, :],
                                            extra[:].unsqueeze(1).to_broadcast([P, 4, 32]), ALU.add)\
                      .then_inc(S["m_fix"], 1)
            order(pool, weights, start, finish, nothing, nothing, exps, nothing, nothing, nothing, nothing, nothing,
                  nothing)

        @block.scalar
        def _(act):
            act.wait_ge(s_const, 16 * 7)
            nc.scalar.activation(scale[:], scale[:], ACT.Exp).then_inc(s_sc, 1)
            act.wait_ge(s_sc, 1)
            nc.scalar.mul(scale[:], scale[:], float(32.0 ** -0.5)).then_inc(s_sc, 1)
            nc.scalar.copy(perm[:], t1[0][:, 0:P]).then_inc(s_perm, 1)
            act.wait_ge(s_sc, 2)
            act.wait_ge(s_zero, 8)

            def weights(wait, g, part):
                c0, c1 = PARTS[part]
                if part == 0:
                    wait("q32", 0)
                    nc.scalar.copy(scale_now[:], scale[:, 2 * g:2 * g + 2] if isinstance(g, int) else
                                   scale[:, bass.ds(2 * g, 2)]).then_inc(S["scale"], 1)
                    act.wait_ge(s_kv, 16 * g + 16)
                    wait("q_sum", 0)
                else:
                    act.wait_ge(s_q, 32 * g + 16 * part)
                    if part == 2:
                        wait("s_sum", 0)
                nc.scalar.copy(w[HI][:, c0:c1], (raw_kv if part == 0 else raw_q)[:]).then_inc(S["w_hi"], 1)

            def start(wait, g, u):
                j = u % 2
                wait("q_sum", u + 1)
                wait("t1", u - 1)
                if u < 4:
                    nc.scalar.copy(q32[j][:], bA[j][:]).then_inc(S["q32"], 1)
                else:
                    c = (u - 4) % 2
                    wait("scale", 1)
                    nc.scalar.activation(q32[j][:], bA[j][:], ACT.Copy, scale=scale_now[:, c:c + 1])\
                      .then_inc(S["q32"], 1)
                wait("q32", u + 1)
                wait("swapped", u - 1)
                nc.scalar.copy(qp[j][HI][:], q32[j][:]).then_inc(S["q_hi"], 1)

            def finish(wait, g, u):
                wait("rotated", u + 1)
                if u >= 4:
                    n = u - 4
                    wait("scores", n // 2)
                    if n < 2:
                        wait("win_s", 0)
                    nc.scalar.copy(qr[HI][:, n % 2, :], rot[u % 2][:]).then_inc(S["qr_hi"], 1)
                elif u == 3:
                    wait("win_s", 0)
                    for e in range(2):
                        rows = slice(64 * e, 64 * e + 64)
                        nc.scalar.copy(kwin[HI][rows, e, :], rot[1][rows, BLK - WIN:BLK]).then_inc(S["k_hi"], 1)
                    wait("kp_mean", 1)
                    for e in range(2):
                        rows = slice(64 * e, 64 * e + 64)
                        nc.scalar.copy(kbd[HI][rows, e, 0:NPOOL], kpool[rows, 0:NPOOL]).then_inc(S["k_hi"], 1)

            def values(wait):
                wait("v_sum", 1)
                for h in range(4):
                    rows = slice(32 * h, 32 * h + 32)
                    nc.scalar.copy(vbd[HI][rows, h // 2, h % 2, :], bT[rows, 0:DV]).then_inc(S["v_hi"], 1)
                for kt in range(2):
                    wait("v_sum", kt + 2)
                    nc.scalar.copy(vwin[HI][:, kt, 1, :], bO[kt][:, 0:DV]).then_inc(S["v_hi"], 1)

            def exps(wait, tb):
                wait("shifted", tb + 1)
                nc.scalar.activation(sm[tb % 2][:], sm[tb % 2][:], ACT.Exp).then_inc(S["exps"], 1)
                if tb == 3:
                    for i in range(2):
                        wait("win_sh", i + 1)
                        nc.scalar.activation(sw[:, i], sw[:, i], ACT.Exp).then_inc(S["win_e"], 1)

            def turn(wait, tb):
                wait("pT_sum", tb + 1)
                nc.scalar.copy(pT[HI][:], bT[:]).then_inc(S["pT_hi"], 1)

            def attend(wait, tb, p):
                if tb < 3:
                    wait("pv", 2 * tb + p + 1)
                else:
                    wait("win_pv", 2 * p + 2)
                if p == 0:
                    wait("s_sum", 4 * tb)
                nc.scalar.copy(oT[HI][:, p, :], bP[:]).then_inc(S["o_hi"], 1)

            def attend_win(wait, h):
                wait("win_T", h + 1)
                wait("win_pv", h)
                nc.scalar.copy(pw[HI][:].rearrange("p a n -> p (a n)"), bW[h % 2]).then_inc(S["win_hi"], 1)
                if h % 2:
                    attend(wait, 3, h // 2)
            order(act, weights, start, finish, values, nothing, exps, nothing, turn, attend, nothing, attend_win, nothing)

        @block.vector
        def _(dve):
            link = Chain(dve, s_xb)
            for s in (HI, LO):
                for c in range(KC):
                    nc.vector.tensor_reduce(pool_s[s][:, c, 0:NPOOL], f32(xn[s][:, c, 0:NPOOL * MBLK])
                                            .rearrange("p (b m) -> p b m", m=MBLK), AX.X, ALU.add)
                    link(nc.vector.tensor_reduce(pool_s[s][:, c, NPOOL:NPOOL + 1], f32(xn[s][:, c, T - WIN:T]),
                                                 AX.X, ALU.add))
            link(nc.vector.tensor_tensor(pool_s[0][:, :, 0:29], pool_s[0][:, :, 0:29], pool_s[1][:, :, 0:29], ALU.add))
            link(nc.vector.memset(pool_s[0][:, :, 29:32], 0.0))
            link(nc.vector.tensor_scalar_mul(pool_s[0][:, :, 0:NPOOL], pool_s[0][:, :, 0:NPOOL], 1.0 / MBLK))
            link(nc.vector.tensor_scalar_mul(pool_s[0][:, :, NPOOL:NPOOL + 1], pool_s[0][:, :, NPOOL:NPOOL + 1], 1.0 / WIN))
            for h in range(4):
                link(nc.vector.tensor_copy(xbar[HI][:, :, h, :], pool_s[0]))
            for h in range(4):
                nc.vector.tensor_tensor(xbar[LO][:, :, h, :], pool_s[0], f32(xbar[HI][:, :, h, :]), ALU.subtract)\
                  .then_inc(s_xbr, 1)
            link(nc.vector.memset(s_acc[:], 0.0))
            dve.wait_ge(s_xbr, 4)
            dve.wait_ge(s_zero, 8)
            dve.wait_ge(s_const, 16 * 7)

            def finish(wait, g, u):
                j = u % 2
                i = slot_of(u)
                wait("swapped", u + 1)
                dve.wait_ge(s_rope[i % 2], 16 * (4 * g + i // 2 + 1))
                if u < 2:
                    wait("qr_lo", u - 1)
                elif u < 6:
                    wait("k_pool", u - 1 if u < 5 else 4)
                    if u == 5:
                        wait("k_lo", 2)
                else:
                    wait("qr_lo", u - 5)
                nc.vector.tensor_tensor(rot[j][:], bB[:], rope[i % 2][:, 1, :], ALU.mult).then_inc(S["t2"], 1)
                wait("t2", u + 1)
                wait("t1", u + 1)
                nc.vector.tensor_tensor(rot[j][:], rot[j][:], t1[j][:], ALU.add).then_inc(S["rotated"], 1)
                if u < 4:
                    wait("rotated", u + 1)
                    nb = 8 if u < 3 else 4
                    nc.vector.tensor_reduce(kpool[:, 8 * u:8 * u + nb], rot[j][:, 0:nb * MBLK]
                                            .rearrange("p (b m) -> p b m", m=MBLK), AX.X, ALU.add)\
                      .then_inc(S["k_pool"], 1)
                if u == 3:
                    wait("k_pool", 4)
                    nc.vector.tensor_scalar_mul(kpool[:, 0:NPOOL], kpool[:, 0:NPOOL], 1.0 / MBLK)\
                      .then_inc(S["kp_mean"], 1)
                    wait("kp_mean", 1)
                    for e in range(2):
                        rows = slice(64 * e, 64 * e + 64)
                        wait("k_hi", e + 1)
                        nc.vector.tensor_tensor(kwin[LO][rows, e, :], rot[1][rows, BLK - WIN:BLK],
                                                f32(kwin[HI][rows, e, :]), ALU.subtract).then_inc(S["k_lo"], 1)
                    for e in range(2):
                        rows = slice(64 * e, 64 * e + 64)
                        wait("k_hi", e + 3)
                        nc.vector.tensor_tensor(kbd[LO][rows, e, 0:NPOOL], kpool[rows, 0:NPOOL],
                                                f32(kbd[HI][rows, e, 0:NPOOL]), ALU.subtract).then_inc(S["k_lo"], 1)

            def values(wait):
                for h in range(4):
                    rows = slice(32 * h, 32 * h + 32)
                    wait("v_hi", h + 1)
                    nc.vector.tensor_tensor(vbd[LO][rows, h // 2, h % 2, :], bT[rows, 0:DV],
                                            f32(vbd[HI][rows, h // 2, h % 2, :]), ALU.subtract).then_inc(S["v_lo"], 1)
                for kt in range(2):
                    wait("v_hi", kt + 5)
                    nc.vector.tensor_tensor(vwin[LO][:, kt, 1, :], bO[kt][:, 0:DV], f32(vwin[HI][:, kt, 1, :]),
                                            ALU.subtract).then_inc(S["v_lo"], 1)

            def mask(wait, tb, more=True):
                m = sm[tb % 2]
                sc = bS[:].rearrange("p t c h k -> p t (c h) k")
                wait("scores", tb + 1)
                wait("pT_sum", tb - 1)
                wait("prob", tb)
                first = 0
                if tb == 0:
                    wait("win_p", 0)
                    first = 1
                    nc.vector.tensor_tensor(m[:, 0], sc[:, 0], mmul[:].unsqueeze(1).to_broadcast([P, 4, 32]),
                                            ALU.mult).then_inc(S["m_mul"], 1)
                nc.vector.tensor_tensor(m[:, first:], sc[:, first:], madd[:, 4 * tb + first:4 * tb + 4, :].unsqueeze(2)
                                        .to_broadcast([P, 4 - first, 4, 32]), ALU.add).then_inc(S["masked"], 1)
                if tb == 0:
                    wait("m_mul", 1)
                    nc.vector.tensor_tensor(m[:, 0], m[:, 0], madd[:, 0, :].unsqueeze(1).to_broadcast([P, 4, 32]),
                                            ALU.add).then_inc(S["m_add"], 1)
                    wait("m_add", 1)
                if tb == 3:
                    wait("win_T", 0)
                    for i in range(2):
                        for c in range(2):
                            n = 2 * i + c
                            wait("win_s", n + 1)
                            nc.vector.tensor_tensor(sw[:, i, 2 * c:2 * c + 2, :], bA[c][:]
                                                    .rearrange("p (h k) -> p h k", h=2),
                                                    wmask[:, (1 - i) * P:(3 - i) * P].unsqueeze(1).to_broadcast([P, 2, WIN]), ALU.add)\
                              .then_inc(S["win_m"], 1)
                wait("masked", tb + 1)
                nc.vector.tensor_reduce(mx[:], m[:].rearrange("p t h k -> p (t h) k"), AX.X, ALU.max)\
                  .then_inc(S["max"], 1)
                wait("max", tb + 1)
                if tb == 3:
                    wait("win_m", 4)
                    nc.vector.tensor_reduce(mw[:], sw[:].rearrange("p t h k -> p (t h) k"), AX.X, ALU.max)\
                      .then_inc(S["win_max"], 1)
                    wait("win_max", 1)
                    nc.vector.tensor_tensor(mx[:, 8:16], mx[:, 8:16], mw[:], ALU.max).then_inc(S["win_mx"], 1)
                    wait("win_mx", 1)
                nc.vector.tensor_tensor(m[:], m[:], mx[:].rearrange("p (t h) -> p t h", h=4).unsqueeze(3)
                                        .to_broadcast([P, 4, 4, 32]), ALU.subtract).then_inc(S["shifted"], 1)
                if tb == 3:
                    for i in range(2):
                        nc.vector.tensor_tensor(sw[:, i], sw[:, i], mx[:, 8 + 4 * i:12 + 4 * i].unsqueeze(2)
                                                .to_broadcast([P, 4, WIN]), ALU.subtract).then_inc(S["win_sh"], 1)

            def probs(wait, tb):
                m = sm[tb % 2]
                wait("exps", tb + 1)
                if tb == 0:
                    wait("m_fix", 1)
                if tb == 3:
                    wait("win_sh", 2)
                nc.vector.tensor_reduce(mx[:], m[:].rearrange("p t h k -> p (t h) k"), AX.X, ALU.add)\
                  .then_inc(S["sums"], 1)
                wait("sums", tb + 1)
                if tb == 3:
                    wait("win_e", 2)
                    nc.vector.tensor_reduce(mw[:], sw[:].rearrange("p t h k -> p (t h) k"), AX.X, ALU.add)\
                      .then_inc(S["win_sum"], 1)
                    wait("win_sum", 1)
                    nc.vector.tensor_tensor(mx[:, 8:16], mx[:, 8:16], mw[:], ALU.add).then_inc(S["win_tot"], 1)
                    wait("win_tot", 1)
                nc.vector.reciprocal(mx[:], mx[:]).then_inc(S["inv"], 1)
                wait("inv", tb + 1)
                nc.vector.tensor_tensor(m[:], m[:], mx[:].rearrange("p (t h) -> p t h", h=4).unsqueeze(3)
                                        .to_broadcast([P, 4, 4, 32]), ALU.mult).then_inc(S["prob"], 1)
                if tb == 3:
                    for i in range(2):
                        nc.vector.tensor_tensor(sw[:, i], sw[:, i], mx[:, 8 + 4 * i:12 + 4 * i].unsqueeze(2)
                                                .to_broadcast([P, 4, WIN]), ALU.mult).then_inc(S["win_p"], 1)

            def turn(wait, tb):
                wait("pT_hi", tb + 1)
                nc.vector.tensor_tensor(pT[LO][:], bT[:], f32(pT[HI][:]), ALU.subtract).then_inc(S["pT_lo"], 1)

            def attend(wait, tb, p):
                wait("o_hi", 2 * tb + p + 1)
                nc.vector.tensor_tensor(oT[LO][:, p, :], bP[:], f32(oT[HI][:, p, :]), ALU.subtract)\
                  .then_inc(S["o_lo"], 1)

            def attend_win(wait, h):
                wait("win_hi", h + 1)
                nc.vector.tensor_tensor(pw[LO][:].rearrange("p a n -> p (a n)"), bW[h % 2],
                                        f32(pw[HI][:]).rearrange("p a n -> p (a n)"), ALU.subtract)\
                  .then_inc(S["win_lo"], 1)
                if h % 2:
                    attend(wait, 3, h // 2)

            def output(wait, tb, tt):
                t = 4 * tb + tt
                wait("s_sum", t + 1)
                nc.vector.tensor_tensor(s_acc[:, t, :], bO[tt % 2][:], s_acc[:, t, :], ALU.add)\
                  .then_inc(S["s_add"], 1)

            order(dve, nothing, nothing, finish, values, mask, nothing, probs, turn, attend, nothing, attend_win, output)
            fin = Chain(dve, s_fin)
            for i in range(NT // 2):
                dve.wait_ge(s_tile[i % 2], 32 * (i // 2 + 1))
                if i == 0:
                    dve.wait_ge(S["s_add"], N["s_add"] * HKV)
                pair = s_acc[:, 2 * i:2 * i + 2, :]
                fin(nc.vector.tensor_tensor(pair, pair, pair_g[i % 2], ALU.mult))
                nc.vector.tensor_tensor(pair, pair, pair_x[i % 2], ALU.add).then_inc(s_res, 1)

        @block.tensor
        def _(pe):
            pe.wait_ge(s_perm, 1)
            pe.wait_ge(s_xbr, 4)
            pe.wait_ge(s_zero, 8)

            def start(wait, g, u):
                j = u % 2
                tb = block_of(u)
                if u == 0:
                    wait("w_lo", 1)
                if u == 4:
                    wait("w_lo", 2)
                wait("q32", u - 1)
                if u in (1, 2):
                    wait("win_m", u - 2)
                cols = tb * BLK
                for c in range(KC):
                    col = (WK + c * P) if u < 4 else (WQ + c * 256 + (u - 4) % 2 * P)
                    for n, (p, q) in enumerate(PASSES):
                        last = nc.tensor.matmul(bA[j][:], w[p][:, col:col + P], xn[q][:, c, cols:cols + BLK],
                                                start=(c == 0 and n == 0), stop=(c == KC - 1 and n == 2))
                last.then_inc(S["q_sum"], 1)

            def finish(wait, g, u):
                j = u % 2
                wait("q_lo", u + 1)
                wait("t2", u)
                for s in (HI, LO):
                    last = nc.tensor.matmul(bB[:], perm[:], qp[j][s][:], start=(s == HI), stop=(s == LO))
                last.then_inc(S["swapped"], 1)

            def values(wait):
                wait("win_lo", 0)
                for c in range(KC):
                    for n, (p, q) in enumerate(PASSES):
                        last = nc.tensor.matmul(bT[:, 0:DV], xbar[p][:, c].rearrange("p h k -> p (h k)"),
                                                w[q][:, WV + c * DV:WV + (c + 1) * DV],
                                                start=(c == 0 and n == 0), stop=(c == KC - 1 and n == 2))
                last.then_inc(S["v_sum"], 1)
                for kt in range(2):
                    wait("s_add", kt - 1)
                    k0 = T - WIN + kt * P
                    for c in range(KC):
                        for n, (p, q) in enumerate(PASSES):
                            last = nc.tensor.matmul(bO[kt][:, 0:DV], xn[p][:, c, k0:k0 + P],
                                                    w[q][:, WV + c * DV:WV + (c + 1) * DV],
                                                    start=(c == 0 and n == 0), stop=(c == KC - 1 and n == 2))
                    last.then_inc(S["v_sum"], 1)

            def mask(wait, tb, more=True):
                wait("k_lo", 4)
                wait("qr_lo", 2 * tb + 2)
                wait("masked", tb)
                if tb == 0:
                    wait("win_lo", 0)
                if tb == 1:
                    wait("m_mul", 1)
                for tt in range(TPB):
                    for c in range(2):
                        for n, (p, q) in enumerate(PASSES):
                            last = nc.tensor.matmul(bS[:, tt, c].rearrange("p h k -> p (h k)"),
                                                    qr[p][:, c, tt * P:(tt + 1) * P],
                                                    kbd[q][:].rearrange("p h k -> p (h k)"),
                                                    start=(n == 0), stop=(n == 2))
                last.then_inc(S["scores"], 1)
                if tb < 3:
                    return
                for i in range(2):
                    for c in range(2):
                        if i:
                            wait("win_m", c + 1)
                        else:
                            wait("q32", 13 if c == 0 and more else 12)
                        for n, (p, q) in enumerate(PASSES):
                            last = nc.tensor.matmul(bA[c][:], qr[p][:, c, (2 + i) * P:(3 + i) * P],
                                                    kwin[q][:].rearrange("p h k -> p (h k)"),
                                                    start=(n == 0), stop=(n == 2))
                        last.then_inc(S["win_s"], 1)

            def turn(wait, tb):
                wait("prob", tb + 1)
                if tb == 0:
                    wait("v_lo", 6)
                else:
                    wait("pT_lo", tb)
                for tt in range(TPB):
                    last = nc.tensor.transpose(bT[:, tt * P:(tt + 1) * P],
                                               sm[tb % 2][:, tt].rearrange("p h k -> p (h k)"), ident[:])
                last.then_inc(S["pT_sum"], 1)

            def pooled(p_, last_pass):
                for n, (p, q) in enumerate(PASSES):
                    last = nc.tensor.matmul(bP[:], vbd[p][:, p_].rearrange("p h d -> p (h d)"), pT[q][:],
                                            start=(n == 0), stop=(n == 2 and last_pass))
                return last

            def attend(wait, tb, p_):
                wait("pT_lo", tb + 1)
                wait("o_lo", 2 * tb + p_)
                pooled(p_, True).then_inc(S["pv"], 1)

            def turn_win(wait, h):
                wait("win_p", 2)
                if h == 0:
                    wait("masked", 4)
                elif h == 1:
                    wait("pT_lo", 4)
                else:
                    wait("win_lo", h - 1)
                for kt in range(2):
                    for i in range(2):
                        o = kt * WIN + i * P
                        last = nc.tensor.transpose(bW[h % 2][:, o:o + P], sw[:, i, h, kt * P:(kt + 1) * P], ident[:])
                last.then_inc(S["win_T"], 1)

            def attend_win(wait, h):
                e = h % 2
                if e == 0:
                    wait("pT_lo", 4)
                    wait("o_lo", 6 + h // 2)
                    pooled(h // 2, False)
                wait("win_lo", h + 1)
                for kt in range(2):
                    for n, (p, q) in enumerate(PASSES):
                        vv = vwin[p][:, kt, 1 - e:3 - e, :].rearrange("p a d -> p (a d)")
                        last = nc.tensor.matmul(bP[:, WIN:BLK], vv, pw[q][:, kt, :], start=False,
                                                stop=(e == 1 and kt == 1 and n == 2))
                last.then_inc(S["win_pv"], 1)

            def output(wait, tb, tt):
                if tt == 0:
                    wait("o_lo", 2 * tb + 2)
                    wait("w_lo", 3)
                wait("s_add", 4 * tb + tt - 1)
                for c in range(2):
                    for n, (p, q) in enumerate(PASSES):
                        col = WOUT + c * D
                        last = nc.tensor.matmul(bO[tt % 2][:], oT[p][:, c, tt * P:(tt + 1) * P],
                                                w[q][:, col:col + D], start=(c == 0 and n == 0),
                                                stop=(c == 1 and n == 2))
                last.then_inc(S["s_sum"], 1)
            order(pe, nothing, start, finish, values, mask, nothing, nothing, turn, attend, turn_win, attend_win, output)


class Keep:
    pass


def program(nc, A, out):
    with ExitStack() as ctx:
        def scratch(name, shape=(T, D)):
            return nc.dram_tensor(name, shape, F32, kind="Internal").ap()
        g0, x1, g1, xT = scratch("g0"), scratch("x1"), scratch("g1"), scratch("xT", (P, KC, T))
        keep = Keep()

        def parts(c, tag):
            return [c.enter_context(nc.sbuf_tensor(f"{tag}{'hl'[s]}", [P, KC, T], F32R)) for s in (HI, LO)]

        xs, ys = scratch("xs", (RT * P, D)), scratch("ys", (RT * P, D))
        with ExitStack() as c0:
            keep.pos = c0.enter_context(nc.sbuf_tensor("pos", [P, NT], mybir.dt.uint32))
            keep.top = c0.enter_context(nc.sbuf_tensor("top", [P, NT], F32))
            keep.offset = c0.enter_context(nc.sbuf_tensor("offset", [P, RT], mybir.dt.int32))
            with ExitStack() as c:
                keep.xn = parts(c, "xn0")
                keep.y = c.enter_context(nc.sbuf_tensor("y0", [P, NT, D], F32))
                layernorm_stage(nc, "ln0", A["x"], A["ident"], keep, xT)
                dispatch_stage(nc, A, keep, xs)
            routed_ffn_stage(nc, A["ffn_w"], xs, ys, A["ident"], keep)
            combine_stage(nc, ys, keep, g0)
        time_mix_stage(nc, A["mix_w"], A["mix_vec"], xT, A["x"], g0, x1)
        with ExitStack() as c:
            keep.xn = parts(c, "xn1")
            with ExitStack() as c2:
                keep.y = c2.enter_context(nc.sbuf_tensor("y1", [P, NT, D], F32))
                keep.pos4 = c2.enter_context(nc.sbuf_tensor("pos4", [P, 4, NT], mybir.dt.uint32))
                keep.gate4 = c2.enter_context(nc.sbuf_tensor("gate4", [P, 4, NT], F32))
                keep.expert = c2.enter_context(nc.sbuf_tensor("expert", [P, MT], mybir.dt.int32))
                xn_rows, idx, ys1 = scratch("xn_rows"), scratch("idx", (MT * MR, 1)), scratch("ys1", (MT * MR, D))
                layernorm_stage(nc, "ln1", x1, A["ident"], keep)
                shared_experts_stage(nc, A, top4_router(nc, A, keep, xn_rows, idx), keep)
                routed_experts_stage(nc, A, xn_rows, idx, ys1, keep)
                mix_experts_stage(nc, ys1, keep, g1)
            attention_stage(nc, A, x1, g1, out, keep)


def kernel(**inp):
    import numpy as np
    import concourse.bacc as bacc
    from concourse.bass_utils import run_bass_kernel_spmd as run

    nc = bacc.Bacc("TRN2", target_bir_lowering=False, num_devices=1)
    arrays, A = {}, {}

    def give(name, a):
        a = np.ascontiguousarray(a)
        arrays["in_" + name] = a
        A[name] = nc.dram_tensor("in_" + name, a.shape, mybir.dt.from_np(a.dtype), kind="ExternalInput").ap()

    def chunks(wt, cols):
        k, m = wt.shape
        return wt.reshape(k // P, P, m // cols, cols).transpose(2, 1, 0, 3)

    inp = {n: np.asarray(v) for n, v in inp.items()}
    give("x", inp["L0_attn_x"].reshape(T, D))
    give("ident", np.eye(P, dtype=np.float32))
    give("ffn_gw", inp["L0_ffn_gate_w"].T.reshape(KC, P, 2).transpose(1, 0, 2))
    gate, up, down = (inp["L0_ffn_w_" + n] for n in ("gate", "up", "down"))
    gu = np.stack([gate, up], axis=1).reshape(2, 2, RG, P, KC, P).transpose(2, 5, 0, 4, 1, 3).reshape(RG, P, 2, KC * 2 * P)
    dn = down.transpose(0, 2, 1).reshape(2, RG, P, D).transpose(1, 2, 0, 3)
    give("ffn_w", np.concatenate([gu, dn], axis=3).reshape(RG, P, 2 * RW))
    p_, t_ = np.arange(P, dtype=np.float32)[:, None], np.arange(NT, dtype=np.float32)[None, :]
    give("route_consts", np.concatenate([(p_ <= p_.T).astype(np.float32), p_ + P * t_, 0 * p_ + P * t_,
                                         0 * p_ + np.arange(RT, dtype=np.float32)[None, :]], axis=1))
    give("mix_w", np.stack([inp["L0_attn_" + n].T.reshape(KC, P, D).transpose(1, 0, 2)
                            for n in ("Wk", "Wv", "Wr", "Wo")]))
    give("mix_vec", np.stack([inp["L0_attn_" + n].reshape(KC, P).T for n in
                              ("tm_k", "tm_v", "tm_r", "time_decay", "time_first", "ln_g", "ln_b")], axis=1))
    FH = 384
    w1 = np.concatenate([inp["L1_ffn_shared_w1"], inp["L1_ffn_routed_w1"]])
    w2 = np.concatenate([inp["L1_ffn_shared_w2"], inp["L1_ffn_routed_w2"]])
    b1 = np.concatenate([inp["L1_ffn_shared_b1"], inp["L1_ffn_routed_b1"]])
    b2 = np.concatenate([inp["L1_ffn_shared_b2"], inp["L1_ffn_routed_b2"]])
    G, F = b1.shape
    w1 = np.pad(w1, ((0, 0), (0, 0), (0, FH - F))).reshape(G, KC, P, FH).transpose(0, 2, 1, 3).reshape(G, P, KC * FH)
    w2 = np.concatenate([w2, b2[:, None, :], np.zeros((G, FH - F - 1, D), w2.dtype)], axis=1)
    b1 = np.concatenate([b1, np.ones((G, 1), b1.dtype), np.zeros((G, FH - F - 1), b1.dtype)], axis=1)
    w2 = w2.reshape(G, 3, P, D).transpose(0, 2, 1, 3).reshape(G, P, 3 * D)
    b1 = b1.reshape(G, 3, P).transpose(0, 2, 1)
    give("moe_shared", np.concatenate([w1, w2], axis=2)[0:2])
    give("moe_b1", b1[0:2].transpose(1, 2, 0))
    give("moe_w1", np.concatenate([w1, b1], axis=2)[2:])
    give("moe_w2", w2[2:])
    give("moe_consts", np.concatenate([(p_ <= p_.T).astype(np.float32), p_ + P * t_, 0 * p_ + (t_ > 0),
                                       0 * p_ + MR * np.arange(8, dtype=np.float32)[None, :],
                                       0 * p_ + np.arange(MT, dtype=np.float32)[None, :]], axis=1).astype(np.float32))
    give("moe_cen", inp["L1_ffn_centroids"].T.reshape(KC, P, 16).transpose(1, 0, 2))
    give("moe_bias", np.broadcast_to(inp["L1_ffn_bias"], (P, 16)))
    give("moe_lower", np.broadcast_to(np.tril(np.ones((16, 16), np.float32), -1), (P, 16, 16)))
    qs, qg = (inp["L1_attn_Wq_" + n].reshape(D, H, 32) for n in ("sem", "geo"))
    ks, kg = (inp["L1_attn_Wk_" + n].reshape(D, HKV, 32) for n in ("sem", "geo"))
    wq = np.concatenate([qs, qg], axis=2).reshape(KC, P, HKV, 256)
    wk = np.concatenate([ks, kg, ks, kg], axis=2).reshape(KC, P, HKV, P)
    wv = inp["L1_attn_Wv"].reshape(KC, P, HKV, DV)
    wo = inp["L1_attn_Wo"].reshape(HKV, 2, P, D)
    att = np.concatenate([m.transpose(2, 1, 0, 3).reshape(HKV, P, -1) for m in (wq, wk, wv)]
                         + [wo.transpose(0, 2, 1, 3).reshape(HKV, P, -1)], axis=2)
    for name, c0, c1 in (("kv", WK, WOUT), ("q", WQ, WK), ("out", WOUT, AW)):
        give("att_" + name, att[:, :, c0:c1].reshape(HKV * P, c1 - c0))
    give("att_scale", np.repeat(inp["L1_attn_logit_scale"].reshape(8, 2), 64, axis=1).T)
    f4 = np.float32
    inv = (f4(1.0) / f4(10000.0) ** (np.arange(0, 32, 2, dtype=f4) / f4(32))).astype(f4)
    ang = (np.arange(T, dtype=f4)[None, :] * inv[:, None]).astype(f4)
    cos, sin = np.cos(ang).astype(f4), np.sin(ang).astype(f4)
    one, zero = np.ones((32, T), f4), np.zeros((32, T), f4)
    C = np.concatenate([one, cos, cos] * 2)
    S = np.concatenate([zero, -sin, sin] * 2)
    give("att_rope", np.stack([C, S], axis=1).reshape(P, 2, TB, BLK).transpose(2, 0, 1, 3))
    perm = np.zeros((P, P), f4)
    for m in range(P):
        if m % 64 >= 32:
            perm[m // 64 * 64 + 32 + (m % 64 - 32 + 16) % 32, m] = 1.0
    give("att_perm", perm)
    tok = np.arange(T).reshape(NT, P).T[:, :, None]
    slot = np.arange(32)[None, None, :]
    seen = (slot < NPOOL) & (MBLK * slot + MBLK - 1 <= tok)
    give("att_madd", np.where(seen, 0.0, np.where(slot < NPOOL, -1e9, -2e9)).astype(f4))
    give("att_mmul", seen[:, 0, :].astype(f4))
    give("att_extra", ((slot[:, 0] == NPOOL) & (np.arange(P)[:, None] < MBLK - 1)).astype(f4) * f4(WIN))
    give("att_wmask", np.where(np.arange(-P, 2 * P)[None, :] <= np.arange(P)[:, None], 0.0, -1e9).astype(f4))
    o = nc.dram_tensor("out", (T, D), F32, kind="ExternalOutput").ap()
    program(nc, A, o)
    r = run(nc, [arrays], core_ids=[0])
    return r.results[0]["out"].reshape(1, T, D)
```
